# Optimizing a Trainium2 kernel written in Bass

```python
import numpy as np
import jax
import jax.numpy as jnp

def _softmax(x, axis=-1):
    return jax.nn.softmax(x, axis=axis)

def _gelu(x):
    return jax.nn.gelu(x, approximate=True)

def _silu(x):
    return jax.nn.silu(x)

def _sigmoid(x):
    return jax.nn.sigmoid(x)

def _layernorm(x, axis=-1, eps=1e-05):
    m = jnp.mean(x, axis=axis, keepdims=True)
    v = jnp.var(x, axis=axis, keepdims=True)
    return (x - m) / jnp.sqrt(v + eps)

def _scatter_add(tgt, idx, src, axis=0):
    return tgt.at[idx].add(src)

def _segment_sum(src, seg, n):
    return jax.ops.segment_sum(src, seg, n)
kernel_name = 'mk_vit_tower_d1_tok_img4096_r4_8986f3'

def setup_inputs(seed: int=0):
    np.random.seed(seed)
    _w = jnp.asarray

    def _rec_inputs():
        import jax
        import jax.numpy as jnp
        _rk = jax.random.key(seed)
        x = -0.00348982 + 0.707501 * jax.random.normal(jax.random.fold_in(_rk, 1), (32, 128, 64, 2), jnp.float32)
        return x
    x = _rec_inputs()

    def _L0_tok_setup():
        import jax, jax.numpy as jnp
        import numpy as np
        H, N, S, CH, LEN = (128, 64, 128, 1, 1024)

        def _s4d_kernel(log_dt, C, B, inv_A_real, A_imag, L):
            dt = jnp.exp(log_dt)
            Cc = C[..., 0] + 1j * C[..., 1]
            Bc = B[..., 0] + 1j * B[..., 1]
            A = -jnp.exp(inv_A_real) + 1j * A_imag
            rep = H // A.shape[0]
            A = jnp.tile(A, (rep, 1))
            Bc = jnp.tile(Bc, (rep, 1))
            dtA = A * dt[:, None]
            Cc = Bc[None, :, :] * Cc
            Cc = Cc * (jnp.exp(dtA) - 1.0) / A
            ell = jnp.arange(L, dtype=jnp.float32)
            V = jnp.exp(dtA[:, :, None] * ell)
            K = 2.0 * jnp.einsum('chn,hnl->chl', Cc, V).real
            return K.astype(jnp.float32)
        key = jax.random.key(seed)
        k1, k2 = jax.random.split(key, 2)
        log_dt = jax.random.uniform(k1, (H,), minval=float(np.log(0.001)), maxval=float(np.log(0.1))).astype(jnp.float32)
        inv_A_real = jnp.full((S, N), float(np.log(0.5)), dtype=jnp.float32)
        A_imag = jnp.tile((np.pi * jnp.arange(N, dtype=jnp.float32))[None, :], (S, 1))
        B = jnp.stack([jnp.ones((S, N), jnp.float32), jnp.zeros((S, N), jnp.float32)], axis=-1)
        C = (jax.random.normal(k2, (CH, H, N, 2)) * 0.5 ** 0.5).astype(jnp.float32)
        return {'log_dt': log_dt, 'C': C, 'B': B, 'inv_A_real': inv_A_real, 'A_imag': A_imag, 'L': LEN}
    _L0_tok_all = _L0_tok_setup()
    _L0_tok_in = {k: v for k, v in _L0_tok_all.items() if k in ('log_dt', 'B', 'inv_A_real', 'A_imag')}
    del _L0_tok_all

    def _L0_attn_setup():
        import jax, jax.numpy as jnp
        import numpy as np
        DEPTH, DIM, DFF, VOCAB = (4, 128, 512, 1024)
        EPS = 1e-05

        def layernorm(x, w, b):
            mu = jnp.mean(x, axis=-1, keepdims=True)
            var = jnp.mean((x - mu) ** 2, axis=-1, keepdims=True)
            return (x - mu) * jax.lax.rsqrt(var + EPS) * w + b

        def sconv(x, phazor_c, last_conv_c):
            B, L, D = x.shape
            r = jnp.abs(phazor_c)
            p = jnp.tanh(r) * jnp.exp(1j * jnp.angle(phazor_c))
            prog = p[None, :] ** jnp.arange(L, dtype=jnp.float32)[:, None]
            filt_fft = jnp.fft.fft(prog, n=2 * L, axis=0)
            x_fft = jnp.fft.fft(x.astype(jnp.complex64), n=2 * L, axis=1)
            conv = jnp.fft.ifft(filt_fft[None] * x_fft, axis=1)[:, :L]
            conv = conv + last_conv_c[None, None, :] * prog[None] * p[None, None, :]
            return conv.real.astype(x.dtype)

        def _forward(x, Win, bin, ln1_w, ln1_b, phz_re, phz_im, lc_re, lc_im, sc_lin, ln2_w, ln2_b, W1, b1, W2, b2, lnl_w, lnl_b, Wout, bout):
            h = jnp.einsum('blv,dv->bld', x, Win) + bin

            def body(h, p):
                l1w, l1b, pr, pi, lr, li, scl, l2w, l2b, w1, b1_, w2, b2_ = p
                y = jax.nn.silu(layernorm(h, l1w, l1b))
                y = sconv(y, pr + 1j * pi, lr + 1j * li)
                h = h + y * scl
                y = layernorm(h, l2w, l2b)
                y = jax.nn.silu(jnp.einsum('bld,fd->blf', y, w1) + b1_)
                y = jnp.einsum('blf,df->bld', y, w2) + b2_
                return (h + y, None)
            xs = (ln1_w, ln1_b, phz_re, phz_im, lc_re, lc_im, sc_lin, ln2_w, ln2_b, W1, b1, W2, b2)
            h, _ = jax.lax.scan(body, h, xs)
            h = layernorm(h, lnl_w, lnl_b)
            return jnp.einsum('bld,vd->blv', h, Wout) + bout
        key = jax.random.key(seed)
        ks = jax.random.split(key, 20)
        f32 = jnp.float32
        inp = {}
        inp['x'] = jax.random.normal(ks[0], (2, 1024, VOCAB), dtype=f32)
        inp['Win'] = jax.random.normal(ks[1], (DIM, VOCAB), dtype=f32) * VOCAB ** (-0.5)
        inp['bin'] = jnp.zeros((DIM,), f32)
        inp['ln1_w'] = jnp.ones((DEPTH, DIM), f32)
        inp['ln1_b'] = jnp.zeros((DEPTH, DIM), f32)
        ang = 2 * np.pi * jnp.arange(DIM, dtype=f32) / DIM
        mag = jnp.abs(jax.random.normal(ks[2], (DEPTH, DIM), dtype=f32))
        inp['phz_re'] = mag * jnp.cos(ang)[None]
        inp['phz_im'] = mag * jnp.sin(ang)[None]
        inp['lc_re'] = jax.random.normal(ks[3], (DEPTH, DIM), dtype=f32)
        inp['lc_im'] = jax.random.normal(ks[4], (DEPTH, DIM), dtype=f32)
        inp['sc_lin'] = jnp.ones((DEPTH, DIM), f32)
        inp['ln2_w'] = jnp.ones((DEPTH, DIM), f32)
        inp['ln2_b'] = jnp.zeros((DEPTH, DIM), f32)
        inp['W1'] = jax.random.normal(ks[5], (DEPTH, DFF, DIM), dtype=f32) * DIM ** (-0.5)
        inp['b1'] = jnp.zeros((DEPTH, DFF), f32)
        inp['W2'] = jax.random.normal(ks[6], (DEPTH, DIM, DFF), dtype=f32) * DFF ** (-0.5)
        inp['b2'] = jnp.zeros((DEPTH, DIM), f32)
        inp['lnl_w'] = jnp.ones((DIM,), f32)
        inp['lnl_b'] = jnp.zeros((DIM,), f32)
        inp['Wout'] = jax.random.normal(ks[7], (VOCAB, DIM), dtype=f32) * DIM ** (-0.5)
        inp['bout'] = jnp.zeros((VOCAB,), f32)
        return inp
    _L0_attn_all = _L0_attn_setup()
    _L0_attn_in = {k: v for k, v in _L0_attn_all.items() if k in ('Win', 'bin', 'ln1_w', 'ln1_b', 'phz_re', 'phz_im', 'lc_re', 'lc_im', 'sc_lin', 'ln2_w', 'ln2_b', 'W1', 'b1', 'W2', 'b2', 'lnl_w', 'lnl_b', 'Wout', 'bout')}
    del _L0_attn_all

    def _L0_ffn_setup():
        import jax, jax.numpy as jnp
        import numpy as np
        NUM_EXPERTS = 8
        TOP_K = 2
        RANK = 16
        LORA_ALPHA = 32
        SCALING = LORA_ALPHA / RANK
        key = jax.random.key(seed)
        ks = jax.random.split(key, 6)
        B, S, D_IN, D_OUT = (4, 512, 1024, 1024)
        x = jax.random.normal(ks[0], (B, S, D_IN), dtype=jnp.float32)
        W_base = jax.random.normal(ks[1], (D_OUT, D_IN), dtype=jnp.float32) * 0.02
        b_base = jax.random.normal(ks[2], (D_OUT,), dtype=jnp.float32) * 0.02
        W_router = jax.random.normal(ks[3], (NUM_EXPERTS, D_IN), dtype=jnp.float32) * 0.02
        A = jax.random.normal(ks[4], (NUM_EXPERTS, RANK, D_IN), dtype=jnp.float32) * 0.02
        Bm = jax.random.normal(ks[5], (D_OUT, RANK), dtype=jnp.float32) * 0.02
        Bm = jnp.broadcast_to(Bm, (NUM_EXPERTS, D_OUT, RANK)) * jnp.arange(1, NUM_EXPERTS + 1, dtype=jnp.float32)[:, None, None] * 0.2
        return {'x': x, 'W_base': W_base, 'b_base': b_base, 'W_router': W_router, 'A': A, 'B': Bm}
    _L0_ffn_all = _L0_ffn_setup()
    _L0_ffn_in = {k: v for k, v in _L0_ffn_all.items() if k in ('W_base', 'b_base', 'W_router', 'A', 'B')}
    del _L0_ffn_all
    return {'x': x, 'L0_tok_log_dt': _L0_tok_in['log_dt'], 'L0_tok_B': _L0_tok_in['B'], 'L0_tok_inv_A_real': _L0_tok_in['inv_A_real'], 'L0_tok_A_imag': _L0_tok_in['A_imag'], 'L0_attn_Win': _L0_attn_in['Win'], 'L0_attn_bin': _L0_attn_in['bin'], 'L0_attn_ln1_w': _L0_attn_in['ln1_w'], 'L0_attn_ln1_b': _L0_attn_in['ln1_b'], 'L0_attn_phz_re': _L0_attn_in['phz_re'], 'L0_attn_phz_im': _L0_attn_in['phz_im'], 'L0_attn_lc_re': _L0_attn_in['lc_re'], 'L0_attn_lc_im': _L0_attn_in['lc_im'], 'L0_attn_sc_lin': _L0_attn_in['sc_lin'], 'L0_attn_ln2_w': _L0_attn_in['ln2_w'], 'L0_attn_ln2_b': _L0_attn_in['ln2_b'], 'L0_attn_W1': _L0_attn_in['W1'], 'L0_attn_b1': _L0_attn_in['b1'], 'L0_attn_W2': _L0_attn_in['W2'], 'L0_attn_b2': _L0_attn_in['b2'], 'L0_attn_lnl_w': _L0_attn_in['lnl_w'], 'L0_attn_lnl_b': _L0_attn_in['lnl_b'], 'L0_attn_Wout': _L0_attn_in['Wout'], 'L0_attn_bout': _L0_attn_in['bout'], 'L0_ffn_W_base': _L0_ffn_in['W_base'], 'L0_ffn_b_base': _L0_ffn_in['b_base'], 'L0_ffn_W_router': _L0_ffn_in['W_router'], 'L0_ffn_A': _L0_ffn_in['A'], 'L0_ffn_B': _L0_ffn_in['B']}

def reference(x, L0_tok_log_dt, L0_tok_B, L0_tok_inv_A_real, L0_tok_A_imag, L0_attn_Win, L0_attn_bin, L0_attn_ln1_w, L0_attn_ln1_b, L0_attn_phz_re, L0_attn_phz_im, L0_attn_lc_re, L0_attn_lc_im, L0_attn_sc_lin, L0_attn_ln2_w, L0_attn_ln2_b, L0_attn_W1, L0_attn_b1, L0_attn_W2, L0_attn_b2, L0_attn_lnl_w, L0_attn_lnl_b, L0_attn_Wout, L0_attn_bout, L0_ffn_W_base, L0_ffn_b_base, L0_ffn_W_router, L0_ffn_A, L0_ffn_B):
    import jax
    import jax.numpy as jnp

    def _L0_tok_ref(log_dt, C, B, inv_A_real, A_imag, L):
        import jax, jax.numpy as jnp
        import numpy as np
        H, N, S, CH, LEN = (128, 64, 128, 1, 1024)

        def _s4d_kernel(log_dt, C, B, inv_A_real, A_imag, L):
            dt = jnp.exp(log_dt)
            Cc = C[..., 0] + 1j * C[..., 1]
            Bc = B[..., 0] + 1j * B[..., 1]
            A = -jnp.exp(inv_A_real) + 1j * A_imag
            rep = H // A.shape[0]
            A = jnp.tile(A, (rep, 1))
            Bc = jnp.tile(Bc, (rep, 1))
            dtA = A * dt[:, None]
            Cc = Bc[None, :, :] * Cc
            Cc = Cc * (jnp.exp(dtA) - 1.0) / A
            ell = jnp.arange(L, dtype=jnp.float32)
            V = jnp.exp(dtA[:, :, None] * ell)
            K = 2.0 * jnp.einsum('chn,hnl->chl', Cc, V).real
            return K.astype(jnp.float32)
        return _s4d_kernel(log_dt, C, B, inv_A_real, A_imag, L)

    def _L0_attn_ref(x, Win, bin, ln1_w, ln1_b, phz_re, phz_im, lc_re, lc_im, sc_lin, ln2_w, ln2_b, W1, b1, W2, b2, lnl_w, lnl_b, Wout, bout):
        import jax, jax.numpy as jnp
        import numpy as np
        DEPTH, DIM, DFF, VOCAB = (4, 128, 512, 1024)
        EPS = 1e-05

        def layernorm(x, w, b):
            mu = jnp.mean(x, axis=-1, keepdims=True)
            var = jnp.mean((x - mu) ** 2, axis=-1, keepdims=True)
            return (x - mu) * jax.lax.rsqrt(var + EPS) * w + b

        def sconv(x, phazor_c, last_conv_c):
            B, L, D = x.shape
            r = jnp.abs(phazor_c)
            p = jnp.tanh(r) * jnp.exp(1j * jnp.angle(phazor_c))
            prog = p[None, :] ** jnp.arange(L, dtype=jnp.float32)[:, None]
            filt_fft = jnp.fft.fft(prog, n=2 * L, axis=0)
            x_fft = jnp.fft.fft(x.astype(jnp.complex64), n=2 * L, axis=1)
            conv = jnp.fft.ifft(filt_fft[None] * x_fft, axis=1)[:, :L]
            conv = conv + last_conv_c[None, None, :] * prog[None] * p[None, None, :]
            return conv.real.astype(x.dtype)

        def _forward(x, Win, bin, ln1_w, ln1_b, phz_re, phz_im, lc_re, lc_im, sc_lin, ln2_w, ln2_b, W1, b1, W2, b2, lnl_w, lnl_b, Wout, bout):
            h = jnp.einsum('blv,dv->bld', x, Win) + bin

            def body(h, p):
                l1w, l1b, pr, pi, lr, li, scl, l2w, l2b, w1, b1_, w2, b2_ = p
                y = jax.nn.silu(layernorm(h, l1w, l1b))
                y = sconv(y, pr + 1j * pi, lr + 1j * li)
                h = h + y * scl
                y = layernorm(h, l2w, l2b)
                y = jax.nn.silu(jnp.einsum('bld,fd->blf', y, w1) + b1_)
                y = jnp.einsum('blf,df->bld', y, w2) + b2_
                return (h + y, None)
            xs = (ln1_w, ln1_b, phz_re, phz_im, lc_re, lc_im, sc_lin, ln2_w, ln2_b, W1, b1, W2, b2)
            h, _ = jax.lax.scan(body, h, xs)
            h = layernorm(h, lnl_w, lnl_b)
            return jnp.einsum('bld,vd->blv', h, Wout) + bout
        return _forward(x, Win, bin, ln1_w, ln1_b, phz_re, phz_im, lc_re, lc_im, sc_lin, ln2_w, ln2_b, W1, b1, W2, b2, lnl_w, lnl_b, Wout, bout)

    def _L0_ffn_ref(x, W_base, b_base, W_router, A, B):
        import jax, jax.numpy as jnp
        import numpy as np
        NUM_EXPERTS = 8
        TOP_K = 2
        RANK = 16
        LORA_ALPHA = 32
        SCALING = LORA_ALPHA / RANK
        bs, seq, d_in = x.shape
        T = bs * seq
        xf = x.reshape(T, d_in)
        base = xf @ W_base.T + b_base
        logits = xf @ W_router.T
        rw, sel = jax.lax.top_k(logits, TOP_K)
        rw = jax.nn.softmax(rw, axis=-1)
        onehot = jax.nn.one_hot(sel, NUM_EXPERTS, dtype=rw.dtype)
        w = jnp.einsum('tk,tke->te', rw, onehot)
        h = jnp.einsum('td,erd->ter', xf, A)
        lora = jnp.einsum('ter,te,eor->to', h, w, B) * SCALING
        return (base + lora).reshape(bs, seq, -1)
    h = _L0_tok_ref(L0_tok_log_dt, x, L0_tok_B, L0_tok_inv_A_real, L0_tok_A_imag, 1024)
    h = h + _L0_attn_ref(_layernorm(h, axis=-1), L0_attn_Win, L0_attn_bin, L0_attn_ln1_w, L0_attn_ln1_b, L0_attn_phz_re, L0_attn_phz_im, L0_attn_lc_re, L0_attn_lc_im, L0_attn_sc_lin, L0_attn_ln2_w, L0_attn_ln2_b, L0_attn_W1, L0_attn_b1, L0_attn_W2, L0_attn_b2, L0_attn_lnl_w, L0_attn_lnl_b, L0_attn_Wout, L0_attn_bout)
    h = h + _L0_ffn_ref(_layernorm(h, axis=-1), L0_ffn_W_base, L0_ffn_b_base, L0_ffn_W_router, L0_ffn_A, L0_ffn_B)
    return h

_drawn_inputs = setup_inputs


def setup_inputs(seed=0):
    import zlib

    import numpy as np

    out = dict(_drawn_inputs(seed))
    spreads = {'L0_tok_inv_A_real': (-0.6931471824645996, 0.2),
     'L0_attn_bin': (0.0, 0.1),
     'L0_attn_ln1_w': (1.0, 0.2),
     'L0_attn_ln1_b': (0.0, 0.1),
     'L0_attn_sc_lin': (1.0, 0.2),
     'L0_attn_ln2_w': (1.0, 0.2),
     'L0_attn_ln2_b': (0.0, 0.1),
     'L0_attn_b1': (0.0, 0.1),
     'L0_attn_b2': (0.0, 0.1),
     'L0_attn_lnl_w': (1.0, 0.2),
     'L0_attn_lnl_b': (0.0, 0.1),
     'L0_attn_bout': (0.0, 0.1)}
    factors = {'L0_ffn_b_base': 3.305}
    for name, (base, spread) in spreads.items():
        noise = np.random.default_rng([zlib.crc32(name.encode()), seed]).standard_normal(out[name].shape)
        drawn = base * np.exp(spread * noise) if base else spread * noise
        out[name] = jnp.asarray(drawn.astype(out[name].dtype))
    for name, factor in factors.items():
        out[name] = (out[name] * factor).astype(out[name].dtype)
    return out
```

```python
from contextlib import ExitStack

import concourse.bass as bass
from concourse import mybir

F32 = mybir.dt.float32
F32R = mybir.dt.float32r
U32 = mybir.dt.uint32
I32 = mybir.dt.int32
ALU = mybir.AluOpType
ACT = mybir.ActivationFunctionType
AX_X = mybir.AxisListType.X

P = 128
C, L = 32, 1024
H = 128
D = 128
NL = 4
FC = 4
A = L // P
GH = 8
NG = H // GH
PAIR = 2
NP = GH // PAIR
CH = 4
NCH = C // CH
T = CH * H
E, RK = 8, 16
ER = E * RK
AR = ER + E
EPS = 1e-5
SCALING = 32 / RK
ROUND = 1.5 * 2.0 ** 23
TWO_PI = 6.283185
TWO_PI_HI = 6.28125
TWO_PI_LO = 0.0019353071795864769
LN2 = 0.6931471805599453
LN2_HI = 0.693359375
LN2_LO = -2.1219444005469057e-4
EXP_TERMS = [1 / 5040, 1 / 720, 1 / 120, 1 / 24, 1 / 6, 1 / 2, 1.0]
NPOW = 7

LN1W, LN1B, LN2W, LN2B, B2, B1, LNLW, LNLB, BOUT, ZRE, ZIM, CRE, CIM, SCL, SIGN, QUARTER, NVEC = (
    0, 4, 8, 12, 16, 20, 36, 37, 38, 46, 50, 54, 58, 62, 66, 67, 68)
A_IM, B_RE, B_IM, INV_A, LOG_DT, NPAR = 0, 1, 2, 3, 4, 5


def wait(eng, semaphore, value):
    if isinstance(value, int) and value <= 0:
        return
    eng.wait_ge(semaphore, value)


def plain(eng, ready):
    eng.nop(nofuse=True)


def steps(eng, body, n, unroll=2):
    for k in range(unroll):
        body(k, k % unroll)
    with eng.Fori(unroll, n - unroll, unroll) as i:
        for k in range(unroll):
            body(i + k, k)
    for k in range(n - unroll, n):
        body(k, k % unroll)


def tower_slots(eng, slot):
    def at(lay, t, lo, hi):
        def run(offset):
            if not lo <= t - offset < hi:
                return None
            return lay * NCH + (t - offset), (t - offset) % NCH, lay + (t - offset) // NCH
        slot(run)
    for t in range(NCH):
        at(0, t, 0, NCH)
    with eng.Fori(1, NL) as lay:
        for t in range(NCH):
            at(lay, t, -NCH, NCH)
    for t in range(NCH, NCH + 4):
        at(NL - 1, t, -NCH, NCH)


def build_program(nc, x1, x2, params, vecs_in, bin_in, win_t, w1_t, w2_t, wout_t, wbase_t, bbase_in,
                  ar_t, lora_b, k_spill, out):
    with ExitStack() as ctx:
        def sem(name):
            return ctx.enter_context(nc.semaphore(name))

        def held(stack, name, shape, dt=F32):
            return stack.enter_context(nc.sbuf_tensor(name, shape, dt))

        res = held(ctx, "res", [P, C, D])
        ident = held(ctx, "ident", [P, P])
        over_l = held(ctx, "over_l", [P, P])
        cos_t = held(ctx, "cos_t", [P, NL, H])
        sin_t = held(ctx, "sin_t", [P, NL, H])
        cos_s = held(ctx, "cos_s", [P, NL, H])
        sin_s = held(ctx, "sin_s", [P, NL, H])
        last_t = held(ctx, "last_t", [P, NL, D])
        vecs = held(ctx, "vecs", [P, NVEC])
        cols = held(ctx, "cols", [P, 20, NL])
        stat6 = held(ctx, "stat6", [P, 2, 2, CH, 6])
        mv = held(ctx, "mv", [P, 2, 2, CH, 2])
        vare = held(ctx, "vare", [P, 2, 2, CH])
        rstd = held(ctx, "rstd", [P, 2, 2, CH])
        powers = held(ctx, "powers", [P, 3, NL])
        iota8 = held(ctx, "iota8", [P, E])
        warm = held(ctx, "warm", [P, 1])
        ones = held(ctx, "ones", [P, 1])
        wmean = held(ctx, "wmean", [P, L])
        armean = held(ctx, "armean", [P, AR])

        psum = ctx.enter_context(nc.psum_tensor("psum", [P, 8, 512], F32))

        front = ExitStack()
        kt = held(front, "kt", [P, C, A, H])
        s1 = held(front, "s1", [P, H, A])
        s2 = held(front, "s2", [P, H, A])
        decay_pow = held(front, "decay_pow", [P, NPOW, H])
        turns = held(front, "turns", [P, H])
        iota_b = held(front, "iota_b", [P, H])
        x1b = held(front, "x1b", [P, 2, GH, C])
        x2b = held(front, "x2b", [P, 2, GH, C])
        angle = held(front, "angle", [P, GH, P])
        whole = held(front, "whole", [P, GH, P])
        decay = held(front, "decay", [P, GH, P])
        vand = held(front, "vand", [P, 2, GH, P])
        m1 = held(front, "m1", [P, 2, PAIR, A, C])
        m2 = held(front, "m2", [P, 2, PAIR, A, C])
        binb = held(front, "binb", [P, D])
        front.close()

        wbh = held(ctx, "wbh", [P, A, L], F32R)
        wbl = held(ctx, "wbl", [P, A, L], F32R)
        arc = held(ctx, "arc", [P, A, AR])
        lbh = held(ctx, "lbh", [P, L], F32R)
        lbl = held(ctx, "lbl", [P, L], F32R)
        wo = held(ctx, "wo", [P, L])
        bbase = held(ctx, "bbase", [P, L])
        wraw = held(ctx, "wraw", [P, 2, L])
        tower = ExitStack()
        xn1 = held(tower, "xn1", [P, 2, CH, D])
        xn2 = held(tower, "xn2", [P, 2, CH, D])
        act_s = held(tower, "act_s", [P, 2, CH, H])
        uc = held(tower, "uc", [P, CH, H])
        us = held(tower, "us", [P, 2, CH, H])
        scan_c = held(tower, "scan_c", [P, 2, CH, H])
        scan_s = held(tower, "scan_s", [P, 2, CH, H])
        zb = held(tower, "zb", [P, 2, T])
        hid = held(tower, "hid", [P, 2, FC, T])
        yb = held(tower, "yb", [P, 2, CH, H])
        w1c = held(tower, "w1c", [P, FC * P])
        w2c = held(tower, "w2c", [P, FC, D])
        dec = held(tower, "dec", [P, NL, CH, H])
        tower.close()
        xnf = held(ctx, "xnf", [P, 2, D])
        zf = held(ctx, "zf", [P, 2, H])
        kb = held(ctx, "kb", [P, 2, A, H])
        xf = held(ctx, "xf", [P, 2, A, H])
        xh = held(ctx, "xh", [P, 2, A, H], F32R)
        xl = held(ctx, "xl", [P, 2, A, H], F32R)
        h1 = held(ctx, "h1", [P, 2, L])
        lg = held(ctx, "lg", [P, 2, E])
        top = held(ctx, "top", [P, 2, 8])
        topi = held(ctx, "topi", [P, 2, 8], U32)
        gate = held(ctx, "gate", [P, 2, 10])
        wsel = held(ctx, "wsel", [P, 2, 2, E])
        gated = held(ctx, "gated", [P, 2, ER])
        gh = held(ctx, "gh", [P, 2, H], F32R)
        gl = held(ctx, "gl", [P, 2, H], F32R)
        bst = held(ctx, "bst", [P, 2, 2, 6])
        mvo = held(ctx, "mvo", [P, 2, 2])
        rso = held(ctx, "rso", [P, 2, 2])
        bsf = held(ctx, "bsf", [P, 2, 6])
        mvf = held(ctx, "mvf", [P, 2, 2])
        rsf = held(ctx, "rsf", [P, 2, 2])

        s_vecs, s_par, s_win, s_bin = (sem(n) for n in ("s_vecs", "s_par", "s_win", "s_bin"))
        s_x = [sem("s_x0"), sem("s_x1")]
        s_const, s_ident = sem("s_const"), sem("s_ident")
        s_dve, s_pool = sem("s_dve"), sem("s_pool")
        s_setd, s_seta = sem("s_setd"), sem("s_seta")
        s_angle, s_sin, s_decay, s_vand = sem("s_angle"), sem("s_sin"), sem("s_decay"), sem("s_vand")
        s_m1, s_m2, s_kp, s_ke = sem("s_m1"), sem("s_m2"), sem("s_kp"), sem("s_ke")
        s_wmean, s_winc = sem("s_wmean"), sem("s_winc")
        s_sq, s_red, s_stat, s_wvar, s_wr = sem("s_sq"), sem("s_red"), sem("s_stat"), sem("s_wvar"), sem("s_wr")
        s_proj, s_projb, s_projt, s_res = sem("s_proj"), sem("s_projb"), sem("s_projt"), sem("s_res")
        s_dvew, s_half, s_sum = sem("s_dvew"), sem("s_half"), sem("s_sum")
        s_spill = sem("s_spill")
        (s_bn1, s_mv1, s_ve1, s_rs1, s_xn1, s_ta, s_s, s_us, s_uc, s_sc, s_ss, s_m1t, s_m2t, s_m, s_hl, s_tb,
         s_h1, s_bn2, s_mv2, s_ve2, s_rs2, s_xn2, s_tc, s_z, s_w1, s_hid, s_w2, s_y, s_td, s_h2, s_wl) = (
            sem(n) for n in (
                "bn1", "mv1", "ve1", "rs1", "xn1_ready", "ta", "s_ready", "us", "uc", "sc", "ss", "m1t", "m2t",
                "m_ready", "hl", "tb", "h1_done", "bn2", "mv2", "ve2", "rs2", "xn2_ready", "tc", "z_ready", "w1_done",
                "hid_ready", "w2_done", "y_ready", "td", "h2_done", "wl"))
        (f_bn, f_mv, f_ve, f_rs, f_xn, f_tp, f_z, f_wo, f_kb, f_x, f_xh, f_xl) = (
            sem("f_" + n) for n in ("bn", "mv", "ve", "rs", "xn", "tp", "z", "wo", "kb", "x", "xh", "xl"))
        (o_px, o_pa, o_h1, o_bn, o_mv, o_ve, o_rs, o_hb, o_rt, o_gd, o_e, o_g, o_gt, o_gh, o_gl, o_fin, o_out,
         o_st) = (sem("o_" + n) for n in ("px", "pa", "h1", "bn", "mv", "ve", "rs", "hb", "rt", "gd", "e", "g",
                                          "gt", "gh", "gl", "fin", "out", "st"))
        o_wt = sem("o_wt")
        p_raw, f_k = ([sem(n + "0"), sem(n + "1")] for n in ("p_raw", "f_k"))
        p_early, p_mean, p_means, p_cen, p_hi, p_lo, p_arc, p_arcen, p_rest = (
            sem("p_" + n) for n in ("early", "mean", "means", "cen", "hi", "lo", "arc", "arcen", "rest"))
        s_tanh, s_tab, s_lastp, s_last, s_dec = (sem(n) for n in ("s_tanh", "s_tab", "s_lastp", "s_last", "s_dec"))


        block = ctx.enter_context(nc.Block())
        par = kt[:, 0:NPAR, 0, :]

        def big(i):
            return kt[:, 8 + i].rearrange("p a h -> p (a h)").rearrange("p (h a) -> p h a", a=A)

        def col(i):
            return kt[:, 16 + i // 8, i % 8, :]

        lam, psi, em1, sh, sn, t0, t1, t2, gr, gi, kk, fr = (col(i) for i in range(12))
        ex, en, er, eq, es = (kt[:, 18 + i, 0:2, :] for i in range(5))
        a_, dt_ = ex[:, 0], ex[:, 1]
        ea, va, vb, ca, sa = (big(i) for i in range(5))
        wr_, wi_ = big(5), big(6)

        w_early = kt[:, 24:32].rearrange("p c a h -> p c (a h)")
        ar_early = kt[:, 6:8].rearrange("p c a h -> p (c a h)")[:, 0:A * AR].rearrange("p (a n) -> p a n", a=A)

        win_early = res[:, 0:A, :]
        winc = s2[:].rearrange("p h a -> p (h a)").rearrange("p (a d) -> p a d", a=A)

        @block.sync
        def _(sp):
            sp.dma_start(par, params).then_inc(s_par, 16)
            sp.dma_start(vecs[:], vecs_in).then_inc(s_vecs, 16)
            sp.dma_start(win_early, win_t).then_inc(s_win, 16)
            sp.dma_start(binb[:], bin_in).then_inc(s_bin, 16)
            sp.dma_start(ar_early, ar_t).then_inc(p_early, 16)
            for k in range(0, A, 4):
                sp.dma_start(w_early[:, k:k + 4], wbase_t[:, k:k + 4, :]).then_inc(p_early, 16)

            def load_x(q, u):
                wait(sp, s_kp, (q - 1) * NP)
                sp.dma_start(x1b[:, u], x1[:, bass.ds(q * GH, GH), :]).then_inc(s_x[u], 16)
                sp.dma_start(x2b[:, u], x2[:, bass.ds(q * GH, GH), :]).then_inc(s_x[u], 16)
            steps(sp, load_x, NG)

            sp.wait_ge(s_ke, H // PAIR)
            with sp.Fori(0, C) as c:
                sp.dma_start(k_spill[bass.ds(c, 1)].rearrange("o p a h -> p (o a) h"),
                             kt[:, bass.ds(c, 1)].rearrange("p o a h -> p (o a) h")).then_inc(s_spill, 16)
            sp.wait_ge(s_spill, 16 * C)

            sp.wait_ge(s_res, NCH)

            def load_layer(lay):
                wait(sp, s_w2, lay * NCH)
                sp.dma_start(w1c[:], w1_t[bass.ds(lay, 1)].rearrange("o d f -> (o d) f")).then_inc(s_wl, 16)
                sp.dma_start(w2c[:], w2_t[bass.ds(lay, 1)].rearrange("o f c d -> (o f) c d")).then_inc(s_wl, 16)
            load_layer(0)
            sp.dma_start(arc[:], ar_t).then_inc(p_arc, 16)
            sp.dma_start(bbase[:], bbase_in).then_inc(p_rest, 16)
            sp.dma_start(wo[:], wout_t).then_inc(p_rest, 16)
            for i in range(1 + A):
                wait(sp, p_lo, i - 1)
                sp.dma_start(wraw[:, i % 2, :], lora_b if i == 0 else wbase_t[:, i - 1, :]).then_inc(p_raw[i % 2], 16)
            with sp.Fori(1, NL) as lay:
                load_layer(lay)
            sp.wait_ge(s_h2, NL * NCH)

            def load_k(c, u):
                wait(sp, f_x, c - 1)
                sp.dma_start(kb[:, u], k_spill[bass.ds(c, 1)].rearrange("o p a h -> (o p) a h")).then_inc(f_k[u], 16)

            load_k(0, 0)

            def store(c, u):
                if not (isinstance(c, int) and c == C - 1):
                    load_k(c + 1, 1 - u)
                sp.wait_ge(o_out, c + 1)
                sp.dma_start(out[bass.ds(c * H, H), :], h1[:, u, :]).then_inc(o_st, 16)
            steps(sp, store, C)
            sp.wait_ge(o_st, 16 * C)

        @block.gpsimd
        def _(pool):
            g = nc.gpsimd
            g.memset(over_l[:], 1.0 / L)
            g.memset(ones[:], 1.0)
            for i, e in enumerate((-0.5, 0.5, -1.0)):
                g.memset(powers[:, i, :], e)
            g.iota(iota_b[:], [[1, H]], base=0, channel_multiplier=0, allow_small_or_imprecise_dtypes=True)
            g.iota(iota8[:], [[1, E]], base=0, channel_multiplier=0, allow_small_or_imprecise_dtypes=True)
            g.memset(ident[:], 0.0).then_inc(s_const, 1)
            pool.wait_ge(s_const, 1)
            g.affine_select(out=ident[:], in_=ident[:], compare_op=ALU.not_equal, fill=1.0, base=0,
                            pattern=[[-1, P]], channel_multiplier=1).then_inc(s_ident, 1)

            done = [0]

            def step(ins):
                done[0] += 1
                ins.then_inc(s_pool, 1)
                pool.wait_ge(s_pool, done[0])

            def v(i):
                return vecs[:, i:i + NL]

            (r2, zero, rad, inv, cr, ci, mag, c1, c2, c3, pc, ps, pr, lgr, lgi) = (cols[:, i] for i in range(15))
            pool.wait_ge(s_vecs, 16)
            tt = g.tensor_tensor
            step(tt(r2, v(ZRE), v(ZRE), ALU.mult))
            step(tt(c1, v(ZIM), v(ZIM), ALU.mult))
            step(tt(r2, r2, c1, ALU.add))
            step(g.tensor_scalar(zero, r2, 0.0, None, ALU.is_equal))
            step(tt(rad, r2, powers[:, 1], ALU.pow))
            step(tt(c1, rad, zero, ALU.add))
            step(tt(inv, c1, powers[:, 2], ALU.pow))
            step(tt(c1, v(ZRE), zero, ALU.add))
            step(tt(cr, c1, inv, ALU.mult))
            tt(ci, v(ZIM), inv, ALU.mult).then_inc(s_tab, 1)
            pool.wait_ge(s_tab, 1)
            pool.wait_ge(s_tanh, 1)
            rp = vand[:, 0, 0:NL, :]
            b1_, b2_, b3_, b4_ = vand[:, 0, NL:GH, :], vand[:, 1, 0:NL, :], vand[:, 1, NL:GH, :], decay[:, 0:NL, :]
            g.memset(cos_t[:, :, 0:1], 1.0)
            g.memset(rp[:, :, 0:1], 1.0)
            step(g.memset(sin_t[:, :, 0:1], 0.0))
            step(g.tensor_copy(pc, cr))
            step(g.tensor_copy(ps, ci))
            step(g.tensor_copy(pr, mag))
            for k in range(NPOW):
                n = 1 << k

                def wide(x):
                    return x.unsqueeze(2).broadcast_to([P, NL, n])
                tt(b1_[:, :, 0:n], cos_t[:, :, 0:n], wide(pc), ALU.mult)
                tt(b2_[:, :, 0:n], sin_t[:, :, 0:n], wide(ps), ALU.mult)
                tt(b3_[:, :, 0:n], cos_t[:, :, 0:n], wide(ps), ALU.mult)
                tt(b4_[:, :, 0:n], sin_t[:, :, 0:n], wide(pc), ALU.mult)
                step(tt(rp[:, :, n:2 * n], rp[:, :, 0:n], wide(pr), ALU.mult))
                tt(cos_t[:, :, n:2 * n], b1_[:, :, 0:n], b2_[:, :, 0:n], ALU.subtract)
                step(tt(sin_t[:, :, n:2 * n], b3_[:, :, 0:n], b4_[:, :, 0:n], ALU.add))
                if k < NPOW - 1:
                    tt(c1, pc, pc, ALU.mult)
                    tt(c2, ps, ps, ALU.mult)
                    step(tt(c3, pc, ps, ALU.mult))
                    tt(pc, c1, c2, ALU.subtract)
                    tt(ps, c3, c3, ALU.add)
                    step(tt(pr, pr, pr, ALU.mult))
            tt(c1, mag, cr, ALU.mult)
            step(tt(c2, mag, ci, ALU.mult))
            step(tt(lgr, v(CRE), c1, ALU.mult))
            step(tt(c3, v(CIM), c2, ALU.mult))
            step(tt(lgr, lgr, c3, ALU.subtract))
            step(tt(lgi, v(CRE), c2, ALU.mult))
            step(tt(c3, v(CIM), c1, ALU.mult))
            step(tt(lgi, lgi, c3, ALU.add))

            def row(x):
                return x.unsqueeze(2).broadcast_to([P, NL, H])
            tt(b1_, cos_t[:], row(lgr), ALU.mult)
            step(tt(b2_, sin_t[:], row(lgi), ALU.mult))
            step(tt(b1_, b1_, b2_, ALU.subtract))
            step(tt(b1_, b1_, rp, ALU.mult))
            tt(b1_, b1_, row(v(SCL)), ALU.mult)
            tt(cos_s[:], cos_t[:], row(v(SCL)), ALU.mult)
            tt(sin_s[:], sin_t[:], row(v(SCL)), ALU.mult).then_inc(s_tab, 1)
            pool.wait_ge(s_tab, 2)
            g.memset(decay[:, :, 0:1], 1.0).then_inc(s_const, 1)
            pool.wait_ge(s_const, 2)

            def make_decay(q, u):
                wait(pool, s_vand, q)
                for k in range(NPOW):
                    n = 1 << k
                    if k:
                        pool.wait_ge(s_decay, q * NPOW + k)
                    plain(pool, s_const)
                    g.tensor_tensor(decay[:, :, n:2 * n], decay[:, :, 0:n],
                                    decay_pow[:, k, bass.ds(q * GH, GH)].unsqueeze(2).broadcast_to([P, GH, n]),
                                    ALU.mult).then_inc(s_decay, 1)

            def make_m1(q, u):
                pool.wait_ge(s_x[u], (q - u) * 16 + 32)
                for p in range(NP):
                    wait(pool, s_kp, q * NP + p - 1)
                    plain(pool, s_const)
                    g.tensor_tensor(
                        m1[:, p % 2],
                        x1b[:, u, PAIR * p:PAIR * (p + 1), :].unsqueeze(2).broadcast_to([P, PAIR, A, C]),
                        s1[:, bass.ds(q * GH + PAIR * p, PAIR), :].unsqueeze(3).broadcast_to([P, PAIR, A, C]),
                        ALU.mult).then_inc(s_m1, 1)

            pool.wait_ge(s_setd, 3)
            make_decay(0, 0)
            pool.wait_ge(s_setd, 4)

            def group(q, u):
                if not (isinstance(q, int) and q == NG - 1):
                    make_decay(q + 1, 1 - u)
                make_m1(q, u)
            steps(pool, group, NG)

            pool.wait_ge(s_ke, H // PAIR)
            half = vand[:, 0, 0:NL, :]
            quarter = vand[:, 1, 0:2, :]

            def win_rstd(j, u):
                for c in range(CH):
                    kc = kt[:, bass.ds(j * CH + c, 1)].rearrange("p o a h -> p (o a) h")
                    i = (j * CH + c) * 2
                    plain(pool, s_const)
                    tt(half, kc[:, 0:A // 2, :], kc[:, A // 2:A, :], ALU.add).then_inc(s_half, 1)
                    pool.wait_ge(s_half, i + 1)
                    tt(quarter, half[:, 0:2], half[:, 2:4], ALU.add).then_inc(s_half, 1)
                    pool.wait_ge(s_half, i + 2)
                    wait(pool, s_stat, j * CH + c - 1)
                    tt(m2[:, c % 2, 0].rearrange("p a c -> p (a c)")[:, 0:H], quarter[:, 0], quarter[:, 1],
                       ALU.add).then_inc(s_sum, 1)
                pool.wait_ge(s_wvar, j + 1)
                g.tensor_tensor(rstd[:, 0, u], vare[:, 0, u], powers[:, 0, 0:CH], ALU.pow).then_inc(s_wr, 1)
            steps(pool, win_rstd, NCH)

            pool.wait_ge(s_res, NCH)
            pool.wait_ge(s_spill, 16 * C)
            pool.wait_ge(s_last, 1)
            step(g.memset(dec[:], 1.0))
            for k in range(NL):
                g.tensor_scalar(dec[:, k], dec[:, k], mag[:, k:k + 1], None, ALU.mult)
            step(g.tensor_scalar(warm[:], over_l[:, 0:1], 1.0, None, ALU.mult))
            g.memset(dec[:, :, :, 0:1], 0.0).then_inc(s_dec, 1)

            def rstd_of(count, which, u, s_in, s_eps, s_out):
                pool.wait_ge(s_in, count + 1)
                plain(pool, s_const)
                g.tensor_scalar(vare[:, which, u], mv[:, which, u, :, 1], EPS, None, ALU.add).then_inc(s_eps, 1)
                pool.wait_ge(s_eps, count + 1)
                tt(rstd[:, which, u], vare[:, which, u], powers[:, 0, 0:CH], ALU.pow).then_inc(s_out, 1)

            def slot(run):
                if s0 := run(0):
                    k, n, lay = s0
                    rstd_of(k, 0, n % 2, s_mv1, s_ve1, s_rs1)
                if s1_ := run(1):
                    k, n, lay = s1_
                    pool.wait_ge(s_s, k + 1)
                    wait(pool, s_ss, k - 1)
                    plain(pool, s_const)
                    tt(us[:, n % 2], act_s[:, n % 2], sin_t[:, bass.ds(lay, 1), :].broadcast_to([P, CH, H]),
                       ALU.mult).then_inc(s_us, 1)
                if s2_ := run(2):
                    k, n, lay = s2_
                    rstd_of(k, 1, n % 2, s_mv2, s_ve2, s_rs2)
                if s0:
                    k, n, lay = s0
                    pool.wait_ge(s_xn1, k + 1)
                    plain(pool, s_const)
                    r = res[:, n * CH:(n + 1) * CH, :]
                    tt(r, r, last_t[:, bass.ds(lay, 1), :].broadcast_to([P, CH, D]), ALU.add).then_inc(s_hl, 1)
                if s1_:
                    k, n, lay = s1_
                    sc = scan_c[:, n % 2]
                    pool.wait_ge(s_sc, k + 1)
                    plain(pool, s_const)
                    tt(sc, sc, cos_s[:, bass.ds(lay, 1), :].broadcast_to([P, CH, H]), ALU.mult).then_inc(s_m1t, 1)
                    pool.wait_ge(s_m1t, k + 1)
                    pool.wait_ge(s_m2t, k + 1)
                    tt(sc, sc, scan_s[:, n % 2], ALU.add).then_inc(s_m, 1)
            def centre(i):
                k = i - 1
                pool.wait_ge(p_raw[i % 2], 16 * (i // 2 + 1))
                if i:
                    tt(wraw[:, i % 2], wraw[:, i % 2], wmean[:], ALU.subtract).then_inc(p_cen, 1)
                pool.wait_ge(p_hi, i + 1)
                hi, lo = (wbh[:, k], wbl[:, k]) if i else (lbh[:], lbl[:])
                tt(lo, wraw[:, i % 2], hi.bitcast(F32), ALU.subtract).then_inc(p_lo, 1)

            def slot_and_centre(run):
                slot(run)
                s0 = run(0)
                if s0 and isinstance(s0[2], int):
                    centre(s0[1] + 1)

            pool.wait_ge(p_means, 1)
            pool.wait_ge(p_arc, 16)
            tt(arc[:], arc[:], armean[:].unsqueeze(1).broadcast_to([P, A, AR]), ALU.subtract).then_inc(p_arcen, 1)
            centre(0)
            tower_slots(pool, slot_and_centre)

            def front_rstd(c, u):
                pool.wait_ge(f_mv, c + 1)
                plain(pool, s_const)
                g.tensor_scalar(rsf[:, u, 0:1], mvf[:, u, 1:2], EPS, None, ALU.add).then_inc(f_ve, 1)
                pool.wait_ge(f_ve, c + 1)
                tt(rsf[:, u, 1:2], rsf[:, u, 0:1], powers[:, 0, 0:1], ALU.pow).then_inc(f_rs, 1)

            def front_bias(c, u):
                pool.wait_ge(f_k[u], (c - u) * 8 + 16)
                tt(kb[:, u], kb[:, u], vecs[:, BOUT:BOUT + A].unsqueeze(2).broadcast_to([P, A, H]),
                   ALU.add).then_inc(f_kb, 1)

            pool.wait_ge(p_rest, 32)
            pool.wait_ge(s_h2, NL * NCH)
            front_rstd(0, 0)
            front_bias(0, 0)

            def last(c, u):
                more = not (isinstance(c, int) and c == C - 1)
                if more:
                    front_rstd(c + 1, 1 - u)
                pool.wait_ge(o_mv, c + 1)
                plain(pool, s_const)
                g.tensor_scalar(rso[:, u, 0:1], mvo[:, u, 1:2], EPS, None, ALU.add).then_inc(o_ve, 1)
                pool.wait_ge(o_ve, c + 1)
                tt(rso[:, u, 1:2], rso[:, u, 0:1], powers[:, 0, 0:1], ALU.pow).then_inc(o_rs, 1)
                if more:
                    front_bias(c + 1, 1 - u)
                tt(h1[:, u], h1[:, u], bbase[:], ALU.add).then_inc(o_hb, 1)
            steps(pool, last, C)

        @block.scalar
        def _(act):
            a = nc.scalar.activation
            act.wait_ge(s_tab, 1)
            a(cols[:, 6], cols[:, 2], ACT.Tanh).then_inc(s_tanh, 1)
            act.wait_ge(s_setd, 1)
            a(sh, turns[:], ACT.Sin, scale=TWO_PI / 2)
            a(sn, turns[:], ACT.Sin, scale=TWO_PI).then_inc(s_seta, 1)
            act.wait_ge(s_setd, 2)
            a(ca, va, ACT.Sin, scale=TWO_PI)
            a(sa, vb, ACT.Sin, scale=TWO_PI).then_inc(s_seta, 1)

            def sines(q, u):
                act.wait_ge(s_angle, q * 3 + 3)
                a(whole[:], angle[:], ACT.Sin, scale=TWO_PI).then_inc(s_sin, 1)

            def evacuate(q, u):
                for p in range(NP):
                    act.wait_ge(s_kp, q * NP + p + 1)
                    plain(act, s_ident)
                    a(kt[:, :, :, bass.ds(q * GH + p * PAIR, PAIR)].rearrange("p c a h -> p h a c"),
                      psum[:, p, :].rearrange("p (h a c) -> p h a c", h=PAIR, a=A), ACT.Copy).then_inc(s_ke, 1)
            act.wait_ge(p_mean, 1)
            nc.scalar.copy(armean[:], psum[:, 6, 0:AR])
            nc.scalar.copy(wmean[:].rearrange("p (b n) -> p b n", b=2), psum[:, 4:6, :]).then_inc(p_means, 1)
            act.wait_ge(s_lastp, 1)
            a(last_t[:].rearrange("p l d -> p (l d)"), psum[:, 0, :], ACT.Copy).then_inc(s_last, 1)
            act.wait_ge(s_setd, 4)
            sines(0, 0)

            def group(q, u):
                if not (isinstance(q, int) and q == NG - 1):
                    sines(q + 1, 1 - u)
                evacuate(q, u)
            steps(act, group, NG)

            act.wait_ge(s_m2, H // PAIR)
            act.wait_ge(s_winc, 1)
            nc.scalar.copy(winc, win_early).then_inc(s_winc, 1)
            act.wait_ge(s_ke, H // PAIR)

            def project(j, u):
                for c in range(CH):
                    wait(act, s_red, j * CH + c - 1)
                    plain(act, s_ident)
                    a((angle if c % 2 == 0 else whole)[:], kt[:, bass.ds(j * CH + c, 1)].rearrange("p o a h -> p (o a) h"),
                      ACT.Square).then_inc(s_sq, 1)
                act.wait_ge(s_proj, j + 1)
                wait(act, s_projt, j - 1)
                a(m1[:, u].rearrange("p h a c -> p (h a c)"), psum[:, u, :], ACT.Copy).then_inc(s_projb, 1)
            steps(act, project, NCH)

            act.wait_ge(s_spill, 16 * C)
            act.wait_ge(s_res, NCH)

            def vec(i):
                return vecs[:, bass.ds(i, 1)]

            def slot(run):
                if s3 := run(3):
                    k, n, lay = s3
                    wait(act, s_w2, k - 1)
                    for f in range(FC):
                        act.wait_ge(s_w1, k * FC + f + 1)
                        plain(act, s_ident)
                        a(hid[:, n % 2, f, :], psum[:, 3 + f, :], ACT.Silu, bias=vec(lay * FC + B1 + f)).then_inc(s_hid, 1)
                if s0 := run(0):
                    k, n, lay = s0
                    act.wait_ge(s_ta, k + 1)
                    wait(act, s_us, k - 1)
                    wait(act, s_uc, k - 1)
                    plain(act, s_ident)
                    a(act_s[:, n % 2].rearrange("p c h -> p (c h)"), psum[:, 0, :], ACT.Silu, bias=vec(lay + LN1B),
                      scale=vec(lay + LN1W)).then_inc(s_s, 1)
                if s3:
                    k, n, lay = s3
                    act.wait_ge(s_w2, k + 1)
                    wait(act, s_td, k - 1)
                    plain(act, s_ident)
                    a(yb[:, n % 2].rearrange("p c h -> p (c h)"), psum[:, 7, :], ACT.Identity,
                      bias=vec(lay + B2)).then_inc(s_y, 1)
                if s2_ := run(2):
                    k, n, lay = s2_
                    act.wait_ge(s_tc, k + 1)
                    wait(act, s_w1, (k - 1) * FC)
                    plain(act, s_ident)
                    a(zb[:, n % 2], psum[:, 0, :], ACT.Identity, bias=vec(lay + LN2B),
                      scale=vec(lay + LN2W)).then_inc(s_z, 1)
            def leading(i):
                if i:
                    act.wait_ge(p_cen, i)
                else:
                    act.wait_ge(p_raw[0], 16)
                nc.scalar.copy(wbh[:, i - 1] if i else lbh[:], wraw[:, i % 2]).then_inc(p_hi, 1)

            def slot_and_leading(run):
                slot(run)
                s0 = run(0)
                if s0 and isinstance(s0[2], int):
                    leading(s0[1] + 1)
            leading(0)
            tower_slots(act, slot_and_leading)
            act.wait_ge(s_h2, NL * NCH)

            def front_z(c, u):
                act.wait_ge(f_tp, c + 1)
                wait(act, f_wo, c - 1)
                a(zf[:, u], psum[:, 7, 0:H], ACT.Identity, bias=vecs[:, LNLB:LNLB + 1],
                  scale=vecs[:, LNLW:LNLW + 1]).then_inc(f_z, 1)

            def front_xh(c, u):
                act.wait_ge(f_x, c + 1)
                wait(act, o_fin, c - 1)
                nc.scalar.copy(xh[:, u], xf[:, u]).then_inc(f_xh, 1)

            front_z(0, 0)
            front_xh(0, 0)

            def last(c, u):
                more = not (isinstance(c, int) and c == C - 1)
                act.wait_ge(o_px, c + 1)
                wait(act, o_st, 16 * (c - 1))
                nc.scalar.copy(h1[:, u].rearrange("p (b n) -> p b n", b=2), psum[:, 2:4, :]).then_inc(o_h1, 1)
                if more:
                    front_z(c + 1, 1 - u)
                act.wait_ge(o_gd, c + 1)
                act.wait_ge(o_rs, c + 1)
                a(gate[:, u, 3:4], gate[:, u, 2:3], ACT.Exp, scale=rso[:, u, 1:2]).then_inc(o_e, 1)
                act.wait_ge(o_gt, c + 1)
                wait(act, o_fin, c - 1)
                nc.scalar.copy(gh[:, u], psum[:, 7, 0:H]).then_inc(o_gh, 1)
                if more:
                    front_xh(c + 1, 1 - u)
            steps(act, last, C)

        @block.vector
        def _(dve):
            v = nc.vector
            tt, ts, stt = v.tensor_tensor, v.tensor_scalar, v.scalar_tensor_tensor
            done = [0]

            def step(ins):
                done[0] += 1
                ins.then_inc(s_dve, 1)
                dve.wait_ge(s_dve, done[0])

            def exp_parts(x, rows):
                n, r, q, sc = (t[:, 0:rows] for t in (en, er, eq, es))
                step(ts(n, x, 1.0 / LN2, ROUND, ALU.mult, ALU.add))
                step(ts(n, n, -ROUND, None, ALU.add))
                step(stt(r, n, -LN2_HI, x, ALU.mult, ALU.add))
                ts(sc.bitcast(I32), n, 127.0, 2.0 ** 23, ALU.add, ALU.mult)
                step(stt(r, n, -LN2_LO, r, ALU.mult, ALU.add))
                step(ts(q, r, EXP_TERMS[0], None, ALU.mult))
                for term in EXP_TERMS[1:]:
                    step(stt(q, q, term, r, ALU.add, ALU.mult))

            dve.wait_ge(s_par, 16)
            step(ts(ex, par[:, INV_A:INV_A + 2], -87.0, 88.0, ALU.max, ALU.min))
            exp_parts(ex, 2)
            step(stt(ex, eq, 1.0, es, ALU.add, ALU.mult))
            step(stt(lam, a_, -1.0, dt_, ALU.mult, ALU.mult))
            step(tt(psi, par[:, A_IM], dt_, ALU.mult))
            step(ts(kk, psi, 1.0 / (TWO_PI_HI + TWO_PI_LO), None, ALU.mult))
            step(ts(kk, kk, ROUND, -ROUND, ALU.add, ALU.add))
            step(stt(t0, kk, -TWO_PI_HI, psi, ALU.mult, ALU.add))
            step(stt(t0, kk, -TWO_PI_LO, t0, ALU.mult, ALU.add))
            step(ts(t0, t0, 1.0 / (TWO_PI_HI + TWO_PI_LO), None, ALU.mult))
            step(ts(t1, t0, ROUND, -ROUND, ALU.add, ALU.add))
            tt(turns[:], t0, t1, ALU.subtract).then_inc(s_setd, 1)
            dve.wait_ge(s_setd, 1)
            step(ts(fr, turns[:], float(P), None, ALU.mult))
            step(ts(t0, fr, ROUND, -ROUND, ALU.add, ALU.add))
            step(tt(fr, fr, t0, ALU.subtract))
            for k in range(A):
                ts(va[:, :, k], fr, float(k), 0.25, ALU.mult, ALU.add)
                ins = ts(vb[:, :, k], fr, float(k), None, ALU.mult)
            step(ins)
            step(ts(ca, va, ROUND, -ROUND, ALU.add, ALU.add))
            step(ts(sa, vb, ROUND, -ROUND, ALU.add, ALU.add))
            tt(va, va, ca, ALU.subtract)
            tt(vb, vb, sa, ALU.subtract).then_inc(s_setd, 1)
            step(ts(t1, lam, -87.0, None, ALU.max))
            exp_parts(t1.unsqueeze(1), 1)
            step(ts(t0, es[:, 0], -1.0, None, ALU.add))
            step(tt(t1, eq[:, 0], es[:, 0], ALU.mult))
            step(tt(em1, t0, t1, ALU.add))
            step(v.tensor_copy(t0, em1))
            for k in range(NPOW):
                ts(decay_pow[:, k], t0, 1.0, None, ALU.add)
                step(stt(t0, t0, 2.0, t0, ALU.add, ALU.mult))
            ts(ea[:, :, 0], t0, 0.0, 1.0, ALU.mult, ALU.add)
            ts(ea[:, :, 1], t0, 1.0, None, ALU.add).then_inc(s_setd, 1)
            dve.wait_ge(s_setd, 3)
            for k in range(2, A):
                step(tt(ea[:, :, k], ea[:, :, k - 1], ea[:, :, 1], ALU.mult))
            dve.wait_ge(s_seta, 1)
            step(tt(sh, sh, sh, ALU.mult))
            step(ts(sh, sh, 2.0, None, ALU.mult))
            step(ts(t0, sh, -1.0, 1.0, ALU.mult, ALU.add))
            step(tt(t0, em1, t0, ALU.mult))
            step(tt(t0, t0, sh, ALU.subtract))
            step(stt(t1, em1, 1.0, sn, ALU.add, ALU.mult))
            step(tt(gr, par[:, B_RE], t0, ALU.mult))
            step(tt(t2, par[:, B_IM], t1, ALU.mult))
            step(tt(gr, gr, t2, ALU.subtract))
            step(tt(gi, par[:, B_RE], t1, ALU.mult))
            step(tt(t2, par[:, B_IM], t0, ALU.mult))
            step(tt(gi, gi, t2, ALU.add))
            step(tt(t0, a_, a_, ALU.mult))
            step(tt(t1, par[:, A_IM], par[:, A_IM], ALU.mult))
            step(tt(t0, t0, t1, ALU.add))
            step(v.reciprocal(t0, t0))
            step(stt(t1, a_, -2.0, t0, ALU.mult, ALU.mult))
            step(stt(t2, par[:, A_IM], -2.0, t0, ALU.mult, ALU.mult))
            step(tt(kk, gr, t1, ALU.mult))
            step(tt(fr, gi, t2, ALU.mult))
            step(tt(kk, kk, fr, ALU.subtract))
            step(tt(fr, gr, t2, ALU.mult))
            step(tt(gi, gi, t1, ALU.mult))
            step(tt(gi, gi, fr, ALU.add))

            def along(x):
                return x.unsqueeze(2).broadcast_to([P, H, A])
            dve.wait_ge(s_seta, 2)
            step(tt(va, ca, along(kk), ALU.mult))
            step(tt(vb, sa, along(gi), ALU.mult))
            step(tt(wr_, va, vb, ALU.subtract))
            step(tt(va, sa, along(kk), ALU.mult))
            step(tt(vb, ca, along(gi), ALU.mult))
            step(tt(wi_, va, vb, ALU.add))
            dve.wait_ge(s_vecs, 16)
            stt(s1[:], wr_, vecs[:, SIGN:SIGN + 1], ea, ALU.mult, ALU.mult)
            stt(s2[:], wi_, -1.0, ea, ALU.mult, ALU.mult).then_inc(s_setd, 1)
            dve.wait_ge(s_const, 1)
            dve.wait_ge(s_win, 16)
            dve.wait_ge(s_wmean, 1)
            tt(win_early, win_early, psum[:, 7, 0:D].unsqueeze(1).broadcast_to([P, A, D]),
               ALU.subtract).then_inc(s_winc, 1)

            def make_angles(q, u):
                wait(dve, s_sin, q)
                for k in range(GH):
                    ins = ts(angle[:, k, :], iota_b[:], turns[:, bass.ds(q * GH + k, 1)],
                             vecs[:, QUARTER:QUARTER + 1], ALU.mult, ALU.add)
                ins.then_inc(s_angle, 1)
                dve.wait_ge(s_angle, q * 3 + 1)
                ts(whole[:], angle[:], ROUND, -ROUND, ALU.add, ALU.add).then_inc(s_angle, 1)
                dve.wait_ge(s_angle, q * 3 + 2)
                tt(angle[:], angle[:], whole[:], ALU.subtract).then_inc(s_angle, 1)

            def make_vand(q, u):
                dve.wait_ge(s_sin, q + 1)
                dve.wait_ge(s_decay, (q + 1) * NPOW)
                wait(dve, s_kp, (q - 1) * NP)
                tt(vand[:, u], decay[:], whole[:], ALU.mult).then_inc(s_vand, 1)

            def make_m2(q, u, pairs):
                dve.wait_ge(s_x[u], (q - u) * 16 + 32)
                for p in pairs:
                    wait(dve, s_kp, q * NP + p - 1)
                    tt(m2[:, p % 2],
                       x2b[:, u, PAIR * p:PAIR * (p + 1), :].unsqueeze(2).broadcast_to([P, PAIR, A, C]),
                       s2[:, bass.ds(q * GH + PAIR * p, PAIR), :].unsqueeze(3).broadcast_to([P, PAIR, A, C]),
                       ALU.mult).then_inc(s_m2, 1)

            dve.wait_ge(s_setd, 4)
            make_angles(0, 0)
            dve.wait_ge(s_last, 1)
            make_vand(0, 0)

            def group(q, u):
                more = not (isinstance(q, int) and q == NG - 1)
                if more:
                    dve.wait_ge(s_vand, q + 1)
                    make_angles(q + 1, 1 - u)
                make_m2(q, u, range(NP // 2))
                if more:
                    make_vand(q + 1, 1 - u)
                make_m2(q, u, range(NP // 2, NP))
            steps(dve, group, NG)

            dve.wait_ge(s_bin, 16)
            dve.wait_ge(s_winc, 2)

            dve.wait_ge(s_ke, H // PAIR)
            def project(j, u):
                for c in range(CH):
                    wait(dve, s_stat, j * CH + c - 1)
                    sums = m2[:, c % 2].rearrange("p h a c -> p (h a c)")
                    dve.wait_ge(s_sq, j * CH + c + 1)
                    v.tensor_reduce(sums[:, H:2 * H], (angle if c % 2 == 0 else whole)[:].rearrange("p a h -> p h a"),
                                    AX_X, ALU.add).then_inc(s_red, 1)
                dve.wait_ge(s_stat, (j + 1) * CH)
                st = psum[:, 4 + u, 0:2 * CH]
                mean = mv[:, 0, u, :, 0]
                step_w = j * 2
                ts(mean, st[:, 0:CH], 1.0 / L, None, ALU.mult)
                ts(mv[:, 0, u, :, 1], st[:, CH:2 * CH], 1.0 / L, EPS, ALU.mult, ALU.add).then_inc(s_dvew, 1)
                dve.wait_ge(s_dvew, step_w + 1)
                tt(mean, mean, mean, ALU.mult).then_inc(s_dvew, 1)
                dve.wait_ge(s_dvew, step_w + 2)
                tt(vare[:, 0, u], mv[:, 0, u, :, 1], mean, ALU.subtract).then_inc(s_wvar, 1)
                dve.wait_ge(s_wr, j + 1)
                dve.wait_ge(s_projt, j + 1)
                for c in range(CH):
                    ins = stt(res[:, bass.ds(j * CH + c, 1)].rearrange("p o d -> p (o d)"),
                              psum[:, 2 + u, c * D:(c + 1) * D], rstd[:, 0, u, c:c + 1], binb[:], ALU.mult, ALU.add)
                ins.then_inc(s_res, 1)
            steps(dve, project, NCH)

            dve.wait_ge(s_spill, 16 * C)
            dve.wait_ge(s_last, 1)
            dve.wait_ge(s_dec, 1)

            def batches(n):
                return res[:, n * CH:(n + 1) * CH, :]

            def statistics(k, n, which, s_stats, s_out):
                for c in range(CH):
                    ins = v.bn_stats(stat6[:, which, n % 2, c], res[:, n * CH + c, :])
                ins.then_inc(s_stats, 1)
                dve.wait_ge(s_stats, k + 1)
                plain(dve, s_const)
                for c in range(CH):
                    ins = v.bn_aggr(mv[:, which, n % 2, c], stat6[:, which, n % 2, c])
                ins.then_inc(s_out, 1)

            def normalise(k, n, which, dst, s_rs, s_read, s_out):
                dve.wait_ge(s_rs, k + 1)
                wait(dve, s_read, k - 1)
                for c in range(CH):
                    ins = ts(dst[:, n % 2, c, :], res[:, n * CH + c, :], mv[:, which, n % 2, c, 0:1],
                             rstd[:, which, n % 2, c:c + 1], ALU.subtract, ALU.mult)
                ins.then_inc(s_out, 1)

            def flat(x):
                return x.rearrange("p c h -> p (c h)")

            def slot(run):
                if s0 := run(0):
                    k, n, lay = s0
                    wait(dve, s_h2, k - NCH + 1)
                    statistics(k, n, 0, s_bn1, s_mv1)
                if s4 := run(4):
                    k, n, lay = s4
                    dve.wait_ge(s_td, k + 1)
                    tt(flat(batches(n)), psum[:, 2, :], flat(batches(n)), ALU.add).then_inc(s_h2, 1)
                if s2_ := run(2):
                    k, n, lay = s2_
                    dve.wait_ge(s_tb, k + 1)
                    dve.wait_ge(s_hl, k + 1)
                    tt(flat(batches(n)), psum[:, 1, :], flat(batches(n)), ALU.add).then_inc(s_h1, 1)
                    dve.wait_ge(s_h1, k + 1)
                    statistics(k, n, 1, s_bn2, s_mv2)
                if s0:
                    k, n, lay = s0
                    normalise(k, n, 0, xn1, s_rs1, s_ta, s_xn1)
                if s1_ := run(1):
                    k, n, lay = s1_
                    dve.wait_ge(s_s, k + 1)
                    tt(uc[:], act_s[:, n % 2], cos_t[:, bass.ds(lay, 1), :].broadcast_to([P, CH, H]),
                       ALU.mult).then_inc(s_uc, 1)
                    dve.wait_ge(s_uc, k + 1)
                    wait(dve, s_tb, k - 1)
                    decay_l = dec[:, bass.ds(lay, 1)].rearrange("p o c h -> p (o c h)")
                    v.tensor_tensor_scan(flat(scan_c[:, n % 2]), decay_l, flat(uc[:]), 0.0, ALU.mult,
                                         ALU.add).then_inc(s_sc, 1)
                if s2_:
                    k, n, lay = s2_
                    normalise(k, n, 1, xn2, s_rs2, s_tc, s_xn2)
                if s1_:
                    k, n, lay = s1_
                    dve.wait_ge(s_us, k + 1)
                    wait(dve, s_m, k - 1)
                    v.tensor_tensor_scan(flat(scan_s[:, n % 2]), decay_l, flat(us[:, n % 2]), 0.0, ALU.mult,
                                         ALU.add).then_inc(s_ss, 1)
                    dve.wait_ge(s_ss, k + 1)
                    tt(scan_s[:, n % 2], scan_s[:, n % 2], sin_s[:, bass.ds(lay, 1), :].broadcast_to([P, CH, H]),
                       ALU.mult).then_inc(s_m2t, 1)
            tower_slots(dve, slot)

            dve.wait_ge(s_h2, NL * NCH)

            def front_stats(c, u):
                v.bn_stats(bsf[:, u], res[:, bass.ds(c, 1), :].rearrange("p o d -> p (o d)")).then_inc(f_bn, 1)
                dve.wait_ge(f_bn, c + 1)
                plain(dve, s_const)
                v.bn_aggr(mvf[:, u], bsf[:, u]).then_inc(f_mv, 1)

            def front_norm(c, u):
                dve.wait_ge(f_rs, c + 1)
                wait(dve, f_tp, c - 1)
                ts(xnf[:, u], res[:, bass.ds(c, 1), :].rearrange("p o d -> p (o d)"), mvf[:, u, 0:1],
                   rsf[:, u, 1:2], ALU.subtract, ALU.mult).then_inc(f_xn, 1)

            def front_x(c, u):
                dve.wait_ge(f_wo, c + 1)
                dve.wait_ge(f_kb, c + 1)
                wait(dve, f_xh, c - 1)
                wait(dve, o_pa, c - 1)
                tt(xf[:, u].rearrange("p a h -> p (a h)").rearrange("p (b n) -> p b n", b=2), psum[:, 0:2, :],
                   kb[:, u].rearrange("p a h -> p (a h)").rearrange("p (b n) -> p b n", b=2),
                   ALU.add).then_inc(f_x, 1)

            def front_xl(c, u):
                dve.wait_ge(f_xh, c + 1)
                wait(dve, o_fin, c - 1)
                tt(xl[:, u], xf[:, u], xh[:, u].bitcast(F32), ALU.subtract).then_inc(f_xl, 1)

            front_stats(0, 0)
            front_norm(0, 0)
            front_x(0, 0)
            front_xl(0, 0)

            def last(c, u):
                more = not (isinstance(c, int) and c == C - 1)
                if more:
                    front_stats(c + 1, 1 - u)
                dve.wait_ge(o_h1, c + 1)
                for b in range(2):
                    ins = v.bn_stats(bst[:, u, b], h1[:, u, b * 512:(b + 1) * 512])
                ins.then_inc(o_bn, 1)
                dve.wait_ge(o_bn, c + 1)
                plain(dve, s_const)
                v.bn_aggr(mvo[:, u], bst[:, u].rearrange("p b s -> p (b s)")).then_inc(o_mv, 1)
                if more:
                    front_norm(c + 1, 1 - u)
                dve.wait_ge(o_pa, c + 1)
                rt = c * 8
                v.tensor_copy(lg[:, u], psum[:, 4, ER:AR]).then_inc(o_rt, 1)
                dve.wait_ge(o_rt, rt + 1)
                plain(dve, s_const)
                v.max(top[:, u], lg[:, u]).then_inc(o_rt, 1)
                dve.wait_ge(o_rt, rt + 2)
                tt(gate[:, u, 2:3], top[:, u, 1:2], top[:, u, 0:1], ALU.subtract).then_inc(o_gd, 1)
                v.max_index(topi[:, u], top[:, u], lg[:, u]).then_inc(o_rt, 1)
                dve.wait_ge(o_rt, rt + 3)
                v.tensor_copy(gate[:, u, 0:2], topi[:, u, 0:2]).then_inc(o_rt, 1)
                dve.wait_ge(o_e, c + 1)
                ts(gate[:, u, 4:5], gate[:, u, 3:4], 1.0 / SCALING, 1.0 / SCALING, ALU.mult, ALU.add).then_inc(o_rt, 1)
                dve.wait_ge(o_rt, rt + 5)
                v.reciprocal(gate[:, u, 5:6], gate[:, u, 4:5]).then_inc(o_rt, 1)
                dve.wait_ge(o_rt, rt + 6)
                tt(gate[:, u, 6:7], gate[:, u, 3:4], gate[:, u, 5:6], ALU.mult)
                ts(wsel[:, u, 0], iota8[:], gate[:, u, 0:1], gate[:, u, 5:6], ALU.is_equal, ALU.mult).then_inc(o_rt, 1)
                dve.wait_ge(o_rt, rt + 7)
                ts(wsel[:, u, 1], iota8[:], gate[:, u, 1:2], gate[:, u, 6:7], ALU.is_equal, ALU.mult).then_inc(o_rt, 1)
                dve.wait_ge(o_rt, rt + 8)
                tt(wsel[:, u, 0], wsel[:, u, 0], wsel[:, u, 1], ALU.add).then_inc(o_wt, 1)
                dve.wait_ge(o_wt, c + 1)
                tt(gated[:, u].rearrange("p (e r) -> p e r", e=E), psum[:, 4, 0:ER].rearrange("p (e r) -> p e r", e=E),
                   wsel[:, u, 0].unsqueeze(2).broadcast_to([P, E, RK]), ALU.mult).then_inc(o_g, 1)
                dve.wait_ge(o_gh, c + 1)
                wait(dve, o_fin, c - 1)
                tt(gl[:, u], psum[:, 7, 0:H], gh[:, u].bitcast(F32), ALU.subtract).then_inc(o_gl, 1)
                if more:
                    front_x(c + 1, 1 - u)
                    front_xl(c + 1, 1 - u)
                dve.wait_ge(o_fin, c + 1)
                dve.wait_ge(o_hb, c + 1)
                stt(h1[:, u].rearrange("p (b n) -> p b n", b=2), psum[:, 5:7, :], rso[:, u, 1:2],
                    h1[:, u].rearrange("p (b n) -> p b n", b=2), ALU.mult, ALU.add).then_inc(o_out, 1)
            steps(dve, last, C)

        @block.tensor
        def _(pe):
            mm = nc.tensor.matmul

            pe.wait_ge(s_win, 16)
            pe.wait_ge(s_const, 1)
            for k in range(A):
                ins = mm(psum[:, 7, 0:D], over_l[:], win_early[:, k, :], start=(k == 0), stop=(k == A - 1))
            ins.then_inc(s_wmean, 1)
            pe.wait_ge(p_early, 48)
            for k in range(A):
                mm(psum[:, 6, 0:AR], over_l[:], ar_early[:, k, :], start=(k == 0), stop=(k == A - 1))
                for b in range(2):
                    ins = mm(psum[:, 4 + b, :], over_l[:], w_early[:, k, b * 512:(b + 1) * 512], start=(k == 0),
                             stop=(k == A - 1))
            ins.then_inc(p_mean, 1)

            pe.wait_ge(s_tab, 2)
            pe.wait_ge(s_ident, 1)
            for k in range(NL):
                ins = nc.tensor.transpose(psum[:, 0, k * D:(k + 1) * D], vand[:, 0, NL + k, :], ident[:])
            ins.then_inc(s_lastp, 1)
            pe.wait_ge(s_last, 1)

            def group(q, u):
                pe.wait_ge(s_vand, q + 1)
                for p in range(NP):
                    pe.wait_ge(s_m1, q * NP + p + 1)
                    pe.wait_ge(s_m2, q * NP + p + 1)
                    wait(pe, s_ke, (q - 1) * NP + p + 1)
                    for h in range(PAIR):
                        o = psum[:, p, h * A * C:(h + 1) * A * C]
                        w = vand[:, u, p * PAIR + h, :]
                        mm(o, w, m1[:, p % 2, h].rearrange("p a c -> p (a c)"), start=True, stop=False)
                        ins = mm(o, w, m2[:, p % 2, h].rearrange("p a c -> p (a c)"), start=False, stop=True)
                    ins.then_inc(s_kp, 1)
            steps(pe, group, NG)

            pe.wait_ge(s_winc, 2)
            pe.wait_ge(s_ident, 1)
            pe.wait_ge(s_ke, H // PAIR)

            def project(j, u):
                wait(pe, s_projb, j - 1)
                for k in range(A):
                    ins = mm(psum[:, u, :], winc[:, k, :], kt[:, bass.ds(j * CH, CH), k, :],
                             start=(k == 0), stop=(k == A - 1))
                ins.then_inc(s_proj, 1)
                wait(pe, s_res, j - 1)
                for c in range(CH):
                    sums = m2[:, c % 2].rearrange("p h a c -> p (h a c)")
                    pe.wait_ge(s_red, j * CH + c + 1)
                    pe.wait_ge(s_sum, j * CH + c + 1)
                    mm(psum[:, 4 + u, c:c + 1], sums[:, 0:H], ones[:], start=True, stop=True)
                    mm(psum[:, 4 + u, CH + c:CH + c + 1], sums[:, H:2 * H], ones[:], start=True,
                       stop=True).then_inc(s_stat, 1)
                pe.wait_ge(s_projb, j + 1)
                for c in range(CH):
                    y = m1[:, u].rearrange("p h a c -> p (h a c)")[:, c * H:(c + 1) * H]
                    ins = nc.tensor.transpose(psum[:, 2 + u, c * D:(c + 1) * D], y, ident[:])
                ins.then_inc(s_projt, 1)
            steps(pe, project, NCH)

            pe.wait_ge(s_res, NCH)
            pe.wait_ge(s_last, 1)

            def transposes(bank, src):
                for c in range(CH):
                    ins = nc.tensor.transpose(psum[:, bank, c * P:(c + 1) * P], src[:, c, :], ident[:])
                return ins

            def slot(run):
                if s4 := run(4):
                    k, n, lay = s4
                    pe.wait_ge(s_y, k + 1)
                    wait(pe, s_h2, k)
                    transposes(2, yb[:, n % 2]).then_inc(s_td, 1)
                if s2_ := run(2):
                    k, n, lay = s2_
                    pe.wait_ge(s_m, k + 1)
                    wait(pe, s_h1, k)
                    transposes(1, scan_c[:, n % 2]).then_inc(s_tb, 1)
                if s3 := run(3):
                    k, n, lay = s3
                    pe.wait_ge(s_z, k + 1)
                    if n == 0:
                        pe.wait_ge(s_wl, (lay + 1) * 32)
                    for f in range(FC):
                        wait(pe, s_hid, (k - 1) * FC + f + 1)
                        mm(psum[:, 3 + f, :], w1c[:, f * P:(f + 1) * P], zb[:, n % 2], start=True,
                           stop=True).then_inc(s_w1, 1)
                if s0 := run(0):
                    k, n, lay = s0
                    pe.wait_ge(s_xn1, k + 1)
                    wait(pe, s_s, k)
                    wait(pe, s_z, k - 2)
                    transposes(0, xn1[:, n % 2]).then_inc(s_ta, 1)
                if s3:
                    k, n, lay = s3
                    wait(pe, s_y, k)
                    for f in range(FC):
                        pe.wait_ge(s_hid, k * FC + f + 1)
                        ins = mm(psum[:, 7, :], w2c[:, f, :], hid[:, n % 2, f, :], start=(f == 0), stop=(f == FC - 1))
                    ins.then_inc(s_w2, 1)
                if s2_:
                    k, n, lay = s2_
                    pe.wait_ge(s_xn2, k + 1)
                    pe.wait_ge(s_s, min(k + 3, NL * NCH) if isinstance(k, int) else k + 3)
                    transposes(0, xn2[:, n % 2]).then_inc(s_tc, 1)
            tower_slots(pe, slot)

            def front_transpose(c, u):
                pe.wait_ge(f_xn, c + 1)
                wait(pe, o_gl, c - 1)
                nc.tensor.transpose(psum[:, 7, 0:H], xnf[:, u], ident[:]).then_inc(f_tp, 1)

            def front_wout(c, u):
                pe.wait_ge(f_z, c + 1)
                wait(pe, f_x, c)
                for k in range(A):
                    ins = mm(psum[:, k // 4, (k % 4) * H:(k % 4 + 1) * H], wo[:, k * P:(k + 1) * P], zf[:, u],
                             start=True, stop=True)
                ins.then_inc(f_wo, 1)

            pe.wait_ge(p_rest, 32)
            pe.wait_ge(p_arcen, 1)
            pe.wait_ge(p_lo, 1 + A)
            front_transpose(0, 0)
            front_wout(0, 0)

            def base(u, chunks):
                for k in chunks:
                    for b in range(2):
                        cols_b = slice(b * 512, (b + 1) * 512)
                        mm(psum[:, 5 + b, :], xh[:, u, k, :], wbh[:, k, cols_b], start=(k == 0), stop=False)
                        mm(psum[:, 5 + b, :], xh[:, u, k, :], wbl[:, k, cols_b], start=False, stop=False)
                        mm(psum[:, 5 + b, :], xl[:, u, k, :], wbh[:, k, cols_b], start=False, stop=False)

            def last(c, u):
                more = not (isinstance(c, int) and c == C - 1)
                pe.wait_ge(f_x, c + 1)
                wait(pe, o_h1, c)
                for k in range(A):
                    ins = nc.tensor.transpose(psum[:, 2 + k // 4, (k % 4) * P:(k % 4 + 1) * P], xf[:, u, k, :],
                                              ident[:])
                ins.then_inc(o_px, 1)
                wait(pe, o_g, c)
                for k in range(A):
                    ins = mm(psum[:, 4, 0:AR], xf[:, u, k, :], arc[:, k, :], start=(k == 0), stop=(k == A - 1))
                ins.then_inc(o_pa, 1)
                if more:
                    front_transpose(c + 1, 1 - u)
                wait(pe, o_out, c)
                pe.wait_ge(f_xl, c + 1)
                base(u, range(0, A // 2))
                pe.wait_ge(o_g, c + 1)
                pe.wait_ge(f_z, c + 2 if more else c + 1)
                nc.tensor.transpose(psum[:, 7, 0:ER], gated[:, u], ident[:]).then_inc(o_gt, 1)
                if more:
                    front_wout(c + 1, 1 - u)
                base(u, range(A // 2, A))
                pe.wait_ge(o_gl, c + 1)
                for b in range(2):
                    cols_b = slice(b * 512, (b + 1) * 512)
                    mm(psum[:, 5 + b, :], gh[:, u], lbh[:, cols_b], start=False, stop=False)
                    mm(psum[:, 5 + b, :], gh[:, u], lbl[:, cols_b], start=False, stop=False)
                    ins = mm(psum[:, 5 + b, :], gl[:, u], lbh[:, cols_b], start=False, stop=True)
                ins.then_inc(o_fin, 1)
            steps(pe, last, C)


def kernel(x, L0_tok_log_dt, L0_tok_B, L0_tok_inv_A_real, L0_tok_A_imag, L0_attn_Win, L0_attn_bin, L0_attn_ln1_w,
           L0_attn_ln1_b, L0_attn_phz_re, L0_attn_phz_im, L0_attn_lc_re, L0_attn_lc_im, L0_attn_sc_lin,
           L0_attn_ln2_w, L0_attn_ln2_b, L0_attn_W1, L0_attn_b1, L0_attn_W2, L0_attn_b2, L0_attn_lnl_w,
           L0_attn_lnl_b, L0_attn_Wout, L0_attn_bout, L0_ffn_W_base, L0_ffn_b_base, L0_ffn_W_router, L0_ffn_A,
           L0_ffn_B):
    import numpy as np
    import concourse.bacc as bacc
    from concourse.bass_utils import run_bass_kernel_spmd

    def whole(a):
        return np.ascontiguousarray(a)

    x = np.asarray(x)
    x_re, x_im = (x[..., i].transpose(2, 1, 0) for i in range(2))

    def twice(a):
        return np.concatenate([np.asarray(a).T] * 2, axis=0)

    B = np.asarray(L0_tok_B)
    params = np.stack([twice(L0_tok_A_imag), twice(B[..., 0]), twice(B[..., 1]), twice(L0_tok_inv_A_real),
                       np.broadcast_to(np.asarray(L0_tok_log_dt)[None, :], (P, H))], axis=1)
    sign = np.repeat(np.array([1.0, -1.0], np.float32), P // 2)[:, None]
    quarter = np.repeat(np.array([0.25, 0.0], np.float32), P // 2)[:, None]
    vec_cols = [np.asarray(a).T for a in (L0_attn_ln1_w, L0_attn_ln1_b, L0_attn_ln2_w, L0_attn_ln2_b, L0_attn_b2)]
    vec_cols += [np.asarray(L0_attn_b1).reshape(NL * FC, P).T]
    vec_cols += [np.asarray(a).reshape(-1, P).T for a in (L0_attn_lnl_w, L0_attn_lnl_b, L0_attn_bout)]
    vec_cols += [np.asarray(a).T for a in (L0_attn_phz_re, L0_attn_phz_im, L0_attn_lc_re, L0_attn_lc_im,
                                           L0_attn_sc_lin)]
    router = np.asarray(L0_ffn_W_router)
    lora_a = np.asarray(L0_ffn_A).reshape(ER, L)

    def width_on_partitions(w):
        return np.asarray(w).T.reshape(A, P, -1).transpose(1, 0, 2)

    arrays = {
        "x1": np.concatenate([x_re, x_im], axis=0),
        "x2": np.concatenate([x_im, x_re], axis=0),
        "params": params,
        "vecs_in": np.concatenate(vec_cols + [sign, quarter], axis=1),
        "bin_in": np.broadcast_to(np.asarray(L0_attn_bin)[None, :], (P, D)),
        "win_t": width_on_partitions(L0_attn_Win),
        "w1_t": np.asarray(L0_attn_W1).transpose(0, 2, 1),
        "w2_t": np.asarray(L0_attn_W2).transpose(0, 2, 1).reshape(NL, FC, P, D).transpose(0, 2, 1, 3),
        "wout_t": np.asarray(L0_attn_Wout).T,
        "wbase_t": width_on_partitions(L0_ffn_W_base),
        "bbase_in": np.broadcast_to(np.asarray(L0_ffn_b_base)[None, :], (P, L)),
        "ar_t": width_on_partitions(np.concatenate([lora_a, router], axis=0)),
        "lora_b": np.asarray(L0_ffn_B).transpose(0, 2, 1).reshape(ER, L),
    }
    nc = bacc.Bacc("TRN2", target_bir_lowering=False, num_devices=1)
    args = {}
    for name, a in arrays.items():
        arrays[name] = a = whole(a)
        args[name] = nc.dram_tensor(name, a.shape, mybir.dt.from_np(a.dtype), kind="ExternalInput").ap()
    args["k_spill"] = nc.dram_tensor("k_spill", (C, P, A, H), F32, kind="Internal").ap()
    args["out"] = nc.dram_tensor("out", (C * H, L), F32, kind="ExternalOutput").ap()
    build_program(nc, **args)
    r = run_bass_kernel_spmd(nc, [arrays], core_ids=[0])
    return r.results[0]["out"].reshape(C, H, L)
```

```python
from contextlib import ExitStack

import concourse.bass as bass
from concourse import mybir

F32 = mybir.dt.float32
F32R = mybir.dt.float32r
U32 = mybir.dt.uint32
I32 = mybir.dt.int32
ALU = mybir.AluOpType
ACT = mybir.ActivationFunctionType
AX_X = mybir.AxisListType.X

P = 128
C, L = 32, 1024
H = 128
D = 128
NL = 4
FC = 4
A = L // P
GH = 8
NG = H // GH
PAIR = 2
NP = GH // PAIR
CH = 4
NCH = C // CH
T = CH * H
E, RK = 8, 16
ER = E * RK
AR = ER + E
PER = A // NL
NCHP = NCH // PER
EPS = 1e-5
SCALING = 32 / RK
ROUND = 1.5 * 2.0 ** 23
TWO_PI = 6.283185
TWO_PI_HI = 6.28125
TWO_PI_LO = 0.0019353071795864769
LN2 = 0.6931471805599453
LN2_HI = 0.693359375
LN2_LO = -2.1219444005469057e-4
EXP_TERMS = [1 / 5040, 1 / 720, 1 / 120, 1 / 24, 1 / 6, 1 / 2, 1.0]
NPOW = 7

LN1W, LN1B, LN2W, LN2B, B2, B1, LNLW, LNLB, BOUT, ZRE, ZIM, CRE, CIM, SCL, SIGN, QUARTER, NVEC = (
    0, 4, 8, 12, 16, 20, 36, 37, 38, 46, 50, 54, 58, 62, 66, 67, 68)
A_IM, B_RE, B_IM, INV_A, LOG_DT, NPAR = 0, 1, 2, 3, 4, 5


def wait(eng, semaphore, value):
    if isinstance(value, int) and value <= 0:
        return
    eng.wait_ge(semaphore, value)


def plain(eng, ready):
    eng.nop(nofuse=True)


def steps(eng, body, n, unroll=2, tail=2):
    for k in range(unroll):
        body(k, k % unroll)
    with eng.Fori(unroll, n - tail, unroll) as i:
        for k in range(unroll):
            body(i + k, k)
    for k in range(n - tail, n):
        body(k, k % unroll)


def tower_slots(eng, slot, ahead=None):
    def at(lay, t, lo, hi):
        def run(offset):
            if not lo <= t - offset < hi:
                return None
            return lay * NCH + (t - offset), (t - offset) % NCH, lay + (t - offset) // NCH
        slot(run)
    for t in range(NCH):
        at(0, t, 0, NCH)
    with eng.Fori(1, NL) as lay:
        for t in range(NCH):
            at(lay, t, -NCH, NCH)
    for t in range(NCH, NCH + 5):
        if t == NCH + 4 and ahead:
            ahead()
        at(NL - 1, t, -NCH, NCH)


def build_program(nc, x1, x2, params, vecs_in, bin_in, win_t, w1_t, w2_t, wout_t, wbase_t, bbase_in,
                  ar_t, lora_b, k_spill, out):
    with ExitStack() as ctx:
        def sem(name):
            return ctx.enter_context(nc.semaphore(name))

        def held(stack, name, shape, dt=F32):
            return stack.enter_context(nc.sbuf_tensor(name, shape, dt))

        res = held(ctx, "res", [P, C, D])
        ident = held(ctx, "ident", [P, P])
        over_l = held(ctx, "over_l", [P, P])
        cos_t = held(ctx, "cos_t", [P, NL, H])
        sin_t = held(ctx, "sin_t", [P, NL, H])
        cos_s = held(ctx, "cos_s", [P, NL, H])
        sin_s = held(ctx, "sin_s", [P, NL, H])
        last_t = held(ctx, "last_t", [P, NL, D])
        vecs = held(ctx, "vecs", [P, NVEC])
        cols = held(ctx, "cols", [P, 20, NL])
        stat6 = held(ctx, "stat6", [P, 2, 2, CH, 6])
        mv = held(ctx, "mv", [P, 2, 2, CH, 2])
        vare = held(ctx, "vare", [P, 2, 2, CH])
        rstd = held(ctx, "rstd", [P, 2, 2, CH])
        powers = held(ctx, "powers", [P, 3, NL])
        iota8 = held(ctx, "iota8", [P, E])
        warm = held(ctx, "warm", [P, 1])
        ones = held(ctx, "ones", [P, 1])
        wmean = held(ctx, "wmean", [P, L])
        armean = held(ctx, "armean", [P, AR])

        psum = ctx.enter_context(nc.psum_tensor("psum", [P, 8, 512], F32))

        front = ExitStack()
        kt = held(front, "kt", [P, C, A, H])
        s1 = held(front, "s1", [P, H, A])
        s2 = held(front, "s2", [P, H, A])
        decay_pow = held(front, "decay_pow", [P, NPOW, H])
        turns = held(front, "turns", [P, H])
        iota_b = held(front, "iota_b", [P, H])
        x1b = held(front, "x1b", [P, 2, GH, C])
        x2b = held(front, "x2b", [P, 2, GH, C])
        angle = held(front, "angle", [P, GH, P])
        whole = held(front, "whole", [P, GH, P])
        decay = held(front, "decay", [P, 2, GH, P // 2])
        vand = held(front, "vand", [P, 2, GH, P])
        m1 = held(front, "m1", [P, 2, PAIR, A, C])
        m2 = held(front, "m2", [P, 2, PAIR, A, C])
        binb = held(front, "binb", [P, D])
        front.close()

        wbh = held(ctx, "wbh", [P, A, L], F32R)
        wbl = held(ctx, "wbl", [P, A, L], F32R)
        arc = held(ctx, "arc", [P, A, AR])
        lbh = held(ctx, "lbh", [P, L], F32R)
        lbl = held(ctx, "lbl", [P, L], F32R)
        wo = held(ctx, "wo", [P, L])
        bbase = held(ctx, "bbase", [P, L])
        wraw = held(ctx, "wraw", [P, 2, L])
        xnf = held(ctx, "xnf", [P, 2, D])
        zf = held(ctx, "zf", [P, 2, H])
        kb = held(ctx, "kb", [P, 2, A, H])
        bsf = held(ctx, "bsf", [P, 2, 6])
        mvf = held(ctx, "mvf", [P, 2, 2])
        rsf = held(ctx, "rsf", [P, 2, 2])
        tower = ExitStack()
        xn1 = held(tower, "xn1", [P, 2, CH, D])
        xn2 = held(tower, "xn2", [P, 2, CH, D])
        act_s = held(tower, "act_s", [P, 2, CH, H])
        uc = held(tower, "uc", [P, CH, H])
        us = held(tower, "us", [P, 2, CH, H])
        scan_c = held(tower, "scan_c", [P, 2, CH, H])
        scan_s = held(tower, "scan_s", [P, 2, CH, H])
        zb = held(tower, "zb", [P, 2, T])
        hid = held(tower, "hid", [P, 2, FC, T])
        yb = held(tower, "yb", [P, 2, CH, H])
        w1c = held(tower, "w1c", [P, FC * P])
        w2c = held(tower, "w2c", [P, FC, D])
        dec = held(tower, "dec", [P, NL, CH, H])
        tower.close()
        xf = held(ctx, "xf", [P, 2, A, H])
        xh = held(ctx, "xh", [P, 2, A, H], F32R)
        xl = held(ctx, "xl", [P, 2, A, H], F32R)
        h1 = held(ctx, "h1", [P, 2, L])
        lg = held(ctx, "lg", [P, 2, E])
        top = held(ctx, "top", [P, 2, 8])
        topi = held(ctx, "topi", [P, 2, 8], U32)
        gate = held(ctx, "gate", [P, 2, 10])
        wsel = held(ctx, "wsel", [P, 2, 2, E])
        gated = held(ctx, "gated", [P, 2, ER])
        gh = held(ctx, "gh", [P, 2, H], F32R)
        gl = held(ctx, "gl", [P, 2, H], F32R)
        bst = held(ctx, "bst", [P, 2, 2, 6])
        mvo = held(ctx, "mvo", [P, 2, 2])
        rso = held(ctx, "rso", [P, 2, 2])

        s_vecs, s_par, s_win, s_bin = (sem(n) for n in ("s_vecs", "s_par", "s_win", "s_bin"))
        s_x = [sem("s_x0"), sem("s_x1")]
        s_const, s_ident = sem("s_const"), sem("s_ident")
        s_dve, s_pool = sem("s_dve"), sem("s_pool")
        s_setd, s_seta = sem("s_setd"), sem("s_seta")
        s_turned, s_whole, s_angle, s_sin = sem("s_turned"), sem("s_whole"), sem("s_angle"), sem("s_sin")
        s_decay, s_decayed, s_vand = sem("s_decay"), sem("s_decayed"), sem("s_vand")
        s_m1, s_m2, s_kp, s_ke = sem("s_m1"), sem("s_m2"), sem("s_kp"), sem("s_ke")
        s_wmean, s_winc = sem("s_wmean"), sem("s_winc")
        s_sq, s_red, s_stat, s_wvar, s_wr = sem("s_sq"), sem("s_red"), sem("s_stat"), sem("s_wvar"), sem("s_wr")
        s_proj, s_projb, s_projt, s_res = sem("s_proj"), sem("s_projb"), sem("s_projt"), sem("s_res")
        s_dvew, s_half, s_sum = sem("s_dvew"), sem("s_half"), sem("s_sum")
        s_spill = sem("s_spill")
        (s_bn1, s_mv1, s_ve1, s_rs1, s_xn1, s_ta, s_s, s_us, s_uc, s_sc, s_ss, s_m1t, s_m2t, s_m, s_hl, s_tb,
         s_h1, s_bn2, s_mv2, s_ve2, s_rs2, s_xn2, s_tc, s_z, s_w1, s_hid, s_w2, s_y, s_td, s_h2, s_wl1, s_wl2) = (
            sem(n) for n in (
                "bn1", "mv1", "ve1", "rs1", "xn1_ready", "ta", "s_ready", "us", "uc", "sc", "ss", "m1t", "m2t",
                "m_ready", "hl", "tb", "h1_done", "bn2", "mv2", "ve2", "rs2", "xn2_ready", "tc", "z_ready", "w1_done",
                "hid_ready", "w2_done", "y_ready", "td", "h2_done", "wl1", "wl2"))
        (f_bn, f_mv, f_ve, f_rs, f_xn, f_tp, f_z, f_wo, f_kb, f_x, f_xh, f_xl) = (
            sem("f_" + n) for n in ("bn", "mv", "ve", "rs", "xn", "tp", "z", "wo", "kb", "x", "xh", "xl"))
        (o_px, o_pa, o_h1, o_bn, o_mv, o_ve, o_rs, o_hb, o_rt, o_gd, o_e, o_g, o_gt, o_gh, o_gl, o_fin, o_out,
         o_st) = (sem("o_" + n) for n in ("px", "pa", "h1", "bn", "mv", "ve", "rs", "hb", "rt", "gd", "e", "g",
                                          "gt", "gh", "gl", "fin", "out", "st"))
        o_wt = sem("o_wt")
        p_raw, f_k = ([sem(n + "0"), sem(n + "1")] for n in ("p_raw", "f_k"))
        p_early, p_mean, p_means, p_cen, p_hi, p_lo, p_arc, p_arcen, p_rest = (
            sem("p_" + n) for n in ("early", "mean", "means", "cen", "hi", "lo", "arc", "arcen", "rest"))
        s_tanh, s_tab, s_lastp, s_last, s_dec = (sem(n) for n in ("s_tanh", "s_tab", "s_lastp", "s_last", "s_dec"))


        block = ctx.enter_context(nc.Block())
        par = kt[:, 0:NPAR, 0, :]

        def big(i):
            return kt[:, 8 + i].rearrange("p a h -> p (a h)").rearrange("p (h a) -> p h a", a=A)

        def col(i):
            return kt[:, 16 + i // 8, i % 8, :]

        lam, psi, em1, sh, sn, t0, t1, t2, gr, gi, kk, fr = (col(i) for i in range(12))
        ex, en, er, eq, es = (kt[:, 18 + i, 0:2, :] for i in range(5))
        a_, dt_ = ex[:, 0], ex[:, 1]
        ea, va, vb, ca, sa = (big(i) for i in range(5))
        wr_, wi_ = big(5), big(6)

        w_early = kt[:, 24:32].rearrange("p c a h -> p c (a h)")
        ar_early = kt[:, 6:8].rearrange("p c a h -> p (c a h)")[:, 0:A * AR].rearrange("p (a n) -> p a n", a=A)

        win_early = res[:, 0:A, :]
        winc = s2[:].rearrange("p h a -> p (h a)").rearrange("p (a d) -> p a d", a=A)

        @block.sync
        def _(sp):
            sp.dma_start(par, params).then_inc(s_par, 16)
            sp.dma_start(vecs[:], vecs_in).then_inc(s_vecs, 16)
            sp.dma_start(win_early, win_t).then_inc(s_win, 16)
            sp.dma_start(binb[:], bin_in).then_inc(s_bin, 16)
            sp.dma_start(ar_early, ar_t).then_inc(p_early, 16)
            for k in range(0, A, 4):
                sp.dma_start(w_early[:, k:k + 4], wbase_t[:, k:k + 4, :]).then_inc(p_early, 16)

            def load_x(q, u):
                wait(sp, s_kp, (q - 1) * NP)
                sp.dma_start(x1b[:, u], x1[:, bass.ds(q * GH, GH), :]).then_inc(s_x[u], 16)
                sp.dma_start(x2b[:, u], x2[:, bass.ds(q * GH, GH), :]).then_inc(s_x[u], 16)
            steps(sp, load_x, NG)

            sp.wait_ge(s_ke, H // PAIR)
            with sp.Fori(0, C) as c:
                sp.dma_start(k_spill[bass.ds(c, 1)].rearrange("o p a h -> p (o a) h"),
                             kt[:, bass.ds(c, 1)].rearrange("p o a h -> p (o a) h")).then_inc(s_spill, 16)
            sp.wait_ge(s_spill, 16 * C)

            sp.wait_ge(s_res, NCH)

            def load_layer(lay):
                wait(sp, s_w1, lay * NCH * FC)
                sp.dma_start(w1c[:], w1_t[bass.ds(lay, 1)].rearrange("o d f -> (o d) f")).then_inc(s_wl1, 16)
                wait(sp, s_w2, lay * NCH)
                sp.dma_start(w2c[:], w2_t[bass.ds(lay, 1)].rearrange("o f c d -> (o f) c d")).then_inc(s_wl2, 16)

            def load_base(lay):
                for j in range(PER):
                    i = lay * PER + j
                    wait(sp, p_lo, i)
                    sp.dma_start(wraw[:, j, :], wbase_t[:, bass.ds(i, 1), :].rearrange("p o n -> p (o n)")).then_inc(p_raw[j], 16)
            sp.dma_start(wraw[:, 1, :], lora_b).then_inc(p_raw[1], 16)
            sp.dma_start(arc[:], ar_t).then_inc(p_arc, 16)
            load_layer(0)
            load_base(0)
            sp.dma_start(bbase[:], bbase_in).then_inc(p_rest, 16)
            sp.dma_start(wo[:], wout_t).then_inc(p_rest, 16)
            with sp.Fori(1, NL) as lay:
                load_base(lay)
                load_layer(lay)

            def load_k(c, u):
                wait(sp, f_x, c - 1)
                sp.dma_start(kb[:, u], k_spill[bass.ds(c, 1)].rearrange("o p a h -> (o p) a h")).then_inc(f_k[u], 16)

            load_k(0, 0)
            sp.wait_ge(s_h2, NL * NCH)

            def store(c, u):
                if not (isinstance(c, int) and c == C - 1):
                    load_k(c + 1, 1 - u)
                sp.wait_ge(o_out, c + 1)
                sp.dma_start(out[bass.ds(c * H, H), :], h1[:, u, :]).then_inc(o_st, 16)
            steps(sp, store, C)
            sp.wait_ge(o_st, 16 * C)

        @block.gpsimd
        def _(pool):
            g = nc.gpsimd
            g.memset(over_l[:], 1.0 / L)
            g.memset(ones[:], 1.0)
            for i, e in enumerate((-0.5, 0.5, -1.0)):
                g.memset(powers[:, i, :], e)
            g.iota(iota_b[:], [[1, H]], base=0, channel_multiplier=0, allow_small_or_imprecise_dtypes=True)
            g.iota(iota8[:], [[1, E]], base=0, channel_multiplier=0, allow_small_or_imprecise_dtypes=True)
            g.memset(ident[:], 0.0).then_inc(s_const, 1)
            pool.wait_ge(s_const, 1)
            g.affine_select(out=ident[:], in_=ident[:], compare_op=ALU.not_equal, fill=1.0, base=0,
                            pattern=[[-1, P]], channel_multiplier=1).then_inc(s_ident, 1)

            done = [0]

            def step(ins):
                done[0] += 1
                ins.then_inc(s_pool, 1)
                pool.wait_ge(s_pool, done[0])

            def v(i):
                return vecs[:, i:i + NL]

            (r2, zero, rad, inv, cr, ci, mag, c1, c2, c3, pc, ps, pr, lgr, lgi) = (cols[:, i] for i in range(15))
            pool.wait_ge(s_vecs, 16)
            tt = g.tensor_tensor
            step(tt(r2, v(ZRE), v(ZRE), ALU.mult))
            step(tt(c1, v(ZIM), v(ZIM), ALU.mult))
            step(tt(r2, r2, c1, ALU.add))
            step(g.tensor_scalar(zero, r2, 0.0, None, ALU.is_equal))
            step(tt(rad, r2, powers[:, 1], ALU.pow))
            step(tt(c1, rad, zero, ALU.add))
            step(tt(inv, c1, powers[:, 2], ALU.pow))
            step(tt(c1, v(ZRE), zero, ALU.add))
            step(tt(cr, c1, inv, ALU.mult))
            tt(ci, v(ZIM), inv, ALU.mult).then_inc(s_tab, 1)
            pool.wait_ge(s_tab, 1)
            pool.wait_ge(s_tanh, 1)
            rp = vand[:, 0, 0:NL, :]
            b1_, b2_, b3_, b4_ = vand[:, 0, NL:GH, :], vand[:, 1, 0:NL, :], vand[:, 1, NL:GH, :], decay[:, 0].rearrange("p g h -> p (g h)").rearrange("p (l h) -> p l h", l=NL)
            g.memset(cos_t[:, :, 0:1], 1.0)
            g.memset(rp[:, :, 0:1], 1.0)
            step(g.memset(sin_t[:, :, 0:1], 0.0))
            step(g.tensor_copy(pc, cr))
            step(g.tensor_copy(ps, ci))
            step(g.tensor_copy(pr, mag))
            for k in range(NPOW):
                n = 1 << k

                def wide(x):
                    return x.unsqueeze(2).broadcast_to([P, NL, n])
                tt(b1_[:, :, 0:n], cos_t[:, :, 0:n], wide(pc), ALU.mult)
                tt(b2_[:, :, 0:n], sin_t[:, :, 0:n], wide(ps), ALU.mult)
                tt(b3_[:, :, 0:n], cos_t[:, :, 0:n], wide(ps), ALU.mult)
                tt(b4_[:, :, 0:n], sin_t[:, :, 0:n], wide(pc), ALU.mult)
                step(tt(rp[:, :, n:2 * n], rp[:, :, 0:n], wide(pr), ALU.mult))
                tt(cos_t[:, :, n:2 * n], b1_[:, :, 0:n], b2_[:, :, 0:n], ALU.subtract)
                step(tt(sin_t[:, :, n:2 * n], b3_[:, :, 0:n], b4_[:, :, 0:n], ALU.add))
                if k < NPOW - 1:
                    tt(c1, pc, pc, ALU.mult)
                    tt(c2, ps, ps, ALU.mult)
                    step(tt(c3, pc, ps, ALU.mult))
                    tt(pc, c1, c2, ALU.subtract)
                    tt(ps, c3, c3, ALU.add)
                    step(tt(pr, pr, pr, ALU.mult))
            tt(c1, mag, cr, ALU.mult)
            step(tt(c2, mag, ci, ALU.mult))
            step(tt(lgr, v(CRE), c1, ALU.mult))
            step(tt(c3, v(CIM), c2, ALU.mult))
            step(tt(lgr, lgr, c3, ALU.subtract))
            step(tt(lgi, v(CRE), c2, ALU.mult))
            step(tt(c3, v(CIM), c1, ALU.mult))
            step(tt(lgi, lgi, c3, ALU.add))

            def row(x):
                return x.unsqueeze(2).broadcast_to([P, NL, H])
            tt(b1_, cos_t[:], row(lgr), ALU.mult)
            step(tt(b2_, sin_t[:], row(lgi), ALU.mult))
            step(tt(b1_, b1_, b2_, ALU.subtract))
            step(tt(b1_, b1_, rp, ALU.mult))
            tt(b1_, b1_, row(v(SCL)), ALU.mult)
            tt(cos_s[:], cos_t[:], row(v(SCL)), ALU.mult)
            tt(sin_s[:], sin_t[:], row(v(SCL)), ALU.mult).then_inc(s_tab, 1)
            pool.wait_ge(s_tab, 2)
            g.memset(decay[:, :, :, 0:1], 1.0).then_inc(s_const, 1)
            pool.wait_ge(s_const, 2)

            def make_decay(q, u, powers_of_two):
                wait(pool, s_vand, q - 1)
                for k in powers_of_two:
                    n = 1 << k
                    if k:
                        pool.wait_ge(s_decay, q * (NPOW - 1) + k)
                    plain(pool, s_const)
                    g.tensor_tensor(decay[:, u, :, n:2 * n], decay[:, u, :, 0:n],
                                    decay_pow[:, k, bass.ds(q * GH, GH)].unsqueeze(2).broadcast_to([P, GH, n]),
                                    ALU.mult).then_inc(s_decay, 1)

            def make_m1(q, u, p):
                pool.wait_ge(s_x[u], (q - u) * 16 + 32)
                wait(pool, s_kp, q * NP + p - 1)
                plain(pool, s_const)
                g.tensor_tensor(
                    m1[:, p % 2],
                    x1b[:, u, PAIR * p:PAIR * (p + 1), :].unsqueeze(2).broadcast_to([P, PAIR, A, C]),
                    s1[:, bass.ds(q * GH + PAIR * p, PAIR), :].unsqueeze(3).broadcast_to([P, PAIR, A, C]),
                    ALU.mult).then_inc(s_m1, 1)

            pool.wait_ge(s_setd, 3)
            make_decay(0, 0, range(NPOW - 1))
            pool.wait_ge(s_setd, 4)
            make_m1(0, 0, 0)
            make_decay(1, 1, range(NPOW - 1))

            def group(q, u):
                more = not (isinstance(q, int) and q >= NG - 2)
                make_m1(q, u, 1)
                if more:
                    make_decay(q + 2, u, (0, 1))
                make_m1(q, u, 2)
                if more:
                    make_decay(q + 2, u, (2, 3))
                make_m1(q, u, 3)
                if more:
                    make_decay(q + 2, u, (4,))
                if more or q == NG - 2:
                    make_m1(q + 1, 1 - u, 0)
                if more:
                    make_decay(q + 2, u, (5,))
            steps(pool, group, NG, tail=4)

            pool.wait_ge(s_ke, H // PAIR)
            half = vand[:, 0, 0:NL, :]
            quarter = vand[:, 1, 0:2, :]

            def width_sum(j, c):
                kc = kt[:, bass.ds(j * CH + c, 1)].rearrange("p o a h -> p (o a) h")
                i = (j * (CH - 1) + c) * 2
                plain(pool, s_const)
                tt(half, kc[:, 0:A // 2, :], kc[:, A // 2:A, :], ALU.add).then_inc(s_half, 1)
                pool.wait_ge(s_half, i + 1)
                tt(quarter, half[:, 0:2], half[:, 2:4], ALU.add).then_inc(s_half, 1)
                pool.wait_ge(s_half, i + 2)
                wait(pool, s_stat, j * CH + c - 1)
                tt(m2[:, c % 2, 0].rearrange("p a c -> p (a c)")[:, 0:H], quarter[:, 0], quarter[:, 1],
                   ALU.add).then_inc(s_sum, 1)

            def win_rstd(j, u):
                pool.wait_ge(s_wvar, j + 1)
                g.tensor_tensor(rstd[:, 0, u], vare[:, 0, u], powers[:, 0, 0:CH], ALU.pow).then_inc(s_wr, 1)

            def project(j, u):
                width_sum(j, 2)
                if not (isinstance(j, int) and j == 0):
                    win_rstd(j - 1, 1 - u)
                if not (isinstance(j, int) and j == NCH - 1):
                    width_sum(j + 1, 0)
                    width_sum(j + 1, 1)
            width_sum(0, 0)
            width_sum(0, 1)
            steps(pool, project, NCH)
            win_rstd(NCH - 1, (NCH - 1) % 2)

            pool.wait_ge(s_res, NCH)
            pool.wait_ge(s_spill, 16 * C)
            pool.wait_ge(s_last, 1)

            def rstd_of(count, which, u, s_in, s_eps, s_out):
                pool.wait_ge(s_in, count + 1)
                plain(pool, s_const)
                g.tensor_scalar(vare[:, which, u], mv[:, which, u, :, 1], EPS, None, ALU.add).then_inc(s_eps, 1)
                pool.wait_ge(s_eps, count + 1)
                tt(rstd[:, which, u], vare[:, which, u], powers[:, 0, 0:CH], ALU.pow).then_inc(s_out, 1)

            def slot(run):
                s0, s1_, s2_ = run(0), run(1), run(2)
                if s1_:
                    k, n, lay = s1_
                    pool.wait_ge(s_xn1, k + 1)
                    plain(pool, s_const)
                    r = res[:, n * CH:(n + 1) * CH, :]
                    tt(r, r, last_t[:, bass.ds(lay, 1), :].broadcast_to([P, CH, D]), ALU.add).then_inc(s_hl, 1)
                    pool.wait_ge(s_s, k + 1)
                    wait(pool, s_ss, k - 1)
                    plain(pool, s_const)
                    tt(us[:, n % 2], act_s[:, n % 2], sin_t[:, bass.ds(lay, 1), :].broadcast_to([P, CH, H]),
                       ALU.mult).then_inc(s_us, 1)
                if s0:
                    k, n, lay = s0
                    rstd_of(k, 0, n % 2, s_mv1, s_ve1, s_rs1)
                    if isinstance(k, int) and k == 0:
                        pool.wait_ge(p_hi, 1)
                        tt(lbl[:], wraw[:, 1], lbh[:].bitcast(F32), ALU.subtract).then_inc(p_lo, 1)
                        pool.wait_ge(p_arc, 16)
                        tt(arc[:], arc[:], armean[:].unsqueeze(1).broadcast_to([P, A, AR]),
                           ALU.subtract).then_inc(p_arcen, 1)
                    if n % NCHP == 1:
                        centre(lay * PER + n // NCHP, n // NCHP, lay)
                    elif n % NCHP == 3:
                        rest(lay * PER + n // NCHP, n // NCHP)
                if s1_:
                    k, n, lay = s1_
                    sc = scan_c[:, n % 2]
                    pool.wait_ge(s_sc, k + 1)
                    plain(pool, s_const)
                    tt(sc, sc, cos_s[:, bass.ds(lay, 1), :].broadcast_to([P, CH, H]), ALU.mult).then_inc(s_m1t, 1)
                if s2_:
                    k, n, lay = s2_
                    rstd_of(k, 1, n % 2, s_mv2, s_ve2, s_rs2)
                if s1_:
                    k, n, lay = s1_
                    pool.wait_ge(s_m1t, k + 1)
                    pool.wait_ge(s_m2t, k + 1)
                    tt(sc, sc, scan_s[:, n % 2], ALU.add).then_inc(s_m, 1)

            def centre(i, j, lay):
                pool.wait_ge(p_raw[j], 16 * (lay + 1 + j))
                plain(pool, s_const)
                tt(wraw[:, j], wraw[:, j], wmean[:], ALU.subtract).then_inc(p_cen, 1)

            def rest(i, j):
                pool.wait_ge(p_hi, i + 2)
                plain(pool, s_const)
                tt(wbl[:, bass.ds(i, 1)].rearrange("p o n -> p (o n)"), wraw[:, j],
                   wbh[:, bass.ds(i, 1)].bitcast(F32).rearrange("p o n -> p (o n)"), ALU.subtract).then_inc(p_lo, 1)

            pool.wait_ge(p_means, 1)
            tower_slots(pool, slot)

            def front_rstd(c, u):
                pool.wait_ge(f_mv, c + 1)
                plain(pool, s_const)
                g.tensor_scalar(rsf[:, u, 0:1], mvf[:, u, 1:2], EPS, None, ALU.add).then_inc(f_ve, 1)
                pool.wait_ge(f_ve, c + 1)
                tt(rsf[:, u, 1:2], rsf[:, u, 0:1], powers[:, 0, 0:1], ALU.pow).then_inc(f_rs, 1)

            def front_bias(c, u):
                pool.wait_ge(f_k[u], (c - u) * 8 + 16)
                tt(kb[:, u], kb[:, u], vecs[:, BOUT:BOUT + A].unsqueeze(2).broadcast_to([P, A, H]),
                   ALU.add).then_inc(f_kb, 1)

            pool.wait_ge(p_rest, 32)
            front_bias(0, 0)
            front_rstd(0, 0)
            front_rstd(1, 1)
            pool.wait_ge(s_h2, NL * NCH)

            def last(c, u):
                more = not (isinstance(c, int) and c == C - 1)
                pool.wait_ge(o_mv, c + 1)
                plain(pool, s_const)
                g.tensor_scalar(rso[:, u, 0:1], mvo[:, u, 1:2], EPS, None, ALU.add).then_inc(o_ve, 1)
                pool.wait_ge(o_ve, c + 1)
                tt(rso[:, u, 1:2], rso[:, u, 0:1], powers[:, 0, 0:1], ALU.pow).then_inc(o_rs, 1)
                if not (isinstance(c, int) and c >= C - 2):
                    front_rstd(c + 2, u)
                if more:
                    front_bias(c + 1, 1 - u)
                tt(h1[:, u], h1[:, u], bbase[:], ALU.add).then_inc(o_hb, 1)
            steps(pool, last, C)

        @block.scalar
        def _(act):
            a = nc.scalar.activation
            act.wait_ge(s_tab, 1)
            a(cols[:, 6], cols[:, 2], ACT.Tanh).then_inc(s_tanh, 1)
            act.wait_ge(s_setd, 1)
            a(sh, turns[:], ACT.Sin, scale=TWO_PI / 2)
            a(sn, turns[:], ACT.Sin, scale=TWO_PI).then_inc(s_seta, 1)
            act.wait_ge(s_setd, 2)
            a(ca, va, ACT.Sin, scale=TWO_PI)
            a(sa, vb, ACT.Sin, scale=TWO_PI).then_inc(s_seta, 1)

            def turn(q, heads):
                wait(act, s_sin, q)
                for k in heads:
                    plain(act, s_ident)
                    ins = a(angle[:, k, :], iota_b[:], ACT.Identity, bias=vecs[:, QUARTER:QUARTER + 1],
                            scale=turns[:, bass.ds(q * GH + k, 1)])
                return ins

            def sines(q):
                act.wait_ge(s_angle, q + 1)
                a(whole[:], angle[:], ACT.Sin, scale=TWO_PI).then_inc(s_sin, 1)

            def evacuate(q, p):
                act.wait_ge(s_kp, q * NP + p + 1)
                plain(act, s_ident)
                a(kt[:, :, :, bass.ds(q * GH + p * PAIR, PAIR)].rearrange("p c a h -> p h a c"),
                  psum[:, p, :].rearrange("p (h a c) -> p h a c", h=PAIR, a=A), ACT.Copy).then_inc(s_ke, 1)
            act.wait_ge(p_mean, 1)
            nc.scalar.copy(armean[:], psum[:, 6, 0:AR])
            nc.scalar.copy(wmean[:].rearrange("p (b n) -> p b n", b=2), psum[:, 4:6, :]).then_inc(p_means, 1)
            act.wait_ge(s_lastp, 1)
            a(last_t[:].rearrange("p l d -> p (l d)"), psum[:, 0, :], ACT.Copy).then_inc(s_last, 1)
            act.wait_ge(s_const, 1)
            turn(0, range(GH)).then_inc(s_turned, 1)
            sines(0)
            turn(1, range(GH)).then_inc(s_turned, 1)
            act.wait_ge(s_setd, 4)

            def group(q, u):
                more = not (isinstance(q, int) and q >= NG - 2)
                evacuate(q, 0)
                if more or q == NG - 2:
                    sines(q + 1)
                if more:
                    turn(q + 2, range(GH)).then_inc(s_turned, 1)
                for p in range(1, NP):
                    evacuate(q, p)
            steps(act, group, NG, tail=4)

            act.wait_ge(s_m2, H // PAIR)
            act.wait_ge(s_winc, 1)
            nc.scalar.copy(winc, win_early).then_inc(s_winc, 1)
            act.wait_ge(s_ke, H // PAIR)

            def square(j, c):
                wait(act, s_red, j * CH + c - 1)
                plain(act, s_ident)
                a((angle if c % 2 == 0 else whole)[:], kt[:, bass.ds(j * CH + c, 1)].rearrange("p o a h -> p (o a) h"),
                  ACT.Square).then_inc(s_sq, 1)

            def project(j, u):
                square(j, 2)
                square(j, 3)
                if not (isinstance(j, int) and j == NCH - 1):
                    square(j + 1, 0)
                    square(j + 1, 1)
                act.wait_ge(s_proj, j + 1)
                wait(act, s_projt, j - 1)
                a(m1[:, u].rearrange("p h a c -> p (h a c)"), psum[:, u, :], ACT.Copy).then_inc(s_projb, 1)
            square(0, 0)
            square(0, 1)
            steps(act, project, NCH)

            a(warm[:], ones[:], ACT.Silu)
            act.wait_ge(s_spill, 16 * C)
            act.wait_ge(s_res, NCH)

            def vec(i):
                return vecs[:, bass.ds(i, 1)]

            def silu(k, n, lay, f):
                act.wait_ge(s_w1, k * FC + f + 1)
                plain(act, s_ident)
                a(hid[:, n % 2, f, :], psum[:, 3 + f, :], ACT.Silu, bias=vec(lay * FC + B1 + f)).then_inc(s_hid, 1)

            def leading(i, j):
                act.wait_ge(p_cen, i + 1)
                plain(act, s_ident)
                nc.scalar.copy(wbh[:, bass.ds(i, 1)].rearrange("p o n -> p (o n)"), wraw[:, j]).then_inc(p_hi, 1)

            def slot(run):
                s0, s3, s4 = run(0), run(3), run(4)
                if s4:
                    k, n, lay = s4
                    wait(act, s_w2, k - 1)
                    silu(k, n, lay, 0)
                    silu(k, n, lay, 1)
                if s3:
                    k, n, lay = s3
                    act.wait_ge(s_tc, k + 1)
                    wait(act, s_w1, (k - 1) * FC)
                    plain(act, s_ident)
                    a(zb[:, n % 2], psum[:, 0, :], ACT.Identity, bias=vec(lay + LN2B),
                      scale=vec(lay + LN2W)).then_inc(s_z, 1)
                if s4:
                    k, n, lay = s4
                    silu(k, n, lay, 2)
                    silu(k, n, lay, 3)
                if s0:
                    k, n, lay = s0
                    act.wait_ge(s_ta, k + 1)
                    wait(act, s_us, k - 1)
                    wait(act, s_uc, k - 1)
                    plain(act, s_ident)
                    a(act_s[:, n % 2].rearrange("p c h -> p (c h)"), psum[:, 0, :], ACT.Silu, bias=vec(lay + LN1B),
                      scale=vec(lay + LN1W)).then_inc(s_s, 1)
                if s4:
                    k, n, lay = s4
                    act.wait_ge(s_w2, k + 1)
                    wait(act, s_td, k - 1)
                    plain(act, s_ident)
                    a(yb[:, n % 2].rearrange("p c h -> p (c h)"), psum[:, 7, :], ACT.Identity,
                      bias=vec(lay + B2)).then_inc(s_y, 1)
                if s0 and s0[1] % NCHP == 2:
                    k, n, lay = s0
                    leading(lay * PER + n // NCHP, n // NCHP)
            act.wait_ge(p_raw[1], 16)
            nc.scalar.copy(lbh[:], wraw[:, 1]).then_inc(p_hi, 1)
            tower_slots(act, slot)

            def front_z(c, u):
                act.wait_ge(f_tp, c + 1)
                wait(act, f_wo, c - 1)
                a(zf[:, u], psum[:, 7, 0:H], ACT.Identity, bias=vecs[:, LNLB:LNLB + 1],
                  scale=vecs[:, LNLW:LNLW + 1]).then_inc(f_z, 1)

            def front_xh(c, u):
                act.wait_ge(f_x, c + 1)
                wait(act, o_fin, c - 1)
                nc.scalar.copy(xh[:, u], xf[:, u]).then_inc(f_xh, 1)

            front_z(0, 0)
            act.wait_ge(s_h2, NL * NCH)
            front_xh(0, 0)

            def last(c, u):
                more = not (isinstance(c, int) and c == C - 1)
                act.wait_ge(o_px, c + 1)
                wait(act, o_st, 16 * (c - 1))
                nc.scalar.copy(h1[:, u].rearrange("p (b n) -> p b n", b=2), psum[:, 2:4, :]).then_inc(o_h1, 1)
                if more:
                    front_z(c + 1, 1 - u)
                act.wait_ge(o_gd, c + 1)
                act.wait_ge(o_rs, c + 1)
                a(gate[:, u, 3:4], gate[:, u, 2:3], ACT.Exp, scale=rso[:, u, 1:2]).then_inc(o_e, 1)
                act.wait_ge(o_gt, c + 1)
                wait(act, o_fin, c - 1)
                nc.scalar.copy(gh[:, u], psum[:, 7, 0:H]).then_inc(o_gh, 1)
                if more:
                    front_xh(c + 1, 1 - u)
            steps(act, last, C)

        @block.vector
        def _(dve):
            v = nc.vector
            tt, ts, stt = v.tensor_tensor, v.tensor_scalar, v.scalar_tensor_tensor
            done = [0]

            def step(ins):
                done[0] += 1
                ins.then_inc(s_dve, 1)
                dve.wait_ge(s_dve, done[0])

            def exp_parts(x, rows):
                n, r, q, sc = (t[:, 0:rows] for t in (en, er, eq, es))
                step(ts(n, x, 1.0 / LN2, ROUND, ALU.mult, ALU.add))
                step(ts(n, n, -ROUND, None, ALU.add))
                step(stt(r, n, -LN2_HI, x, ALU.mult, ALU.add))
                ts(sc.bitcast(I32), n, 127.0, 2.0 ** 23, ALU.add, ALU.mult)
                step(stt(r, n, -LN2_LO, r, ALU.mult, ALU.add))
                step(ts(q, r, EXP_TERMS[0], None, ALU.mult))
                for term in EXP_TERMS[1:]:
                    step(stt(q, q, term, r, ALU.add, ALU.mult))

            dve.wait_ge(s_par, 16)
            step(ts(ex, par[:, INV_A:INV_A + 2], -87.0, 88.0, ALU.max, ALU.min))
            exp_parts(ex, 2)
            step(stt(ex, eq, 1.0, es, ALU.add, ALU.mult))
            step(stt(lam, a_, -1.0, dt_, ALU.mult, ALU.mult))
            step(tt(psi, par[:, A_IM], dt_, ALU.mult))
            step(ts(kk, psi, 1.0 / (TWO_PI_HI + TWO_PI_LO), None, ALU.mult))
            step(ts(kk, kk, ROUND, -ROUND, ALU.add, ALU.add))
            step(stt(t0, kk, -TWO_PI_HI, psi, ALU.mult, ALU.add))
            step(stt(t0, kk, -TWO_PI_LO, t0, ALU.mult, ALU.add))
            step(ts(t0, t0, 1.0 / (TWO_PI_HI + TWO_PI_LO), None, ALU.mult))
            step(ts(t1, t0, ROUND, -ROUND, ALU.add, ALU.add))
            tt(turns[:], t0, t1, ALU.subtract).then_inc(s_setd, 1)
            dve.wait_ge(s_setd, 1)
            step(ts(fr, turns[:], float(P), None, ALU.mult))
            step(ts(t0, fr, ROUND, -ROUND, ALU.add, ALU.add))
            step(tt(fr, fr, t0, ALU.subtract))
            for k in range(A):
                ts(va[:, :, k], fr, float(k), 0.25, ALU.mult, ALU.add)
                ins = ts(vb[:, :, k], fr, float(k), None, ALU.mult)
            step(ins)
            step(ts(ca, va, ROUND, -ROUND, ALU.add, ALU.add))
            step(ts(sa, vb, ROUND, -ROUND, ALU.add, ALU.add))
            tt(va, va, ca, ALU.subtract)
            tt(vb, vb, sa, ALU.subtract).then_inc(s_setd, 1)
            step(ts(t1, lam, -87.0, None, ALU.max))
            exp_parts(t1.unsqueeze(1), 1)
            step(ts(t0, es[:, 0], -1.0, None, ALU.add))
            step(tt(t1, eq[:, 0], es[:, 0], ALU.mult))
            step(tt(em1, t0, t1, ALU.add))
            step(v.tensor_copy(t0, em1))
            for k in range(NPOW):
                ts(decay_pow[:, k], t0, 1.0, None, ALU.add)
                step(stt(t0, t0, 2.0, t0, ALU.add, ALU.mult))
            ts(ea[:, :, 0], t0, 0.0, 1.0, ALU.mult, ALU.add)
            ts(ea[:, :, 1], t0, 1.0, None, ALU.add).then_inc(s_setd, 1)
            dve.wait_ge(s_setd, 3)
            for k in range(2, A):
                step(tt(ea[:, :, k], ea[:, :, k - 1], ea[:, :, 1], ALU.mult))
            dve.wait_ge(s_seta, 1)
            step(tt(sh, sh, sh, ALU.mult))
            step(ts(sh, sh, 2.0, None, ALU.mult))
            step(ts(t0, sh, -1.0, 1.0, ALU.mult, ALU.add))
            step(tt(t0, em1, t0, ALU.mult))
            step(tt(t0, t0, sh, ALU.subtract))
            step(stt(t1, em1, 1.0, sn, ALU.add, ALU.mult))
            step(tt(gr, par[:, B_RE], t0, ALU.mult))
            step(tt(t2, par[:, B_IM], t1, ALU.mult))
            step(tt(gr, gr, t2, ALU.subtract))
            step(tt(gi, par[:, B_RE], t1, ALU.mult))
            step(tt(t2, par[:, B_IM], t0, ALU.mult))
            step(tt(gi, gi, t2, ALU.add))
            step(tt(t0, a_, a_, ALU.mult))
            step(tt(t1, par[:, A_IM], par[:, A_IM], ALU.mult))
            step(tt(t0, t0, t1, ALU.add))
            step(v.reciprocal(t0, t0))
            step(stt(t1, a_, -2.0, t0, ALU.mult, ALU.mult))
            step(stt(t2, par[:, A_IM], -2.0, t0, ALU.mult, ALU.mult))
            step(tt(kk, gr, t1, ALU.mult))
            step(tt(fr, gi, t2, ALU.mult))
            step(tt(kk, kk, fr, ALU.subtract))
            step(tt(fr, gr, t2, ALU.mult))
            step(tt(gi, gi, t1, ALU.mult))
            step(tt(gi, gi, fr, ALU.add))

            def along(x):
                return x.unsqueeze(2).broadcast_to([P, H, A])
            dve.wait_ge(s_seta, 2)
            step(tt(va, ca, along(kk), ALU.mult))
            step(tt(vb, sa, along(gi), ALU.mult))
            step(tt(wr_, va, vb, ALU.subtract))
            step(tt(va, sa, along(kk), ALU.mult))
            step(tt(vb, ca, along(gi), ALU.mult))
            step(tt(wi_, va, vb, ALU.add))
            dve.wait_ge(s_vecs, 16)
            stt(s1[:], wr_, vecs[:, SIGN:SIGN + 1], ea, ALU.mult, ALU.mult)
            stt(s2[:], wi_, -1.0, ea, ALU.mult, ALU.mult).then_inc(s_setd, 1)
            dve.wait_ge(s_const, 1)
            dve.wait_ge(s_win, 16)
            dve.wait_ge(s_wmean, 1)
            tt(win_early, win_early, psum[:, 7, 0:D].unsqueeze(1).broadcast_to([P, A, D]),
               ALU.subtract).then_inc(s_winc, 1)

            def whole_turns(q):
                dve.wait_ge(s_turned, q + 1)
                ts(whole[:], angle[:], ROUND, -ROUND, ALU.add, ALU.add).then_inc(s_whole, 1)

            def reduce_angles(q):
                dve.wait_ge(s_whole, q + 1)
                tt(angle[:], angle[:], whole[:], ALU.subtract).then_inc(s_angle, 1)

            def last_doubling(q, u):
                n = P // 2
                dve.wait_ge(s_decay, (q + 1) * (NPOW - 1))
                wait(dve, s_kp, (q - 1) * NP)
                tt(vand[:, u, :, n:2 * n], decay[:, u],
                   decay_pow[:, NPOW - 1, bass.ds(q * GH, GH)].unsqueeze(2).broadcast_to([P, GH, n]),
                   ALU.mult).then_inc(s_decayed, 1)

            def make_vand(q, u):
                dve.wait_ge(s_sin, q + 1)
                dve.wait_ge(s_decayed, q + 1)
                n = P // 2
                tt(vand[:, u, :, 0:n], decay[:, u], whole[:, :, 0:n], ALU.mult)
                tt(vand[:, u, :, n:2 * n], vand[:, u, :, n:2 * n], whole[:, :, n:2 * n], ALU.mult).then_inc(s_vand, 1)

            def make_m2(q, u, p):
                dve.wait_ge(s_x[u], (q - u) * 16 + 32)
                wait(dve, s_kp, q * NP + p - 1)
                tt(m2[:, p % 2],
                   x2b[:, u, PAIR * p:PAIR * (p + 1), :].unsqueeze(2).broadcast_to([P, PAIR, A, C]),
                   s2[:, bass.ds(q * GH + PAIR * p, PAIR), :].unsqueeze(3).broadcast_to([P, PAIR, A, C]),
                   ALU.mult).then_inc(s_m2, 1)

            dve.wait_ge(s_setd, 4)
            whole_turns(0)
            reduce_angles(0)
            make_m2(0, 0, 0)
            dve.wait_ge(s_last, 1)
            last_doubling(0, 0)
            make_vand(0, 0)

            def group(q, u):
                more = not (isinstance(q, int) and q == NG - 1)
                make_m2(q, u, 1)
                if more:
                    dve.wait_ge(s_vand, q + 1)
                    whole_turns(q + 1)
                make_m2(q, u, 2)
                if more:
                    reduce_angles(q + 1)
                make_m2(q, u, 3)
                if more:
                    last_doubling(q + 1, 1 - u)
                    make_vand(q + 1, 1 - u)
                    make_m2(q + 1, 1 - u, 0)
            steps(dve, group, NG)

            dve.wait_ge(s_bin, 16)
            dve.wait_ge(s_winc, 2)

            dve.wait_ge(s_ke, H // PAIR)
            def width_sums(j, c):
                wait(dve, s_stat, j * CH + c - 1)
                sums = m2[:, c % 2].rearrange("p h a c -> p (h a c)")
                if c == CH - 1:
                    v.tensor_reduce(sums[:, 0:H], kt[:, bass.ds(j * CH + c, 1)].rearrange("p o a h -> p h (o a)"),
                                    AX_X, ALU.add)
                dve.wait_ge(s_sq, j * CH + c + 1)
                v.tensor_reduce(sums[:, H:2 * H], (angle if c % 2 == 0 else whole)[:].rearrange("p a h -> p h a"),
                                AX_X, ALU.add).then_inc(s_red, 1)

            def variances(j, u):
                dve.wait_ge(s_stat, (j + 1) * CH)
                st = psum[:, 4 + u, 0:2 * CH]
                mean = mv[:, 0, u, :, 0]
                step_w = j * 2
                ts(mean, st[:, 0:CH], 1.0 / L, None, ALU.mult)
                ts(mv[:, 0, u, :, 1], st[:, CH:2 * CH], 1.0 / L, EPS, ALU.mult, ALU.add).then_inc(s_dvew, 1)
                dve.wait_ge(s_dvew, step_w + 1)
                tt(mean, mean, mean, ALU.mult).then_inc(s_dvew, 1)
                dve.wait_ge(s_dvew, step_w + 2)
                tt(vare[:, 0, u], mv[:, 0, u, :, 1], mean, ALU.subtract).then_inc(s_wvar, 1)

            def residual(j, u):
                dve.wait_ge(s_wr, j + 1)
                dve.wait_ge(s_projt, j + 1)
                for c in range(CH):
                    ins = stt(res[:, bass.ds(j * CH + c, 1)].rearrange("p o d -> p (o d)"),
                              psum[:, 2 + u, c * D:(c + 1) * D], rstd[:, 0, u, c:c + 1], binb[:], ALU.mult, ALU.add)
                ins.then_inc(s_res, 1)

            def project(j, u):
                first = isinstance(j, int) and j == 0
                more = not (isinstance(j, int) and j == NCH - 1)
                if not first:
                    variances(j - 1, 1 - u)
                width_sums(j, 2)
                width_sums(j, 3)
                if not first:
                    residual(j - 1, 1 - u)
                if more:
                    width_sums(j + 1, 0)
                    width_sums(j + 1, 1)
            width_sums(0, 0)
            width_sums(0, 1)
            steps(dve, project, NCH)
            variances(NCH - 1, (NCH - 1) % 2)
            residual(NCH - 1, (NCH - 1) % 2)

            dve.wait_ge(s_spill, 16 * C)
            dve.wait_ge(s_last, 1)
            for k in range(NL):
                ins = ts(dec[:, k], over_l[:].unsqueeze(1).broadcast_to([P, CH, H]), 0.0, cols[:, 6, k:k + 1],
                         ALU.mult, ALU.add)
            ins.then_inc(s_dec, 1)
            dve.wait_ge(s_dec, 1)
            v.memset(dec[:, :, :, 0:1], 0.0).then_inc(s_dec, 1)
            dve.wait_ge(s_dec, 2)

            def batches(n):
                return res[:, n * CH:(n + 1) * CH, :]

            def statistics(k, n, which, s_stats, s_out):
                for c in range(CH):
                    ins = v.bn_stats(stat6[:, which, n % 2, c], res[:, n * CH + c, :])
                ins.then_inc(s_stats, 1)
                dve.wait_ge(s_stats, k + 1)
                plain(dve, s_const)
                for c in range(CH):
                    ins = v.bn_aggr(mv[:, which, n % 2, c], stat6[:, which, n % 2, c])
                ins.then_inc(s_out, 1)

            def normalise(k, n, which, dst, s_rs, s_read, s_out):
                dve.wait_ge(s_rs, k + 1)
                wait(dve, s_read, k - 1)
                for c in range(CH):
                    ins = ts(dst[:, n % 2, c, :], res[:, n * CH + c, :], mv[:, which, n % 2, c, 0:1],
                             rstd[:, which, n % 2, c:c + 1], ALU.subtract, ALU.mult)
                ins.then_inc(s_out, 1)

            def flat(x):
                return x.rearrange("p c h -> p (c h)")

            def slot(run):
                s0, s1_, s2_, s3, s5 = (run(i) for i in (0, 1, 2, 3, 5))
                if s3:
                    k, n, lay = s3
                    normalise(k, n, 1, xn2, s_rs2, s_tc, s_xn2)
                if s0:
                    k, n, lay = s0
                    wait(dve, s_h2, k - NCH + 1)
                    statistics(k, n, 0, s_bn1, s_mv1)
                if s1_:
                    k, n, lay = s1_
                    dve.wait_ge(s_s, k + 1)
                    tt(uc[:], act_s[:, n % 2], cos_t[:, bass.ds(lay, 1), :].broadcast_to([P, CH, H]),
                       ALU.mult).then_inc(s_uc, 1)
                    dve.wait_ge(s_uc, k + 1)
                    wait(dve, s_tb, k - 1)
                    decay_l = dec[:, bass.ds(lay, 1)].rearrange("p o c h -> p (o c h)")
                    v.tensor_tensor_scan(flat(scan_c[:, n % 2]), decay_l, flat(uc[:]), 0.0, ALU.mult,
                                         ALU.add).then_inc(s_sc, 1)
                if s5:
                    k, n, lay = s5
                    dve.wait_ge(s_td, k + 1)
                    tt(flat(batches(n)), psum[:, 2, :], flat(batches(n)), ALU.add).then_inc(s_h2, 1)
                if s2_:
                    k, n, lay = s2_
                    dve.wait_ge(s_tb, k + 1)
                    dve.wait_ge(s_hl, k + 1)
                    tt(flat(batches(n)), psum[:, 1, :], flat(batches(n)), ALU.add).then_inc(s_h1, 1)
                    dve.wait_ge(s_h1, k + 1)
                    statistics(k, n, 1, s_bn2, s_mv2)
                if s0:
                    k, n, lay = s0
                    normalise(k, n, 0, xn1, s_rs1, s_ta, s_xn1)
                if s1_:
                    k, n, lay = s1_
                    dve.wait_ge(s_us, k + 1)
                    wait(dve, s_m, k - 1)
                    v.tensor_tensor_scan(flat(scan_s[:, n % 2]), decay_l, flat(us[:, n % 2]), 0.0, ALU.mult,
                                         ALU.add).then_inc(s_ss, 1)
                    dve.wait_ge(s_ss, k + 1)
                    tt(scan_s[:, n % 2], scan_s[:, n % 2], sin_s[:, bass.ds(lay, 1), :].broadcast_to([P, CH, H]),
                       ALU.mult).then_inc(s_m2t, 1)
            def front_stats(c, u):
                v.bn_stats(bsf[:, u], res[:, bass.ds(c, 1), :].rearrange("p o d -> p (o d)")).then_inc(f_bn, 1)
                dve.wait_ge(f_bn, c + 1)
                plain(dve, s_const)
                v.bn_aggr(mvf[:, u], bsf[:, u]).then_inc(f_mv, 1)

            def front_norm(c, u):
                dve.wait_ge(f_rs, c + 1)
                wait(dve, f_tp, c - 1)
                ts(xnf[:, u], res[:, bass.ds(c, 1), :].rearrange("p o d -> p (o d)"), mvf[:, u, 0:1],
                   rsf[:, u, 1:2], ALU.subtract, ALU.mult).then_inc(f_xn, 1)

            def ahead():
                front_stats(0, 0)
                front_stats(1, 1)
                front_norm(0, 0)
            tower_slots(dve, slot, ahead)

            dve.wait_ge(s_h2, NL * NCH)

            def front_x(c, u):
                dve.wait_ge(f_wo, c + 1)
                dve.wait_ge(f_kb, c + 1)
                wait(dve, f_xh, c - 1)
                wait(dve, o_pa, c - 1)
                tt(xf[:, u].rearrange("p a h -> p (a h)").rearrange("p (b n) -> p b n", b=2), psum[:, 0:2, :],
                   kb[:, u].rearrange("p a h -> p (a h)").rearrange("p (b n) -> p b n", b=2),
                   ALU.add).then_inc(f_x, 1)

            def front_xl(c, u):
                dve.wait_ge(f_xh, c + 1)
                wait(dve, o_fin, c - 1)
                tt(xl[:, u], xf[:, u], xh[:, u].bitcast(F32), ALU.subtract).then_inc(f_xl, 1)

            front_x(0, 0)
            front_xl(0, 0)

            def last(c, u):
                more = not (isinstance(c, int) and c == C - 1)
                if more:
                    front_norm(c + 1, 1 - u)
                dve.wait_ge(o_h1, c + 1)
                for b in range(2):
                    ins = v.bn_stats(bst[:, u, b], h1[:, u, b * 512:(b + 1) * 512])
                ins.then_inc(o_bn, 1)
                dve.wait_ge(o_bn, c + 1)
                plain(dve, s_const)
                v.bn_aggr(mvo[:, u], bst[:, u].rearrange("p b s -> p (b s)")).then_inc(o_mv, 1)
                if not (isinstance(c, int) and c >= C - 2):
                    front_stats(c + 2, u)
                dve.wait_ge(o_pa, c + 1)
                rt = c * 8
                v.tensor_copy(lg[:, u], psum[:, 4, ER:AR]).then_inc(o_rt, 1)
                dve.wait_ge(o_rt, rt + 1)
                plain(dve, s_const)
                v.max(top[:, u], lg[:, u]).then_inc(o_rt, 1)
                dve.wait_ge(o_rt, rt + 2)
                tt(gate[:, u, 2:3], top[:, u, 1:2], top[:, u, 0:1], ALU.subtract).then_inc(o_gd, 1)
                v.max_index(topi[:, u], top[:, u], lg[:, u]).then_inc(o_rt, 1)
                dve.wait_ge(o_rt, rt + 3)
                v.tensor_copy(gate[:, u, 0:2], topi[:, u, 0:2]).then_inc(o_rt, 1)
                dve.wait_ge(o_e, c + 1)
                ts(gate[:, u, 4:5], gate[:, u, 3:4], 1.0 / SCALING, 1.0 / SCALING, ALU.mult, ALU.add).then_inc(o_rt, 1)
                dve.wait_ge(o_rt, rt + 5)
                v.reciprocal(gate[:, u, 5:6], gate[:, u, 4:5]).then_inc(o_rt, 1)
                dve.wait_ge(o_rt, rt + 6)
                tt(gate[:, u, 6:7], gate[:, u, 3:4], gate[:, u, 5:6], ALU.mult)
                ts(wsel[:, u, 0], iota8[:], gate[:, u, 0:1], gate[:, u, 5:6], ALU.is_equal, ALU.mult).then_inc(o_rt, 1)
                dve.wait_ge(o_rt, rt + 7)
                ts(wsel[:, u, 1], iota8[:], gate[:, u, 1:2], gate[:, u, 6:7], ALU.is_equal, ALU.mult).then_inc(o_rt, 1)
                dve.wait_ge(o_rt, rt + 8)
                tt(wsel[:, u, 0], wsel[:, u, 0], wsel[:, u, 1], ALU.add).then_inc(o_wt, 1)
                dve.wait_ge(o_wt, c + 1)
                tt(gated[:, u].rearrange("p (e r) -> p e r", e=E), psum[:, 4, 0:ER].rearrange("p (e r) -> p e r", e=E),
                   wsel[:, u, 0].unsqueeze(2).broadcast_to([P, E, RK]), ALU.mult).then_inc(o_g, 1)
                dve.wait_ge(o_gh, c + 1)
                wait(dve, o_fin, c - 1)
                tt(gl[:, u], psum[:, 7, 0:H], gh[:, u].bitcast(F32), ALU.subtract).then_inc(o_gl, 1)
                if more:
                    front_x(c + 1, 1 - u)
                    front_xl(c + 1, 1 - u)
                dve.wait_ge(o_fin, c + 1)
                dve.wait_ge(o_hb, c + 1)
                stt(h1[:, u].rearrange("p (b n) -> p b n", b=2), psum[:, 5:7, :], rso[:, u, 1:2],
                    h1[:, u].rearrange("p (b n) -> p b n", b=2), ALU.mult, ALU.add).then_inc(o_out, 1)
            steps(dve, last, C, tail=4)

        @block.tensor
        def _(pe):
            mm = nc.tensor.matmul

            pe.wait_ge(s_win, 16)
            pe.wait_ge(s_const, 1)
            for k in range(A):
                ins = mm(psum[:, 7, 0:D], over_l[:], win_early[:, k, :], start=(k == 0), stop=(k == A - 1))
            ins.then_inc(s_wmean, 1)
            pe.wait_ge(p_early, 48)
            for k in range(A):
                mm(psum[:, 6, 0:AR], over_l[:], ar_early[:, k, :], start=(k == 0), stop=(k == A - 1))
                for b in range(2):
                    ins = mm(psum[:, 4 + b, :], over_l[:], w_early[:, k, b * 512:(b + 1) * 512], start=(k == 0),
                             stop=(k == A - 1))
            ins.then_inc(p_mean, 1)

            pe.wait_ge(s_tab, 2)
            pe.wait_ge(s_ident, 1)
            for k in range(NL):
                ins = nc.tensor.transpose(psum[:, 0, k * D:(k + 1) * D], vand[:, 0, NL + k, :], ident[:])
            ins.then_inc(s_lastp, 1)
            pe.wait_ge(s_last, 1)

            def group(q, u):
                pe.wait_ge(s_vand, q + 1)
                for p in range(NP):
                    pe.wait_ge(s_m1, q * NP + p + 1)
                    pe.wait_ge(s_m2, q * NP + p + 1)
                    wait(pe, s_ke, (q - 1) * NP + p + 1)
                    for h in range(PAIR):
                        o = psum[:, p, h * A * C:(h + 1) * A * C]
                        w = vand[:, u, p * PAIR + h, :]
                        mm(o, w, m1[:, p % 2, h].rearrange("p a c -> p (a c)"), start=True, stop=False)
                        ins = mm(o, w, m2[:, p % 2, h].rearrange("p a c -> p (a c)"), start=False, stop=True)
                    ins.then_inc(s_kp, 1)
            steps(pe, group, NG)

            pe.wait_ge(s_winc, 2)
            pe.wait_ge(s_ident, 1)
            pe.wait_ge(s_ke, H // PAIR)

            def statistics(j, u, c):
                sums = m2[:, c % 2].rearrange("p h a c -> p (h a c)")
                pe.wait_ge(s_red, j * CH + c + 1)
                if c < CH - 1:
                    pe.wait_ge(s_sum, j * (CH - 1) + c + 1)
                if c == 0:
                    wait(pe, s_wvar, j - 1)
                mm(psum[:, 4 + u, c:c + 1], sums[:, 0:H], ones[:], start=True, stop=True)
                mm(psum[:, 4 + u, CH + c:CH + c + 1], sums[:, H:2 * H], ones[:], start=True,
                   stop=True).then_inc(s_stat, 1)

            def turn_back(j, u):
                pe.wait_ge(s_projb, j + 1)
                wait(pe, s_res, j - 1)
                for c in range(CH):
                    y = m1[:, u].rearrange("p h a c -> p (h a c)")[:, c * H:(c + 1) * H]
                    ins = nc.tensor.transpose(psum[:, 2 + u, c * D:(c + 1) * D], y, ident[:])
                ins.then_inc(s_projt, 1)

            def project(j, u):
                wait(pe, s_projb, j - 1)
                for k in range(A):
                    ins = mm(psum[:, u, :], winc[:, k, :], kt[:, bass.ds(j * CH, CH), k, :],
                             start=(k == 0), stop=(k == A - 1))
                    if k == A - 1:
                        ins.then_inc(s_proj, 1)
                    if k == 2 and not (isinstance(j, int) and j == 0):
                        turn_back(j - 1, 1 - u)
                    if k % 2:
                        statistics(j, u, k // 2)
            assert A == 2 * CH
            steps(pe, project, NCH)
            turn_back(NCH - 1, (NCH - 1) % 2)

            pe.wait_ge(s_res, NCH)
            pe.wait_ge(s_last, 1)

            def transposes(bank, src):
                for c in range(CH):
                    ins = nc.tensor.transpose(psum[:, bank, c * P:(c + 1) * P], src[:, c, :], ident[:])
                return ins

            def hidden(k, n, f):
                wait(pe, s_hid, (k - 1) * FC + f + 1)
                mm(psum[:, 3 + f, :], w1c[:, f * P:(f + 1) * P], zb[:, n % 2], start=True, stop=True).then_inc(s_w1, 1)

            def hidden_back(k, n, f):
                pe.wait_ge(s_hid, k * FC + f + 1)
                return mm(psum[:, 7, :], w2c[:, f, :], hid[:, n % 2, f, :], start=(f == 0), stop=(f == FC - 1))

            def slot(run):
                s0, s2_, s3, s4, s5 = (run(i) for i in (0, 2, 3, 4, 5))
                if s4:
                    k, n, lay = s4
                    pe.wait_ge(s_z, k + 1)
                    if n == 0:
                        pe.wait_ge(s_wl1, (lay + 1) * 16)
                    hidden(k, n, 0)
                    hidden(k, n, 1)
                if s3:
                    k, n, lay = s3
                    pe.wait_ge(s_xn2, k + 1)
                    pe.wait_ge(s_s, min(k + 3, NL * NCH) if isinstance(k, int) else k + 3)
                    transposes(0, xn2[:, n % 2]).then_inc(s_tc, 1)
                if s5:
                    k, n, lay = s5
                    pe.wait_ge(s_y, k + 1)
                    wait(pe, s_h2, k)
                    transposes(2, yb[:, n % 2]).then_inc(s_td, 1)
                if s2_:
                    k, n, lay = s2_
                    pe.wait_ge(s_m, k + 1)
                    wait(pe, s_h1, k)
                    transposes(1, scan_c[:, n % 2]).then_inc(s_tb, 1)
                if s4:
                    k, n, lay = s4
                    hidden(k, n, 2)
                    hidden(k, n, 3)
                    wait(pe, s_y, k)
                    if n == 0:
                        pe.wait_ge(s_wl2, (lay + 1) * 16)
                    for f in range(FC - 1):
                        hidden_back(k, n, f)
                if s0:
                    k, n, lay = s0
                    pe.wait_ge(s_xn1, k + 1)
                    wait(pe, s_s, k)
                    wait(pe, s_z, k - 2)
                    transposes(0, xn1[:, n % 2]).then_inc(s_ta, 1)
                if s4:
                    k, n, lay = s4
                    hidden_back(k, n, FC - 1).then_inc(s_w2, 1)
            tower_slots(pe, slot)

            def front_transpose(c, u):
                pe.wait_ge(f_xn, c + 1)
                wait(pe, o_gl, c - 1)
                nc.tensor.transpose(psum[:, 7, 0:H], xnf[:, u], ident[:]).then_inc(f_tp, 1)

            def front_wout(c, u):
                pe.wait_ge(f_z, c + 1)
                wait(pe, f_x, c)
                for k in range(A):
                    ins = mm(psum[:, k // 4, (k % 4) * H:(k % 4 + 1) * H], wo[:, k * P:(k + 1) * P], zf[:, u],
                             start=True, stop=True)
                ins.then_inc(f_wo, 1)

            pe.wait_ge(p_rest, 32)
            pe.wait_ge(p_arcen, 1)
            pe.wait_ge(p_lo, 1 + A)
            front_transpose(0, 0)
            front_wout(0, 0)

            def base(u, chunks):
                for k in chunks:
                    for b in range(2):
                        cols_b = slice(b * 512, (b + 1) * 512)
                        mm(psum[:, 5 + b, :], xh[:, u, k, :], wbh[:, k, cols_b], start=(k == 0), stop=False)
                        mm(psum[:, 5 + b, :], xh[:, u, k, :], wbl[:, k, cols_b], start=False, stop=False)
                        mm(psum[:, 5 + b, :], xl[:, u, k, :], wbh[:, k, cols_b], start=False, stop=False)

            def last(c, u):
                more = not (isinstance(c, int) and c == C - 1)
                pe.wait_ge(f_x, c + 1)
                wait(pe, o_h1, c)
                for k in range(A):
                    ins = nc.tensor.transpose(psum[:, 2 + k // 4, (k % 4) * P:(k % 4 + 1) * P], xf[:, u, k, :],
                                              ident[:])
                ins.then_inc(o_px, 1)
                wait(pe, o_g, c)
                for k in range(A):
                    ins = mm(psum[:, 4, 0:AR], xf[:, u, k, :], arc[:, k, :], start=(k == 0), stop=(k == A - 1))
                ins.then_inc(o_pa, 1)
                if more:
                    front_transpose(c + 1, 1 - u)
                wait(pe, o_out, c)
                pe.wait_ge(f_xl, c + 1)
                base(u, range(0, A // 2))
                pe.wait_ge(o_g, c + 1)
                pe.wait_ge(f_z, c + 2 if more else c + 1)
                nc.tensor.transpose(psum[:, 7, 0:ER], gated[:, u], ident[:]).then_inc(o_gt, 1)
                if more:
                    front_wout(c + 1, 1 - u)
                base(u, range(A // 2, A))
                pe.wait_ge(o_gl, c + 1)
                for b in range(2):
                    cols_b = slice(b * 512, (b + 1) * 512)
                    mm(psum[:, 5 + b, :], gh[:, u], lbh[:, cols_b], start=False, stop=False)
                    mm(psum[:, 5 + b, :], gh[:, u], lbl[:, cols_b], start=False, stop=False)
                    ins = mm(psum[:, 5 + b, :], gl[:, u], lbh[:, cols_b], start=False, stop=True)
                ins.then_inc(o_fin, 1)
            steps(pe, last, C)


def kernel(x, L0_tok_log_dt, L0_tok_B, L0_tok_inv_A_real, L0_tok_A_imag, L0_attn_Win, L0_attn_bin, L0_attn_ln1_w,
           L0_attn_ln1_b, L0_attn_phz_re, L0_attn_phz_im, L0_attn_lc_re, L0_attn_lc_im, L0_attn_sc_lin,
           L0_attn_ln2_w, L0_attn_ln2_b, L0_attn_W1, L0_attn_b1, L0_attn_W2, L0_attn_b2, L0_attn_lnl_w,
           L0_attn_lnl_b, L0_attn_Wout, L0_attn_bout, L0_ffn_W_base, L0_ffn_b_base, L0_ffn_W_router, L0_ffn_A,
           L0_ffn_B):
    import numpy as np
    import concourse.bacc as bacc
    from concourse.bass_utils import run_bass_kernel_spmd

    def whole(a):
        return np.ascontiguousarray(a)

    x = np.asarray(x)
    x_re, x_im = (x[..., i].transpose(2, 1, 0) for i in range(2))

    def twice(a):
        return np.concatenate([np.asarray(a).T] * 2, axis=0)

    B = np.asarray(L0_tok_B)
    params = np.stack([twice(L0_tok_A_imag), twice(B[..., 0]), twice(B[..., 1]), twice(L0_tok_inv_A_real),
                       np.broadcast_to(np.asarray(L0_tok_log_dt)[None, :], (P, H))], axis=1)
    sign = np.repeat(np.array([1.0, -1.0], np.float32), P // 2)[:, None]
    quarter = np.repeat(np.array([0.25, 0.0], np.float32), P // 2)[:, None]
    vec_cols = [np.asarray(a).T for a in (L0_attn_ln1_w, L0_attn_ln1_b, L0_attn_ln2_w, L0_attn_ln2_b, L0_attn_b2)]
    vec_cols += [np.asarray(L0_attn_b1).reshape(NL * FC, P).T]
    vec_cols += [np.asarray(a).reshape(-1, P).T for a in (L0_attn_lnl_w, L0_attn_lnl_b, L0_attn_bout)]
    vec_cols += [np.asarray(a).T for a in (L0_attn_phz_re, L0_attn_phz_im, L0_attn_lc_re, L0_attn_lc_im,
                                           L0_attn_sc_lin)]
    router = np.asarray(L0_ffn_W_router)
    lora_a = np.asarray(L0_ffn_A).reshape(ER, L)

    def width_on_partitions(w):
        return np.asarray(w).T.reshape(A, P, -1).transpose(1, 0, 2)

    arrays = {
        "x1": np.concatenate([x_re, x_im], axis=0),
        "x2": np.concatenate([x_im, x_re], axis=0),
        "params": params,
        "vecs_in": np.concatenate(vec_cols + [sign, quarter], axis=1),
        "bin_in": np.broadcast_to(np.asarray(L0_attn_bin)[None, :], (P, D)),
        "win_t": width_on_partitions(L0_attn_Win),
        "w1_t": np.asarray(L0_attn_W1).transpose(0, 2, 1),
        "w2_t": np.asarray(L0_attn_W2).transpose(0, 2, 1).reshape(NL, FC, P, D).transpose(0, 2, 1, 3),
        "wout_t": np.asarray(L0_attn_Wout).T,
        "wbase_t": width_on_partitions(L0_ffn_W_base),
        "bbase_in": np.broadcast_to(np.asarray(L0_ffn_b_base)[None, :], (P, L)),
        "ar_t": width_on_partitions(np.concatenate([lora_a, router], axis=0)),
        "lora_b": np.asarray(L0_ffn_B).transpose(0, 2, 1).reshape(ER, L),
    }
    nc = bacc.Bacc("TRN2", target_bir_lowering=False, num_devices=1)
    args = {}
    for name, a in arrays.items():
        arrays[name] = a = whole(a)
        args[name] = nc.dram_tensor(name, a.shape, mybir.dt.from_np(a.dtype), kind="ExternalInput").ap()
    args["k_spill"] = nc.dram_tensor("k_spill", (C, P, A, H), F32, kind="Internal").ap()
    args["out"] = nc.dram_tensor("out", (C * H, L), F32, kind="ExternalOutput").ap()
    build_program(nc, **args)
    r = run_bass_kernel_spmd(nc, [arrays], core_ids=[0])
    return r.results[0]["out"].reshape(C, H, L)
```

```python
from contextlib import ExitStack

import concourse.bass as bass
from concourse import mybir

F32 = mybir.dt.float32
F32R = mybir.dt.float32r
U32 = mybir.dt.uint32
I32 = mybir.dt.int32
ALU = mybir.AluOpType
ACT = mybir.ActivationFunctionType
AX_X = mybir.AxisListType.X

P = 128
C, L = 32, 1024
H = 128
D = 128
NL = 4
FC = 4
A = L // P
GH = 8
NG = H // GH
PAIR = 2
NP = GH // PAIR
CH = 4
NCH = C // CH
T = CH * H
E, RK = 8, 16
ER = E * RK
AR = ER + E
PER = A // NL
NCHP = NCH // PER
AH = A // 2
WC = AR + L
N1 = 512 - AR
N2 = (L - N1) // 2
BANKS = ((4, AR, 0, N1), (5, 0, N1, N2), (6, 0, N1 + N2, N2))
GT = 5
PARTS = 2
EPS = 1e-5
SCALING = 32 / RK
ROUND = 1.5 * 2.0 ** 23
TWO_PI = 6.283185
TWO_PI_HI = 6.28125
TWO_PI_LO = 0.0019353071795864769
LN2 = 0.6931471805599453
LN2_HI = 0.693359375
LN2_LO = -2.1219444005469057e-4
EXP_TERMS = [1 / 5040, 1 / 720, 1 / 120, 1 / 24, 1 / 6, 1 / 2, 1.0]
NPOW = 7

LN1W, LN1B, LN2W, LN2B, B2, B1, LNLW, LNLB, BOUT, ZRE, ZIM, CRE, CIM, SCL, SIGN, QUARTER, NVEC = (
    0, 4, 8, 12, 16, 20, 36, 37, 38, 46, 50, 54, 58, 62, 66, 67, 68)
A_IM, B_RE, B_IM, INV_A, LOG_DT, NPAR = 0, 1, 2, 3, 4, 5


def wait(eng, semaphore, value):
    if isinstance(value, int) and value <= 0:
        return
    eng.wait_ge(semaphore, value)


def plain(eng, _):
    eng.nop(nofuse=True)


def steps(eng, body, n, unroll=2, tail=2):
    for k in range(unroll):
        body(k, k % unroll)
    with eng.Fori(unroll, n - tail, unroll) as i:
        for k in range(unroll):
            body(i + k, k)
    for k in range(n - tail, n):
        body(k, k % unroll)


def tower_slots(eng, slot, between={}):
    def at(lay, t, lo, hi):
        def run(offset):
            if not lo <= t - offset < hi:
                return None
            return lay * NCH + (t - offset), (t - offset) % NCH, lay + (t - offset) // NCH
        slot(run)
    for t in range(NCH):
        if t in between:
            between[t]()
        at(0, t, 0, NCH)
    with eng.Fori(1, NL) as lay:
        for t in range(NCH):
            at(lay, t, -NCH, NCH)
    for t in range(NCH, NCH + 5):
        if t in between:
            between[t]()
        at(NL - 1, t, -NCH, NCH)


def build_program(nc, x1, x2, params, vecs_in, bin_in, win_t, w1_t, w2_t, wout_t, wbase_t, bbase_in,
                  ar_t, lora_b, k_spill, out):
    with ExitStack() as ctx:
        def sem(name):
            return ctx.enter_context(nc.semaphore(name))

        def held(stack, name, shape, dt=F32):
            return stack.enter_context(nc.sbuf_tensor(name, shape, dt))

        res = held(ctx, "res", [P, C, D])
        ident = held(ctx, "ident", [P, P])
        over_l = held(ctx, "over_l", [P, P])
        cos_t = held(ctx, "cos_t", [P, NL, H])
        sin_t = held(ctx, "sin_t", [P, NL, H])
        cos_s = held(ctx, "cos_s", [P, NL, H])
        sin_s = held(ctx, "sin_s", [P, NL, H])
        last_t = held(ctx, "last_t", [P, NL, D])
        vecs = held(ctx, "vecs", [P, NVEC])
        cols = held(ctx, "cols", [P, 20, NL])
        stat6 = held(ctx, "stat6", [P, 2, 2, CH, 6])
        mv = held(ctx, "mv", [P, 2, 2, CH, 2])
        vare = held(ctx, "vare", [P, 2, 2, CH])
        rstd = held(ctx, "rstd", [P, 2, 2, CH])
        shift = held(ctx, "shift", [P, 2, CH])
        powers = held(ctx, "powers", [P, 3, NL])
        iota8 = held(ctx, "iota8", [P, E])
        warm = held(ctx, "warm", [P, 1])
        ones = held(ctx, "ones", [P, 1])
        wmean = held(ctx, "wmean", [P, L])
        armean = held(ctx, "armean", [P, AR])

        psum = ctx.enter_context(nc.psum_tensor("psum", [P, 8, 512], F32))

        front = ExitStack()
        kt = held(front, "kt", [P, C, A, H])
        s1 = held(front, "s1", [P, H, A])
        s2 = held(front, "s2", [P, H, A])
        decay_pow = held(front, "decay_pow", [P, NPOW, H])
        turns = held(front, "turns", [P, H])
        iota_b = held(front, "iota_b", [P, H])
        x1b = held(front, "x1b", [P, 2, GH, C])
        x2b = held(front, "x2b", [P, 2, GH, C])
        angle = held(front, "angle", [P, GH, P])
        whole = held(front, "whole", [P, GH, P])
        decay = held(front, "decay", [P, 2, GH, P // 2])
        vand = held(front, "vand", [P, 2, GH, P])
        m1 = held(front, "m1", [P, 2, PAIR, A, C])
        m2 = held(front, "m2", [P, 2, PAIR, A, C])
        binb = held(front, "binb", [P, D])
        front.close()

        wbh = held(ctx, "wbh", [P, A, WC], F32R)
        wbl = held(ctx, "wbl", [P, A, WC], F32R)
        lbh = held(ctx, "lbh", [P, L], F32R)
        lbl = held(ctx, "lbl", [P, L], F32R)
        woh = held(ctx, "woh", [P, L], F32R)
        wol = held(ctx, "wol", [P, L], F32R)
        wraw = held(ctx, "wraw", [P, 2, L])
        xz = held(ctx, "xz", [P, 2, D])
        zh = held(ctx, "zh", [P, 2 * H], F32R)
        zl = held(ctx, "zl", [P, 2 * H], F32R)
        kb = held(ctx, "kb", [P, 2, 2, AH, H])
        bsf = held(ctx, "bsf", [P, 2, 2, 6])
        mvf = held(ctx, "mvf", [P, 2, 2, 2])
        vef = held(ctx, "vef", [P, 2, 2])
        rsf = held(ctx, "rsf", [P, 2, 2])
        tower = ExitStack()
        xn1 = held(tower, "xn1", [P, CH, D])
        xn2 = held(tower, "xn2", [P, 2, CH, D])
        act_s = held(tower, "act_s", [P, 2, CH, H])
        uc = held(tower, "uc", [P, CH, H])
        us = held(tower, "us", [P, 2, CH, H])
        scan_c = held(tower, "scan_c", [P, 2, CH, H])
        scan_s = held(tower, "scan_s", [P, 2, CH, H])
        zb = held(tower, "zb", [P, T])
        zbh = held(tower, "zbh", [P, 2, T], F32R)
        zbl = held(tower, "zbl", [P, 2, T], F32R)
        hid = held(tower, "hid", [P, FC, T])
        arc = held(tower, "arc", [P, A, AR])
        yb = held(tower, "yb", [P, CH, H])
        w1c = held(tower, "w1c", [P, FC * P])
        w1h = held(tower, "w1h", [P, FC * P], F32R)
        w1l = held(tower, "w1l", [P, FC * P], F32R)
        w2c = held(tower, "w2c", [P, FC, D])
        dec = held(tower, "dec", [P, NL, CH, H])
        tower.close()
        bbase = held(ctx, "bbase", [P, L])
        xf = held(ctx, "xf", [P, 4, A, H])
        xh = held(ctx, "xh", [P, 2, A, H], F32R)
        xl = held(ctx, "xl", [P, 2, A, H], F32R)
        h1 = held(ctx, "h1", [P, 2, L])
        lg = held(ctx, "lg", [P, 2, E])
        top = held(ctx, "top", [P, 2, 8])
        topi = held(ctx, "topi", [P, 2, 8], U32)
        gate = held(ctx, "gate", [P, 2, 10])
        wsel = held(ctx, "wsel", [P, 2, 2, E])
        gated = held(ctx, "gated", [P, 2, ER])
        gh = held(ctx, "gh", [P, 2, H], F32R)
        gl = held(ctx, "gl", [P, 2, H], F32R)
        bst = held(ctx, "bst", [P, 2, 2, 6])
        mvo = held(ctx, "mvo", [P, 2, 2])
        rso = held(ctx, "rso", [P, 2, 2])

        s_vecs, s_par, s_win, s_bin = (sem(n) for n in ("s_vecs", "s_par", "s_win", "s_bin"))
        s_x = [sem("s_x0"), sem("s_x1")]
        s_const, s_ident = sem("s_const"), sem("s_ident")
        s_dve, s_pool = sem("s_dve"), sem("s_pool")
        s_setd, s_seta = sem("s_setd"), sem("s_seta")
        s_turned, s_whole, s_angle, s_sin = sem("s_turned"), sem("s_whole"), sem("s_angle"), sem("s_sin")
        s_decay, s_decayed, s_vand = sem("s_decay"), sem("s_decayed"), sem("s_vand")
        s_m1, s_m2, s_kp, s_ke = sem("s_m1"), sem("s_m2"), sem("s_kp"), sem("s_ke")
        s_wmean, s_winc = sem("s_wmean"), sem("s_winc")
        s_sq, s_red, s_stat, s_wvar, s_wr = sem("s_sq"), sem("s_red"), sem("s_stat"), sem("s_wvar"), sem("s_wr")
        s_proj, s_projb, s_projt, s_res = sem("s_proj"), sem("s_projb"), sem("s_projt"), sem("s_res")
        s_dvew, s_half, s_sum = sem("s_dvew"), sem("s_half"), sem("s_sum")
        s_spill = sem("s_spill")
        (s_bn1, s_mv1, s_ve1, s_rs1, s_xn1, s_ta, s_s, s_us, s_uc, s_sc, s_ss, s_m1t, s_m2t, s_m, s_hl, s_tb,
         s_h1, s_bn2, s_mv2, s_ve2, s_rs2, s_xn2, s_tc, s_z, s_w1, s_hid, s_w2, s_y, s_td, s_h2, s_wl1, s_wl2) = (
            sem(n) for n in (
                "bn1", "mv1", "ve1", "rs1", "xn1_ready", "ta", "s_ready", "us", "uc", "sc", "ss", "m1t", "m2t",
                "m_ready", "hl", "tb", "h1_done", "bn2", "mv2", "ve2", "rs2", "xn2_ready", "tc", "z_ready", "w1_done",
                "hid_ready", "w2_done", "y_ready", "td", "h2_done", "wl1", "wl2"))
        (f_bn, f_mv, f_ve, f_rs, f_xn, f_tp, f_z, f_zl, f_wo, f_kb, f_x, f_xh, f_xl) = (
            sem("f_" + n) for n in ("bn", "mv", "ve", "rs", "xn", "tp", "z", "zl", "wo", "kb", "x", "xh", "xl"))
        (o_px, o_pa, o_h1, o_bn, o_mv, o_ve, o_rs, o_hb, o_rt, o_gd, o_e, o_g, o_gt, o_gh, o_gl, o_fin,
         o_out) = (sem("o_" + n) for n in ("px", "pa", "h1", "bn", "mv", "ve", "rs", "hb", "rt", "gd", "e", "g",
                                          "gt", "gh", "gl", "fin", "out"))
        o_st = [sem("o_st0"), sem("o_st1")]
        o_wt = sem("o_wt")
        p_raw, f_k = ([sem(n + "0"), sem(n + "1")] for n in ("p_raw", "f_k"))
        p_early, p_mean, p_means, p_cen, p_hi, p_lo, p_arc, p_arcen, p_rest = (
            sem("p_" + n) for n in ("early", "mean", "means", "cen", "hi", "lo", "arc", "arcen", "rest"))
        p_archi, p_arclo = sem("p_archi"), sem("p_arclo")
        s_shift, s_zl, s_w1h, s_w1s = sem("s_shift"), sem("s_zl"), sem("s_w1h"), sem("s_w1s")
        o_l1, o_b1, o_first = sem("o_l1"), sem("o_b1"), sem("o_first")
        s_tanh, s_tab, s_lastp, s_last, s_dec = (sem(n) for n in ("s_tanh", "s_tab", "s_lastp", "s_last", "s_dec"))


        block = ctx.enter_context(nc.Block())
        par = kt[:, 0:NPAR, 0, :]

        def big(i):
            return kt[:, 8 + i].rearrange("p a h -> p (a h)").rearrange("p (h a) -> p h a", a=A)

        def col(i):
            return kt[:, 16 + i // 8, i % 8, :]

        lam, psi, em1, sh, sn, t0, t1, t2, gr, gi, kk, fr, i0, i1, low, dd = (col(i) for i in range(16))
        ex, en, er, eq, es = (kt[:, 18 + i, 0:2, :] for i in range(5))
        a_, dt_ = ex[:, 0], ex[:, 1]
        ea, va, vb, ca, sa = (big(i) for i in range(5))
        wr_, wi_ = big(5), big(6)

        w_early = kt[:, 24:32].rearrange("p c a h -> p c (a h)")
        ar_early = kt[:, 6:8].rearrange("p c a h -> p (c a h)")[:, 0:A * AR].rearrange("p (a n) -> p a n", a=A)

        win_early = res[:, 0:A, :]
        winc = s2[:].rearrange("p h a -> p (h a)").rearrange("p (a d) -> p a d", a=A)

        @block.sync
        def _(sp):
            sp.dma_start(par, params).then_inc(s_par, 16)
            sp.dma_start(vecs[:], vecs_in).then_inc(s_vecs, 16)
            sp.dma_start(win_early, win_t).then_inc(s_win, 16)
            sp.dma_start(binb[:], bin_in).then_inc(s_bin, 16)
            sp.dma_start(ar_early, ar_t).then_inc(p_early, 16)
            for k in range(0, A, 4):
                sp.dma_start(w_early[:, k:k + 4], wbase_t[:, k:k + 4, :]).then_inc(p_early, 16)

            def load_x(q, u):
                wait(sp, s_kp, (q - 1) * NP)
                sp.dma_start(x1b[:, u], x1[:, bass.ds(q * GH, GH), :]).then_inc(s_x[u], 16)
                sp.dma_start(x2b[:, u], x2[:, bass.ds(q * GH, GH), :]).then_inc(s_x[u], 16)
            steps(sp, load_x, NG)

            sp.wait_ge(s_ke, H // PAIR)
            with sp.Fori(0, C) as c:
                sp.dma_start(k_spill[bass.ds(c, 1)].rearrange("o p a h -> p (o a) h"),
                             kt[:, bass.ds(c, 1)].rearrange("p o a h -> p (o a) h")).then_inc(s_spill, 16)
            sp.wait_ge(s_spill, 16 * C)

            sp.wait_ge(s_res, NCH)

            def load_layer(lay):
                wait(sp, s_w1s, lay)
                sp.dma_start(w1c[:], w1_t[bass.ds(lay, 1)].rearrange("o d f -> (o d) f")).then_inc(s_wl1, 16)
                wait(sp, s_w2, lay * NCH)
                sp.dma_start(w2c[:], w2_t[bass.ds(lay, 1)].rearrange("o f c d -> (o f) c d")).then_inc(s_wl2, 16)

            def load_base(lay):
                for j in range(PER):
                    i = lay * PER + j
                    wait(sp, p_lo, i - 1)
                    sp.dma_start(wraw[:, j, :], wbase_t[:, bass.ds(i, 1), :].rearrange(
                        "p o n -> p (o n)")).then_inc(p_raw[j], 16)
            sp.dma_start(arc[:], ar_t).then_inc(p_arc, 16)
            load_layer(0)
            load_base(0)
            with sp.Fori(1, NL) as lay:
                load_base(lay)
                load_layer(lay)
            sp.wait_ge(p_lo, A - 1)
            sp.dma_start(wraw[:, 0, :], wout_t).then_inc(p_raw[0], 16)
            sp.wait_ge(p_lo, A)
            sp.dma_start(wraw[:, 1, :], lora_b).then_inc(p_raw[1], 16)

            def load_k(s, half):
                wait(sp, f_x, s - 1)
                sp.dma_start(kb[:, half], k_spill[bass.ds(s - half, 2), :, half * AH:(half + 1) * AH, :].rearrange(
                    "b p a h -> p b (a h)")).then_inc(f_k[half], 16)

            load_k(0, 0)
            load_k(1, 1)
            sp.wait_ge(s_h2, NL * NCH)
            sp.wait_ge(p_arclo, 1)
            sp.dma_start(bbase[:], bbase_in).then_inc(p_rest, 16)
            load_k(2, 0)

            def store(c, u):
                if not (isinstance(c, int) and c >= C - 3):
                    load_k(c + 3, 1 - u)
                sp.wait_ge(o_out, c + 1)
                sp.dma_start(out[bass.ds(c * H, H), :], h1[:, u, :]).then_inc(o_st[u], 16)
            steps(sp, store, C, tail=6)
            for u in range(2):
                sp.wait_ge(o_st[u], 8 * C)

        @block.gpsimd
        def _(pool):
            g = nc.gpsimd
            g.memset(over_l[:], 1.0 / L)
            g.memset(ones[:], 1.0)
            for i, e in enumerate((-0.5, 0.5, -1.0)):
                g.memset(powers[:, i, :], e)
            g.iota(iota_b[:], [[1, H]], base=0, channel_multiplier=0, allow_small_or_imprecise_dtypes=True)
            g.iota(iota8[:], [[1, E]], base=0, channel_multiplier=0, allow_small_or_imprecise_dtypes=True)
            g.memset(ident[:], 0.0).then_inc(s_const, 1)
            pool.wait_ge(s_const, 1)
            g.affine_select(out=ident[:], in_=ident[:], compare_op=ALU.not_equal, fill=1.0, base=0,
                            pattern=[[-1, P]], channel_multiplier=1).then_inc(s_ident, 1)

            done = [0]

            def step(ins):
                done[0] += 1
                ins.then_inc(s_pool, 1)
                pool.wait_ge(s_pool, done[0])

            def v(i):
                return vecs[:, i:i + NL]

            (r2, zero, rad, inv, cr, ci, mag, c1, c2, c3, pc, ps, pr, lgr, lgi) = (cols[:, i] for i in range(15))
            pool.wait_ge(s_vecs, 16)
            tt = g.tensor_tensor
            step(tt(r2, v(ZRE), v(ZRE), ALU.mult))
            step(tt(c1, v(ZIM), v(ZIM), ALU.mult))
            step(tt(r2, r2, c1, ALU.add))
            step(g.tensor_scalar(zero, r2, 0.0, None, ALU.is_equal))
            step(tt(rad, r2, powers[:, 1], ALU.pow))
            step(tt(c1, rad, zero, ALU.add))
            step(tt(inv, c1, powers[:, 2], ALU.pow))
            step(tt(c1, v(ZRE), zero, ALU.add))
            step(tt(cr, c1, inv, ALU.mult))
            tt(ci, v(ZIM), inv, ALU.mult).then_inc(s_tab, 1)
            pool.wait_ge(s_tab, 1)
            pool.wait_ge(s_tanh, 1)
            rp = vand[:, 0, 0:NL, :]
            b1_, b2_, b3_ = vand[:, 0, NL:GH, :], vand[:, 1, 0:NL, :], vand[:, 1, NL:GH, :]
            b4_ = decay[:, 0].rearrange("p g h -> p (g h)").rearrange("p (l h) -> p l h", l=NL)
            g.memset(cos_t[:, :, 0:1], 1.0)
            g.memset(rp[:, :, 0:1], 1.0)
            step(g.memset(sin_t[:, :, 0:1], 0.0))
            step(g.tensor_copy(pc, cr))
            step(g.tensor_copy(ps, ci))
            step(g.tensor_copy(pr, mag))
            for k in range(NPOW):
                n = 1 << k

                def wide(x):
                    return x.unsqueeze(2).broadcast_to([P, NL, n])
                tt(b1_[:, :, 0:n], cos_t[:, :, 0:n], wide(pc), ALU.mult)
                tt(b2_[:, :, 0:n], sin_t[:, :, 0:n], wide(ps), ALU.mult)
                tt(b3_[:, :, 0:n], cos_t[:, :, 0:n], wide(ps), ALU.mult)
                tt(b4_[:, :, 0:n], sin_t[:, :, 0:n], wide(pc), ALU.mult)
                step(tt(rp[:, :, n:2 * n], rp[:, :, 0:n], wide(pr), ALU.mult))
                tt(cos_t[:, :, n:2 * n], b1_[:, :, 0:n], b2_[:, :, 0:n], ALU.subtract)
                step(tt(sin_t[:, :, n:2 * n], b3_[:, :, 0:n], b4_[:, :, 0:n], ALU.add))
                if k < NPOW - 1:
                    tt(c1, pc, pc, ALU.mult)
                    tt(c2, ps, ps, ALU.mult)
                    step(tt(c3, pc, ps, ALU.mult))
                    tt(pc, c1, c2, ALU.subtract)
                    tt(ps, c3, c3, ALU.add)
                    step(tt(pr, pr, pr, ALU.mult))
            tt(c1, mag, cr, ALU.mult)
            step(tt(c2, mag, ci, ALU.mult))
            step(tt(lgr, v(CRE), c1, ALU.mult))
            step(tt(c3, v(CIM), c2, ALU.mult))
            step(tt(lgr, lgr, c3, ALU.subtract))
            step(tt(lgi, v(CRE), c2, ALU.mult))
            step(tt(c3, v(CIM), c1, ALU.mult))
            step(tt(lgi, lgi, c3, ALU.add))

            def row(x):
                return x.unsqueeze(2).broadcast_to([P, NL, H])
            tt(b1_, cos_t[:], row(lgr), ALU.mult)
            step(tt(b2_, sin_t[:], row(lgi), ALU.mult))
            step(tt(b1_, b1_, b2_, ALU.subtract))
            step(tt(b1_, b1_, rp, ALU.mult))
            tt(b1_, b1_, row(v(SCL)), ALU.mult)
            tt(cos_s[:], cos_t[:], row(v(SCL)), ALU.mult)
            tt(sin_s[:], sin_t[:], row(v(SCL)), ALU.mult).then_inc(s_tab, 1)
            pool.wait_ge(s_tab, 2)
            g.memset(decay[:, :, :, 0:1], 1.0).then_inc(s_const, 1)
            pool.wait_ge(s_const, 2)

            def make_decay(q, u, powers_of_two):
                wait(pool, s_vand, q - 1)
                for k in powers_of_two:
                    n = 1 << k
                    if k:
                        pool.wait_ge(s_decay, q * (NPOW - 1) + k)
                    plain(pool, s_const)
                    g.tensor_tensor(decay[:, u, :, n:2 * n], decay[:, u, :, 0:n],
                                    decay_pow[:, k, bass.ds(q * GH, GH)].unsqueeze(2).broadcast_to([P, GH, n]),
                                    ALU.mult).then_inc(s_decay, 1)

            def make_m1(q, u, p):
                pool.wait_ge(s_x[u], (q - u) * 16 + 32)
                wait(pool, s_kp, q * NP + p - 1)
                plain(pool, s_const)
                g.tensor_tensor(
                    m1[:, p % 2],
                    x1b[:, u, PAIR * p:PAIR * (p + 1), :].unsqueeze(2).broadcast_to([P, PAIR, A, C]),
                    s1[:, bass.ds(q * GH + PAIR * p, PAIR), :].unsqueeze(3).broadcast_to([P, PAIR, A, C]),
                    ALU.mult).then_inc(s_m1, 1)

            pool.wait_ge(s_setd, 3)
            make_decay(0, 0, range(NPOW - 1))
            pool.wait_ge(s_setd, 5)
            make_m1(0, 0, 0)
            make_decay(1, 1, range(NPOW - 1))

            def group(q, u):
                more = not (isinstance(q, int) and q >= NG - 2)
                make_m1(q, u, 1)
                if more:
                    make_decay(q + 2, u, (0, 1))
                make_m1(q, u, 2)
                if more:
                    make_decay(q + 2, u, (2, 3))
                make_m1(q, u, 3)
                if more:
                    make_decay(q + 2, u, (4,))
                if more or q == NG - 2:
                    make_m1(q + 1, 1 - u, 0)
                if more:
                    make_decay(q + 2, u, (5,))
            steps(pool, group, NG, tail=4)

            pool.wait_ge(s_ke, H // PAIR)
            half = vand[:, 0, 0:NL, :]
            quarter = vand[:, 1, 0:2, :]

            def width_sum(j, c):
                kc = kt[:, bass.ds(j * CH + c, 1)].rearrange("p o a h -> p (o a) h")
                i = (j * (CH - 1) + c) * 2
                plain(pool, s_const)
                tt(half, kc[:, 0:A // 2, :], kc[:, A // 2:A, :], ALU.add).then_inc(s_half, 1)
                pool.wait_ge(s_half, i + 1)
                tt(quarter, half[:, 0:2], half[:, 2:4], ALU.add).then_inc(s_half, 1)
                pool.wait_ge(s_half, i + 2)
                wait(pool, s_stat, j * CH + c - 1)
                tt(m2[:, c % 2, 0].rearrange("p a c -> p (a c)")[:, 0:H], quarter[:, 0], quarter[:, 1],
                   ALU.add).then_inc(s_sum, 1)

            def win_rstd(j, u):
                pool.wait_ge(s_wvar, j + 1)
                g.tensor_tensor(rstd[:, 0, u], vare[:, 0, u], powers[:, 0, 0:CH], ALU.pow).then_inc(s_wr, 1)

            def project(j, u):
                width_sum(j, 2)
                if not (isinstance(j, int) and j == 0):
                    win_rstd(j - 1, 1 - u)
                if not (isinstance(j, int) and j == NCH - 1):
                    width_sum(j + 1, 0)
                    width_sum(j + 1, 1)
            width_sum(0, 0)
            width_sum(0, 1)
            steps(pool, project, NCH)
            win_rstd(NCH - 1, (NCH - 1) % 2)

            pool.wait_ge(s_spill, 16 * C)
            pool.wait_ge(s_last, 1)

            def rstd_of(count, which, u, s_in, s_eps, s_out):
                pool.wait_ge(s_in, count + 1)
                plain(pool, s_const)
                g.tensor_scalar(vare[:, which, u], mv[:, which, u, :, 1], EPS, None, ALU.add).then_inc(s_eps, 1)
                pool.wait_ge(s_eps, count + 1)
                tt(rstd[:, which, u], vare[:, which, u], powers[:, 0, 0:CH], ALU.pow).then_inc(s_out, 1)

            def slot(run):
                s0, s1_, s2_ = run(0), run(1), run(2)
                if s1_:
                    k, n, lay = s1_
                    pool.wait_ge(s_xn1, k + 1)
                    plain(pool, s_const)
                    r = res[:, n * CH:(n + 1) * CH, :]
                    tt(r, r, last_t[:, bass.ds(lay, 1), :].broadcast_to([P, CH, D]), ALU.add).then_inc(s_hl, 1)
                if s0:
                    k, n, lay = s0
                    rstd_of(k, 0, n % 2, s_mv1, s_ve1, s_rs1)
                if s1_:
                    k, n, lay = s1_
                    pool.wait_ge(s_s, k + 1)
                    wait(pool, s_ss, k - 1)
                    plain(pool, s_const)
                    tt(us[:, n % 2], act_s[:, n % 2], sin_t[:, bass.ds(lay, 1), :].broadcast_to([P, CH, H]),
                       ALU.mult).then_inc(s_us, 1)
                    sc = scan_c[:, n % 2]
                    pool.wait_ge(s_sc, k + 1)
                    plain(pool, s_const)
                    tt(sc, sc, cos_s[:, bass.ds(lay, 1), :].broadcast_to([P, CH, H]), ALU.mult).then_inc(s_m1t, 1)
                if s2_:
                    k, n, lay = s2_
                    rstd_of(k, 1, n % 2, s_mv2, s_ve2, s_rs2)
                if s1_:
                    k, n, lay = s1_
                    pool.wait_ge(s_m1t, k + 1)
                    pool.wait_ge(s_m2t, k + 1)
                    tt(sc, sc, scan_s[:, n % 2], ALU.add).then_inc(s_m, 1)
                if s0:
                    k, n, lay = s0
                    if n % NCHP in (1, 2):
                        centre(n // NCHP, lay, n % NCHP - 1)

            def centre(j, lay, part):
                part = slice(part * L // PARTS, (part + 1) * L // PARTS)
                pool.wait_ge(p_raw[j], 16 * (lay + 1))
                plain(pool, s_const)
                tt(wraw[:, j, part], wraw[:, j, part], wmean[:, part], ALU.subtract).then_inc(p_cen, 1)

            def wout():
                pool.wait_ge(p_arc, 16)
                tt(arc[:], arc[:], armean[:].unsqueeze(1).broadcast_to([P, A, AR]), ALU.subtract).then_inc(p_arcen, 1)
                pool.wait_ge(p_hi, A + 1)
                pool.wait_ge(p_lo, A)
                tt(wol[:], wraw[:, 0], woh[:].bitcast(F32), ALU.subtract).then_inc(p_lo, 1)

            def lora_and_router():
                pool.wait_ge(p_archi, 1)
                tt(wbl[:, :, 0:AR], arc[:], wbh[:, :, 0:AR].bitcast(F32), ALU.subtract).then_inc(p_arclo, 1)
                pool.wait_ge(p_hi, A + 2)
                tt(lbl[:], wraw[:, 1], lbh[:].bitcast(F32), ALU.subtract).then_inc(p_lo, 1)

            pool.wait_ge(p_means, 1)
            tower_slots(pool, slot, {NCH + 1: wout, NCH + 2: lora_and_router})

            def front_rstd(c, v):
                pool.wait_ge(f_mv, c + 2)
                plain(pool, s_const)
                g.tensor_scalar(vef[:, v], mvf[:, v, :, 1], EPS, None, ALU.add).then_inc(f_ve, 2)
                pool.wait_ge(f_ve, c + 2)
                tt(rsf[:, v], vef[:, v], powers[:, 0, 0:2], ALU.pow).then_inc(f_rs, 2)

            def front_bias(s, half):
                pool.wait_ge(f_k[half], (s - half) * 8 + 16)
                tt(kb[:, half], kb[:, half], vecs[:, BOUT + half * AH:BOUT + (half + 1) * AH].unsqueeze(1).unsqueeze(
                    3).broadcast_to([P, 2, AH, H]), ALU.add).then_inc(f_kb, 1)

            front_rstd(0, 0)
            front_rstd(2, 1)
            front_bias(0, 0)
            front_bias(1, 1)
            front_bias(2, 0)
            pool.wait_ge(s_h2, NL * NCH)
            pool.wait_ge(p_rest, 16)

            def last(c, v):
                u = v % 2
                pool.wait_ge(o_mv, c + 1)
                plain(pool, s_const)
                g.tensor_scalar(rso[:, u, 0:1], mvo[:, u, 1:2], EPS, None, ALU.add).then_inc(o_ve, 1)
                pool.wait_ge(o_ve, c + 1)
                tt(rso[:, u, 1:2], rso[:, u, 0:1], powers[:, 0, 0:1], ALU.pow).then_inc(o_rs, 1)
                if u == 0 and not (isinstance(c, int) and c >= C - 4):
                    front_rstd(c + 4, v // 2)
                tt(h1[:, u], h1[:, u], bbase[:], ALU.add).then_inc(o_hb, 1)
                if not (isinstance(c, int) and c >= C - 3):
                    front_bias(c + 3, 1 - u)
            steps(pool, last, C, unroll=4, tail=4)

        @block.scalar
        def _(act):
            a = nc.scalar.activation
            act.wait_ge(s_tab, 1)
            a(cols[:, 6], cols[:, 2], ACT.Tanh).then_inc(s_tanh, 1)
            act.wait_ge(s_setd, 1)
            a(sh, turns[:], ACT.Sin, scale=TWO_PI / 2)
            a(sn, turns[:], ACT.Sin, scale=TWO_PI).then_inc(s_seta, 1)
            act.wait_ge(s_setd, 2)
            for k in range(A):
                a(va[:, :, k], fr, ACT.Copy, bias=0.25, scale=float(k))
                ins = a(vb[:, :, k], fr, ACT.Copy, scale=float(k))
            ins.then_inc(s_seta, 1)
            def turn(q, heads):
                wait(act, s_sin, q)
                for k in heads:
                    plain(act, s_ident)
                    ins = a(angle[:, k, :], iota_b[:], ACT.Identity, bias=vecs[:, QUARTER:QUARTER + 1],
                            scale=turns[:, bass.ds(q * GH + k, 1)])
                return ins

            act.wait_ge(s_const, 1)
            act.wait_ge(s_vecs, 16)
            turn(0, range(GH)).then_inc(s_turned, 1)
            act.wait_ge(s_setd, 4)
            a(ca, va, ACT.Sin, scale=TWO_PI)
            a(sa, vb, ACT.Sin, scale=TWO_PI).then_inc(s_seta, 1)

            def sines(q):
                act.wait_ge(s_angle, q + 1)
                a(whole[:], angle[:], ACT.Sin, scale=TWO_PI).then_inc(s_sin, 1)

            def evacuate(q, p):
                act.wait_ge(s_kp, q * NP + p + 1)
                plain(act, s_ident)
                a(kt[:, :, :, bass.ds(q * GH + p * PAIR, PAIR)].rearrange("p c a h -> p h a c"),
                  psum[:, p, :].rearrange("p (h a c) -> p h a c", h=PAIR, a=A), ACT.Copy).then_inc(s_ke, 1)
            sines(0)
            turn(1, range(GH)).then_inc(s_turned, 1)
            act.wait_ge(p_mean, 1)
            nc.scalar.copy(armean[:], psum[:, 6, 0:AR])
            nc.scalar.copy(wmean[:].rearrange("p (b n) -> p b n", b=2), psum[:, 4:6, :]).then_inc(p_means, 1)
            act.wait_ge(s_lastp, 1)
            a(last_t[:].rearrange("p l d -> p (l d)"), psum[:, 0, :], ACT.Copy).then_inc(s_last, 1)
            act.wait_ge(s_setd, 5)

            def group(q, u):
                more = not (isinstance(q, int) and q >= NG - 2)
                evacuate(q, 0)
                if more or q == NG - 2:
                    sines(q + 1)
                if more:
                    turn(q + 2, range(GH)).then_inc(s_turned, 1)
                for p in range(1, NP):
                    evacuate(q, p)
            steps(act, group, NG, tail=4)

            act.wait_ge(s_m2, H // PAIR)
            act.wait_ge(s_winc, 1)
            nc.scalar.copy(winc, win_early).then_inc(s_winc, 1)
            act.wait_ge(s_ke, H // PAIR)

            def square(j, c):
                wait(act, s_red, j * CH + c - 1)
                plain(act, s_ident)
                a((angle if c % 2 == 0 else whole)[:], kt[:, bass.ds(j * CH + c, 1)].rearrange("p o a h -> p (o a) h"),
                  ACT.Square).then_inc(s_sq, 1)

            def project(j, u):
                square(j, 2)
                square(j, 3)
                if not (isinstance(j, int) and j == NCH - 1):
                    square(j + 1, 0)
                    square(j + 1, 1)
                act.wait_ge(s_proj, j + 1)
                wait(act, s_projt, j - 1)
                a(m1[:, u].rearrange("p h a c -> p (h a c)"), psum[:, u, :], ACT.Copy).then_inc(s_projb, 1)
            square(0, 0)
            square(0, 1)
            steps(act, project, NCH)

            a(warm[:], ones[:], ACT.Silu)
            act.wait_ge(s_spill, 16 * C)

            def vec(i):
                return vecs[:, bass.ds(i, 1)]

            def split_w1(lay):
                act.wait_ge(s_wl1, (lay + 1) * 16)
                wait(act, s_w1, lay * NCH * FC)
                nc.scalar.copy(w1h[:], w1c[:]).then_inc(s_w1h, 1)

            def silu(k, n, lay, f):
                act.wait_ge(s_w1, k * FC + f + 1)
                plain(act, s_ident)
                a(hid[:, f, :], psum[:, 3 + f, :], ACT.Silu, bias=vec(lay * FC + B1 + f)).then_inc(s_hid, 1)

            def leading(i, j):
                act.wait_ge(p_cen, (i + 1) * PARTS)
                plain(act, s_ident)
                nc.scalar.copy(wbh[:, bass.ds(i, 1), AR:WC].rearrange("p o n -> p (o n)"), wraw[:, j]).then_inc(p_hi, 1)

            def slot(run):
                s0, s3, s4 = run(0), run(3), run(4)
                if s4:
                    k, n, lay = s4
                    wait(act, s_w2, k)
                    silu(k, n, lay, 0)
                    silu(k, n, lay, 1)
                if s3:
                    k, n, lay = s3
                    act.wait_ge(s_tc, k + 1)
                    wait(act, s_zl, k)
                    wait(act, s_w1, (k - 1) * FC)
                    plain(act, s_ident)
                    for dst in (zb[:], zbh[:, n % 2]):
                        ins = a(dst, psum[:, 0, :], ACT.Identity, bias=vec(lay + LN2B), scale=vec(lay + LN2W))
                    ins.then_inc(s_z, 1)
                if s4:
                    k, n, lay = s4
                    silu(k, n, lay, 2)
                    silu(k, n, lay, 3)
                    if n == NCH - 1 and not isinstance(lay, int):
                        split_w1(lay + 1)
                if s0 and s0[1] % NCHP == 3:
                    k, n, lay = s0
                    leading(lay * PER + n // NCHP, n // NCHP)
                if s0:
                    k, n, lay = s0
                    act.wait_ge(s_shift, k + 1)
                    wait(act, s_ta, k)
                    for c in range(CH):
                        ins = a(xn1[:, c, :], res[:, n * CH + c, :], ACT.Identity, bias=shift[:, n % 2, c:c + 1],
                                scale=rstd[:, 0, n % 2, c:c + 1])
                    ins.then_inc(s_xn1, 1)
                if s0:
                    k, n, lay = s0
                    act.wait_ge(s_ta, k + 1)
                    wait(act, s_us, k - 1)
                    wait(act, s_uc, k - 1)
                    plain(act, s_ident)
                    a(act_s[:, n % 2].rearrange("p c h -> p (c h)"), psum[:, 0, :], ACT.Silu, bias=vec(lay + LN1B),
                      scale=vec(lay + LN1W)).then_inc(s_s, 1)
                if s4:
                    k, n, lay = s4
                    act.wait_ge(s_w2, k + 1)
                    wait(act, s_td, k)
                    plain(act, s_ident)
                    a(yb[:].rearrange("p c h -> p (c h)"), psum[:, 7, :], ACT.Identity,
                      bias=vec(lay + B2)).then_inc(s_y, 1)
            def wout():
                act.wait_ge(p_raw[0], 16 * (NL + 1))
                nc.scalar.copy(woh[:], wraw[:, 0]).then_inc(p_hi, 1)

            def lora():
                act.wait_ge(p_arcen, 1)
                nc.scalar.copy(wbh[:, :, 0:AR], arc[:]).then_inc(p_archi, 1)
                act.wait_ge(p_raw[1], 16 * (NL + 1))
                nc.scalar.copy(lbh[:], wraw[:, 1]).then_inc(p_hi, 1)
            def front_z(c, bank=7):
                act.wait_ge(f_tp, c + 2)
                wait(act, f_wo, c)
                for dst in (xz[:].rearrange("p b d -> p (b d)"), zh[:]):
                    ins = a(dst, psum[:, bank, 0:2 * H], ACT.Identity, bias=vecs[:, LNLB:LNLB + 1],
                            scale=vecs[:, LNLW:LNLW + 1])
                ins.then_inc(f_z, 2)

            tower_slots(act, slot, {2: lambda: split_w1(0), NCH + 1: wout, NCH + 2: lora,
                                    NCH + 3: lambda: front_z(0, 1)})

            def front_xh(c, v):
                act.wait_ge(f_x, c - v % 2 + 2)
                wait(act, o_fin, c - 1)
                nc.scalar.copy(xh[:, v % 2], xf[:, v]).then_inc(f_xh, 1)

            act.wait_ge(s_h2, NL * NCH)
            front_xh(0, 0)
            front_z(2)

            def last(c, v):
                u = v % 2
                act.wait_ge(o_px, c + 1)
                wait(act, o_st[u], 8 * (c - u))
                nc.scalar.copy(h1[:, u].rearrange("p (b n) -> p b n", b=2), psum[:, 2:4, :]).then_inc(o_h1, 1)
                if not (isinstance(c, int) and c == C - 1):
                    front_xh(c + 1, (v + 1) % 4)
                if u == 1 and not (isinstance(c, int) and c >= C - 4):
                    front_z(c + 3)
                act.wait_ge(o_gd, c + 1)
                act.wait_ge(o_rs, c + 1)
                a(gate[:, u, 3:4], gate[:, u, 2:3], ACT.Exp, scale=rso[:, u, 1:2]).then_inc(o_e, 1)
                act.wait_ge(o_gt, c + 1)
                wait(act, o_fin, c - 1)
                nc.scalar.copy(gh[:, u], psum[:, 7, 0:H]).then_inc(o_gh, 1)
            steps(act, last, C, unroll=4, tail=4)

        @block.vector
        def _(dve):
            v = v_ = nc.vector
            tt, ts, stt = v.tensor_tensor, v.tensor_scalar, v.scalar_tensor_tensor
            done = [0]

            def step(ins):
                done[0] += 1
                ins.then_inc(s_dve, 1)
                dve.wait_ge(s_dve, done[0])

            def exp_whole(x, rows):
                return ts(en[:, 0:rows], x, 1.0 / LN2, ROUND, ALU.mult, ALU.add)

            def exp_whole_back(rows):
                return ts(en[:, 0:rows], en[:, 0:rows], -ROUND, None, ALU.add)

            def exp_rest(x, rows):
                return stt(er[:, 0:rows], en[:, 0:rows], -LN2_HI, x, ALU.mult, ALU.add)

            def exp_rest_low(rows):
                ts(es[:, 0:rows].bitcast(I32), en[:, 0:rows], 127.0, 2.0 ** 23, ALU.add, ALU.mult)
                return stt(er[:, 0:rows], en[:, 0:rows], -LN2_LO, er[:, 0:rows], ALU.mult, ALU.add)

            def exp_series(i, rows):
                if i == 0:
                    return ts(eq[:, 0:rows], er[:, 0:rows], EXP_TERMS[0], None, ALU.mult)
                return stt(eq[:, 0:rows], eq[:, 0:rows], EXP_TERMS[i], er[:, 0:rows], ALU.add, ALU.mult)

            dve.wait_ge(s_par, 16)
            step(ts(ex, par[:, INV_A:INV_A + 2], -87.0, 88.0, ALU.max, ALU.min))
            step(exp_whole(ex, 2))
            step(exp_whole_back(2))
            step(exp_rest(ex, 2))
            step(exp_rest_low(2))
            for i in range(len(EXP_TERMS)):
                step(exp_series(i, 2))
            step(stt(ex, eq, 1.0, es, ALU.add, ALU.mult))
            tt(psi, par[:, A_IM], dt_, ALU.mult)
            stt(lam, a_, -1.0, dt_, ALU.mult, ALU.mult)
            tt(i0, a_, a_, ALU.mult)
            step(tt(i1, par[:, A_IM], par[:, A_IM], ALU.mult))
            ts(kk, psi, 1.0 / (TWO_PI_HI + TWO_PI_LO), None, ALU.mult)
            ts(low, lam, -87.0, None, ALU.max)
            step(tt(i0, i0, i1, ALU.add))
            low1 = low.unsqueeze(1)
            ts(kk, kk, ROUND, -ROUND, ALU.add, ALU.add)
            step(exp_whole(low1, 1))
            stt(t0, kk, -TWO_PI_HI, psi, ALU.mult, ALU.add)
            step(exp_whole_back(1))
            stt(t0, kk, -TWO_PI_LO, t0, ALU.mult, ALU.add)
            step(exp_rest(low1, 1))
            ts(t0, t0, 1.0 / (TWO_PI_HI + TWO_PI_LO), None, ALU.mult)
            step(exp_rest_low(1))
            ts(t1, t0, ROUND, -ROUND, ALU.add, ALU.add)
            step(exp_series(0, 1))
            tt(turns[:], t0, t1, ALU.subtract).then_inc(s_setd, 1)
            step(exp_series(1, 1))
            dve.wait_ge(s_setd, 1)
            ts(fr, turns[:], float(P), None, ALU.mult)
            step(exp_series(2, 1))
            ts(t0, fr, ROUND, -ROUND, ALU.add, ALU.add)
            step(exp_series(3, 1))
            tt(fr, fr, t0, ALU.subtract).then_inc(s_setd, 1)
            step(exp_series(4, 1))
            v.reciprocal(i0, i0)
            step(exp_series(5, 1))
            stt(i1, par[:, A_IM], -2.0, i0, ALU.mult, ALU.mult)
            stt(i0, a_, -2.0, i0, ALU.mult, ALU.mult)
            step(exp_series(6, 1))
            dve.wait_ge(s_seta, 1)
            tt(sh, sh, sh, ALU.mult)
            ts(t0, es[:, 0], -1.0, None, ALU.add)
            step(tt(t1, eq[:, 0], es[:, 0], ALU.mult))
            ts(sh, sh, 2.0, None, ALU.mult)
            tt(em1, t0, t1, ALU.add)
            step(tt(dd, t0, t1, ALU.add))
            def doubling(k):
                ts(decay_pow[:, k], dd, 1.0, None, ALU.add)
                return stt(dd, dd, 2.0, dd, ALU.add, ALU.mult)

            ts(t0, sh, -1.0, 1.0, ALU.mult, ALU.add)
            step(doubling(0))
            tt(t0, em1, t0, ALU.mult)
            stt(t1, em1, 1.0, sn, ALU.add, ALU.mult)
            step(doubling(1))
            tt(t0, t0, sh, ALU.subtract)
            step(doubling(2))
            tt(gr, par[:, B_RE], t0, ALU.mult)
            tt(t2, par[:, B_IM], t1, ALU.mult)
            tt(gi, par[:, B_RE], t1, ALU.mult)
            tt(kk, par[:, B_IM], t0, ALU.mult)
            step(doubling(3))
            tt(gr, gr, t2, ALU.subtract)
            tt(gi, gi, kk, ALU.add)
            step(doubling(4))
            tt(kk, gr, i0, ALU.mult)
            tt(t2, gi, i1, ALU.mult)
            tt(t0, gr, i1, ALU.mult)
            tt(gi, gi, i0, ALU.mult)
            step(doubling(5))
            tt(kk, kk, t2, ALU.subtract)
            tt(gi, gi, t0, ALU.add)
            step(doubling(6))
            ts(ea[:, :, 0], dd, 0.0, 1.0, ALU.mult, ALU.add)
            ts(ea[:, :, 1], dd, 1.0, None, ALU.add).then_inc(s_setd, 1)
            dve.wait_ge(s_seta, 2)
            ts(ca, va, ROUND, -ROUND, ALU.add, ALU.add)
            step(ts(sa, vb, ROUND, -ROUND, ALU.add, ALU.add))
            tt(va, va, ca, ALU.subtract)
            tt(vb, vb, sa, ALU.subtract).then_inc(s_setd, 1)
            for k in range(2, A):
                step(tt(ea[:, :, k], ea[:, :, k - 1], ea[:, :, 1], ALU.mult))

            def along(x):
                return x.unsqueeze(2).broadcast_to([P, H, A])
            def whole_turns(q):
                dve.wait_ge(s_turned, q + 1)
                ts(whole[:], angle[:], ROUND, -ROUND, ALU.add, ALU.add).then_inc(s_whole, 1)

            def reduce_angles(q):
                dve.wait_ge(s_whole, q + 1)
                tt(angle[:], angle[:], whole[:], ALU.subtract).then_inc(s_angle, 1)

            whole_turns(0)
            reduce_angles(0)
            dve.wait_ge(s_seta, 3)
            tt(va, ca, along(kk), ALU.mult)
            step(tt(vb, sa, along(gi), ALU.mult))
            step(tt(wr_, va, vb, ALU.subtract))
            tt(va, sa, along(kk), ALU.mult)
            step(tt(vb, ca, along(gi), ALU.mult))
            step(tt(wi_, va, vb, ALU.add))
            dve.wait_ge(s_vecs, 16)
            stt(s1[:], wr_, vecs[:, SIGN:SIGN + 1], ea, ALU.mult, ALU.mult)
            stt(s2[:], wi_, -1.0, ea, ALU.mult, ALU.mult).then_inc(s_setd, 1)
            dve.wait_ge(s_const, 1)
            dve.wait_ge(s_win, 16)
            dve.wait_ge(s_wmean, 1)
            tt(win_early, win_early, psum[:, 7, 0:D].unsqueeze(1).broadcast_to([P, A, D]),
               ALU.subtract).then_inc(s_winc, 1)

            def last_doubling(q, u):
                n = P // 2
                dve.wait_ge(s_decay, (q + 1) * (NPOW - 1))
                wait(dve, s_kp, (q - 1) * NP)
                tt(vand[:, u, :, n:2 * n], decay[:, u],
                   decay_pow[:, NPOW - 1, bass.ds(q * GH, GH)].unsqueeze(2).broadcast_to([P, GH, n]),
                   ALU.mult).then_inc(s_decayed, 1)

            def make_vand(q, u):
                dve.wait_ge(s_sin, q + 1)
                dve.wait_ge(s_decayed, q + 1)
                n = P // 2
                tt(vand[:, u, :, 0:n], decay[:, u], whole[:, :, 0:n], ALU.mult)
                tt(vand[:, u, :, n:2 * n], vand[:, u, :, n:2 * n], whole[:, :, n:2 * n], ALU.mult).then_inc(s_vand, 1)

            def make_m2(q, u, p):
                dve.wait_ge(s_x[u], (q - u) * 16 + 32)
                wait(dve, s_kp, q * NP + p - 1)
                tt(m2[:, p % 2],
                   x2b[:, u, PAIR * p:PAIR * (p + 1), :].unsqueeze(2).broadcast_to([P, PAIR, A, C]),
                   s2[:, bass.ds(q * GH + PAIR * p, PAIR), :].unsqueeze(3).broadcast_to([P, PAIR, A, C]),
                   ALU.mult).then_inc(s_m2, 1)

            dve.wait_ge(s_setd, 5)
            make_m2(0, 0, 0)
            dve.wait_ge(s_last, 1)
            last_doubling(0, 0)
            make_vand(0, 0)

            def group(q, u):
                more = not (isinstance(q, int) and q == NG - 1)
                make_m2(q, u, 1)
                if more:
                    last_doubling(q + 1, 1 - u)
                    dve.wait_ge(s_vand, q + 1)
                    whole_turns(q + 1)
                make_m2(q, u, 2)
                if more:
                    reduce_angles(q + 1)
                make_m2(q, u, 3)
                if more:
                    make_vand(q + 1, 1 - u)
                    make_m2(q + 1, 1 - u, 0)
            steps(dve, group, NG)

            dve.wait_ge(s_bin, 16)
            dve.wait_ge(s_winc, 2)

            dve.wait_ge(s_ke, H // PAIR)
            def width_sums(j, c):
                wait(dve, s_stat, j * CH + c - 1)
                sums = m2[:, c % 2].rearrange("p h a c -> p (h a c)")
                if c == CH - 1:
                    v.tensor_reduce(sums[:, 0:H], kt[:, bass.ds(j * CH + c, 1)].rearrange("p o a h -> p h (o a)"),
                                    AX_X, ALU.add)
                dve.wait_ge(s_sq, j * CH + c + 1)
                v.tensor_reduce(sums[:, H:2 * H], (angle if c % 2 == 0 else whole)[:].rearrange("p a h -> p h a"),
                                AX_X, ALU.add).then_inc(s_red, 1)

            def variances(j, u):
                dve.wait_ge(s_stat, (j + 1) * CH)
                st = psum[:, 4 + u, 0:2 * CH]
                mean = mv[:, 0, u, :, 0]
                step_w = j * 2
                ts(mean, st[:, 0:CH], 1.0 / L, None, ALU.mult)
                ts(mv[:, 0, u, :, 1], st[:, CH:2 * CH], 1.0 / L, EPS, ALU.mult, ALU.add).then_inc(s_dvew, 1)
                dve.wait_ge(s_dvew, step_w + 1)
                tt(mean, mean, mean, ALU.mult).then_inc(s_dvew, 1)
                dve.wait_ge(s_dvew, step_w + 2)
                tt(vare[:, 0, u], mv[:, 0, u, :, 1], mean, ALU.subtract).then_inc(s_wvar, 1)

            def residual(j, u):
                dve.wait_ge(s_wr, j + 1)
                dve.wait_ge(s_projt, j + 1)
                for c in range(CH):
                    ins = stt(res[:, bass.ds(j * CH + c, 1)].rearrange("p o d -> p (o d)"),
                              psum[:, 2 + u, c * D:(c + 1) * D], rstd[:, 0, u, c:c + 1], binb[:], ALU.mult, ALU.add)
                ins.then_inc(s_res, 1)

            def project(j, u):
                first = isinstance(j, int) and j == 0
                more = not (isinstance(j, int) and j == NCH - 1)
                if not first:
                    variances(j - 1, 1 - u)
                width_sums(j, 2)
                width_sums(j, 3)
                if not first:
                    residual(j - 1, 1 - u)
                if more:
                    width_sums(j + 1, 0)
                    width_sums(j + 1, 1)
            width_sums(0, 0)
            width_sums(0, 1)
            steps(dve, project, NCH)
            variances(NCH - 1, (NCH - 1) % 2)

            dve.wait_ge(s_spill, 16 * C)
            dve.wait_ge(s_proj, NCH)
            dve.wait_ge(s_last, 1)
            def batches(n):
                return res[:, n * CH:(n + 1) * CH, :]

            def statistics(k, n, which, s_stats):
                for c in range(CH):
                    ins = v.bn_stats(stat6[:, which, n % 2, c], res[:, n * CH + c, :])
                ins.then_inc(s_stats, 1)

            def aggregate(k, n, which, s_stats, s_out):
                dve.wait_ge(s_stats, k + 1)
                plain(dve, s_const)
                for c in range(CH):
                    ins = v.bn_aggr(mv[:, which, n % 2, c], stat6[:, which, n % 2, c])
                ins.then_inc(s_out, 1)

            def normalise(k, n, which, dst, s_rs, s_read, s_out):
                dve.wait_ge(s_rs, k + 1)
                wait(dve, s_read, k - 1)
                for c in range(CH):
                    ins = ts(dst[:, n % 2, c, :], res[:, n * CH + c, :], mv[:, which, n % 2, c, 0:1],
                             rstd[:, which, n % 2, c:c + 1], ALU.subtract, ALU.mult)
                ins.then_inc(s_out, 1)

            def flat(x):
                return x.rearrange("p c h -> p (c h)")

            def slot(run):
                s0, s1_, s2_, s3, s4, s5 = (run(i) for i in range(6))
                if s3:
                    k, n, lay = s3
                    normalise(k, n, 1, xn2, s_rs2, s_tc, s_xn2)
                if s0:
                    k, n, lay = s0
                    wait(dve, s_h2, k - NCH + 1)
                    statistics(k, n, 0, s_bn1)
                if s1_:
                    k, n, lay = s1_
                    dve.wait_ge(s_s, k + 1)
                    tt(uc[:], act_s[:, n % 2], cos_t[:, bass.ds(lay, 1), :].broadcast_to([P, CH, H]),
                       ALU.mult).then_inc(s_uc, 1)
                if s0:
                    k, n, lay = s0
                    aggregate(k, n, 0, s_bn1, s_mv1)
                if s1_:
                    k, n, lay = s1_
                    dve.wait_ge(s_uc, k + 1)
                    wait(dve, s_tb, k - 1)
                    decay_l = dec[:, bass.ds(lay, 1)].rearrange("p o c h -> p (o c h)")
                    v.tensor_tensor_scan(flat(scan_c[:, n % 2]), decay_l, flat(uc[:]), 0.0, ALU.mult,
                                         ALU.add).then_inc(s_sc, 1)
                if s2_:
                    k, n, lay = s2_
                    dve.wait_ge(s_tb, k + 1)
                    dve.wait_ge(s_hl, k + 1)
                    tt(flat(batches(n)), psum[:, 1, :], flat(batches(n)), ALU.add).then_inc(s_h1, 1)
                if s5:
                    k, n, lay = s5
                    dve.wait_ge(s_td, k + 1)
                    tt(flat(batches(n)), psum[:, 2, :], flat(batches(n)), ALU.add).then_inc(s_h2, 1)
                if s0:
                    k, n, lay = s0
                    dve.wait_ge(s_rs1, k + 1)
                    wait(dve, s_xn1, k - 1)
                    plain(dve, s_const)
                    stt(shift[:, n % 2], mv[:, 0, n % 2, :, 0], -1.0, rstd[:, 0, n % 2], ALU.mult,
                        ALU.mult).then_inc(s_shift, 1)
                if s2_:
                    k, n, lay = s2_
                    dve.wait_ge(s_h1, k + 1)
                    statistics(k, n, 1, s_bn2)
                if s1_:
                    k, n, lay = s1_
                    dve.wait_ge(s_us, k + 1)
                    wait(dve, s_m, k - 1)
                    v.tensor_tensor_scan(flat(scan_s[:, n % 2]), decay_l, flat(us[:, n % 2]), 0.0, ALU.mult,
                                         ALU.add).then_inc(s_ss, 1)
                if s2_:
                    k, n, lay = s2_
                    aggregate(k, n, 1, s_bn2, s_mv2)
                if s0 and s0[1] % NCHP == 3:
                    k, n, lay = s0
                    rest(lay * PER + n // NCHP, n // NCHP)
                if s1_:
                    k, n, lay = s1_
                    dve.wait_ge(s_ss, k + 1)
                    tt(scan_s[:, n % 2], scan_s[:, n % 2], sin_s[:, bass.ds(lay, 1), :].broadcast_to([P, CH, H]),
                       ALU.mult).then_inc(s_m2t, 1)
                if s3:
                    k, n, lay = s3
                    dve.wait_ge(s_z, k + 1)
                    wait(dve, s_w1, (k - 1) * FC)
                    tt(zbl[:, n % 2], zb[:], zbh[:, n % 2].bitcast(F32), ALU.subtract).then_inc(s_zl, 1)
                if s4 and s4[1] == NCH - 1 and not isinstance(s4[2], int):
                    split_w1(s4[2] + 1)
            def front_stats(c, v):
                for b in range(2):
                    ins = v_.bn_stats(bsf[:, v, b], res[:, bass.ds(c + b, 1), :].rearrange("p o d -> p (o d)"))
                ins.then_inc(f_bn, 2)
                dve.wait_ge(f_bn, c + 2)
                plain(dve, s_const)
                for b in range(2):
                    ins = v_.bn_aggr(mvf[:, v, b], bsf[:, v, b])
                ins.then_inc(f_mv, 2)

            def front_norm(c, v):
                dve.wait_ge(f_rs, c + 2)
                wait(dve, f_zl, c)
                for b in range(2):
                    ins = ts(xz[:, b], res[:, bass.ds(c + b, 1), :].rearrange("p o d -> p (o d)"), mvf[:, v, b, 0:1],
                             rsf[:, v, b:b + 1], ALU.subtract, ALU.mult)
                ins.then_inc(f_xn, 2)

            def ahead():
                front_stats(0, 0)
                front_stats(2, 1)
                front_norm(0, 0)

            def ahead_zl():
                front_zl(0)
                front_norm(2, 1)

            def front_zl(c):
                dve.wait_ge(f_z, c + 2)
                wait(dve, f_wo, c)
                tt(zl[:], xz[:].rearrange("p b d -> p (b d)"), zh[:].bitcast(F32), ALU.subtract).then_inc(f_zl, 2)

            def behind():
                residual(NCH - 1, (NCH - 1) % 2)
                for k in range(NL):
                    ins = ts(dec[:, k], over_l[:].unsqueeze(1).broadcast_to([P, CH, H]), 0.0, cols[:, 6, k:k + 1],
                             ALU.mult, ALU.add)
                ins.then_inc(s_dec, 1)
                dve.wait_ge(s_dec, 1)
                v.memset(dec[:, :, :, 0:1], 0.0).then_inc(s_dec, 1)
                dve.wait_ge(s_dec, 2)
            def rest(i, j):
                dve.wait_ge(p_hi, i + 1)
                plain(dve, s_const)
                tt(wbl[:, bass.ds(i, 1), AR:WC].rearrange("p o n -> p (o n)"), wraw[:, j],
                   wbh[:, bass.ds(i, 1), AR:WC].bitcast(F32).rearrange("p o n -> p (o n)"),
                   ALU.subtract).then_inc(p_lo, 1)

            def split_w1(lay):
                dve.wait_ge(s_w1h, lay + 1)
                tt(w1l[:], w1c[:], w1h[:].bitcast(F32), ALU.subtract).then_inc(s_w1s, 1)
            tower_slots(dve, slot, {1: behind, 3: lambda: split_w1(0), NCH + 3: ahead, NCH + 4: ahead_zl})

            dve.wait_ge(s_h2, NL * NCH)

            def front_x(s, v):
                half, pair = v % 2, v - v % 2
                dve.wait_ge(f_wo, s + 1)
                dve.wait_ge(f_kb, s + 1)
                if half == 0:
                    wait(dve, f_xh, s - 2)
                    wait(dve, f_xl, s - 2)
                    wait(dve, o_px, s - 2)
                tt(xf[:, pair:pair + 2, half * AH:(half + 1) * AH, :].rearrange("p b a h -> p a b h"),
                   psum[:, 0:2, :].rearrange("p n (m b h) -> p (n m) b h", b=2, h=H),
                   kb[:, half].rearrange("p b a h -> p a b h"), ALU.add).then_inc(f_x, 1)

            def front_xl(c, v):
                dve.wait_ge(f_xh, c + 1)
                dve.wait_ge(f_x, c - v % 2 + 2)
                wait(dve, o_fin, c - 1)
                tt(xl[:, v % 2], xf[:, v], xh[:, v % 2].bitcast(F32), ALU.subtract).then_inc(f_xl, 1)

            dve.wait_ge(p_arclo, 1)
            front_x(0, 0)
            front_x(1, 1)
            front_xl(0, 0)
            front_zl(2)

            def scaled(u, bank, at, o, n):
                return stt(h1[:, u, o:o + n], psum[:, bank, at:at + n], rso[:, u, 1:2], h1[:, u, o:o + n], ALU.mult,
                           ALU.add)

            def last(c, w):
                u = w % 2
                step_ahead = not (isinstance(c, int) and c >= C - 2)
                pair_ahead = not (isinstance(c, int) and c >= C - 4)
                if u == 1 and pair_ahead:
                    front_norm(c + 3, w // 2)
                dve.wait_ge(o_h1, c + 1)
                for b in range(2):
                    ins = v.bn_stats(bst[:, u, b], h1[:, u, b * 512:(b + 1) * 512])
                ins.then_inc(o_bn, 1)
                dve.wait_ge(o_bn, c + 1)
                plain(dve, s_const)
                v.bn_aggr(mvo[:, u], bst[:, u].rearrange("p b s -> p (b s)")).then_inc(o_mv, 1)
                if u == 0 and pair_ahead:
                    front_stats(c + 4, w // 2)
                if step_ahead:
                    front_x(c + 2, (w + 2) % 4)
                if not (isinstance(c, int) and c == C - 1):
                    front_xl(c + 1, (w + 1) % 4)
                dve.wait_ge(o_pa, c + 1)
                rt = c * 8
                v.tensor_copy(lg[:, u], psum[:, 4, ER:AR]).then_inc(o_rt, 1)
                dve.wait_ge(o_rt, rt + 1)
                plain(dve, s_const)
                v.max(top[:, u], lg[:, u]).then_inc(o_rt, 1)
                dve.wait_ge(o_rt, rt + 2)
                tt(gate[:, u, 2:3], top[:, u, 1:2], top[:, u, 0:1], ALU.subtract).then_inc(o_gd, 1)
                v.max_index(topi[:, u], top[:, u], lg[:, u]).then_inc(o_rt, 1)
                dve.wait_ge(o_rt, rt + 3)
                v.tensor_copy(gate[:, u, 0:2], topi[:, u, 0:2]).then_inc(o_rt, 1)
                if u == 1 and pair_ahead:
                    front_zl(c + 3)
                dve.wait_ge(o_e, c + 1)
                ts(gate[:, u, 4:5], gate[:, u, 3:4], 1.0 / SCALING, 1.0 / SCALING, ALU.mult, ALU.add).then_inc(o_rt, 1)
                dve.wait_ge(o_rt, rt + 5)
                v.reciprocal(gate[:, u, 5:6], gate[:, u, 4:5]).then_inc(o_rt, 1)
                dve.wait_ge(o_rt, rt + 6)
                tt(gate[:, u, 6:7], gate[:, u, 3:4], gate[:, u, 5:6], ALU.mult)
                ts(wsel[:, u, 0], iota8[:], gate[:, u, 0:1], gate[:, u, 5:6], ALU.is_equal, ALU.mult).then_inc(o_rt, 1)
                dve.wait_ge(o_rt, rt + 7)
                ts(wsel[:, u, 1], iota8[:], gate[:, u, 1:2], gate[:, u, 6:7], ALU.is_equal, ALU.mult).then_inc(o_rt, 1)
                dve.wait_ge(o_rt, rt + 8)
                tt(wsel[:, u, 0], wsel[:, u, 0], wsel[:, u, 1], ALU.add).then_inc(o_wt, 1)
                dve.wait_ge(o_wt, c + 1)
                tt(gated[:, u].rearrange("p (e r) -> p e r", e=E), psum[:, 4, 0:ER].rearrange("p (e r) -> p e r", e=E),
                   wsel[:, u, 0].unsqueeze(2).broadcast_to([P, E, RK]), ALU.mult).then_inc(o_g, 1)
                dve.wait_ge(o_gh, c + 1)
                wait(dve, o_fin, c - 1)
                tt(gl[:, u], psum[:, 7, 0:H], gh[:, u].bitcast(F32), ALU.subtract).then_inc(o_gl, 1)
                dve.wait_ge(o_hb, c + 1)
                scaled(u, 4, AR, 0, N1).then_inc(o_b1, 1)
                dve.wait_ge(o_b1, c + 1)
                dve.wait_ge(o_l1, c + 1)
                scaled(u, 1, 0, 0, N1).then_inc(o_first, 1)
                dve.wait_ge(o_fin, c + 1)
                for bank, at, o, n in BANKS[1:]:
                    ins = scaled(u, bank, at, o, n)
                ins.then_inc(o_out, 1)
            steps(dve, last, C, unroll=4, tail=8)

        @block.tensor
        def _(pe):
            mm = nc.tensor.matmul

            pe.wait_ge(s_win, 16)
            pe.wait_ge(s_const, 1)
            for k in range(A):
                ins = mm(psum[:, 7, 0:D], over_l[:], win_early[:, k, :], start=(k == 0), stop=(k == A - 1))
            ins.then_inc(s_wmean, 1)
            pe.wait_ge(p_early, 48)
            for k in range(A):
                mm(psum[:, 6, 0:AR], over_l[:], ar_early[:, k, :], start=(k == 0), stop=(k == A - 1))
                for b in range(2):
                    ins = mm(psum[:, 4 + b, :], over_l[:], w_early[:, k, b * 512:(b + 1) * 512], start=(k == 0),
                             stop=(k == A - 1))
            ins.then_inc(p_mean, 1)

            pe.wait_ge(s_tab, 2)
            pe.wait_ge(s_ident, 1)
            for k in range(NL):
                ins = nc.tensor.transpose(psum[:, 0, k * D:(k + 1) * D], vand[:, 0, NL + k, :], ident[:])
            ins.then_inc(s_lastp, 1)
            pe.wait_ge(s_last, 1)

            def group(q, u):
                pe.wait_ge(s_vand, q + 1)
                for p in range(NP):
                    pe.wait_ge(s_m1, q * NP + p + 1)
                    pe.wait_ge(s_m2, q * NP + p + 1)
                    wait(pe, s_ke, (q - 1) * NP + p + 1)
                    for h in range(PAIR):
                        o = psum[:, p, h * A * C:(h + 1) * A * C]
                        w = vand[:, u, p * PAIR + h, :]
                        mm(o, w, m1[:, p % 2, h].rearrange("p a c -> p (a c)"), start=True, stop=False)
                        ins = mm(o, w, m2[:, p % 2, h].rearrange("p a c -> p (a c)"), start=False, stop=True)
                    ins.then_inc(s_kp, 1)
            steps(pe, group, NG)

            pe.wait_ge(s_winc, 2)
            pe.wait_ge(s_ident, 1)
            pe.wait_ge(s_ke, H // PAIR)

            def statistics(j, u, c):
                sums = m2[:, c % 2].rearrange("p h a c -> p (h a c)")
                pe.wait_ge(s_red, j * CH + c + 1)
                if c < CH - 1:
                    pe.wait_ge(s_sum, j * (CH - 1) + c + 1)
                if c == 0:
                    wait(pe, s_wvar, j - 1)
                mm(psum[:, 4 + u, c:c + 1], sums[:, 0:H], ones[:], start=True, stop=True)
                mm(psum[:, 4 + u, CH + c:CH + c + 1], sums[:, H:2 * H], ones[:], start=True,
                   stop=True).then_inc(s_stat, 1)

            def turn_back(j, u):
                pe.wait_ge(s_projb, j + 1)
                wait(pe, s_res, j)
                for c in range(CH):
                    y = m1[:, u].rearrange("p h a c -> p (h a c)")[:, c * H:(c + 1) * H]
                    ins = nc.tensor.transpose(psum[:, 2 + u, c * D:(c + 1) * D], y, ident[:])
                ins.then_inc(s_projt, 1)

            def project(j, u):
                wait(pe, s_projb, j - 1)
                for k in range(A):
                    ins = mm(psum[:, u, :], winc[:, k, :], kt[:, bass.ds(j * CH, CH), k, :],
                             start=(k == 0), stop=(k == A - 1))
                    if k == A - 1:
                        ins.then_inc(s_proj, 1)
                    if k == 2 and not (isinstance(j, int) and j == 0):
                        turn_back(j - 1, 1 - u)
                    if k % 2:
                        statistics(j, u, k // 2)
            assert A == 2 * CH
            steps(pe, project, NCH)
            turn_back(NCH - 1, (NCH - 1) % 2)

            pe.wait_ge(s_last, 1)

            def transposes(bank, src):
                for c in range(CH):
                    ins = nc.tensor.transpose(psum[:, bank, c * P:(c + 1) * P], src[:, c, :], ident[:])
                return ins

            def hidden(k, n, f):
                wait(pe, s_hid, (k - 1) * FC + f + 1)
                w, dst = slice(f * P, (f + 1) * P), psum[:, 3 + f, :]
                mm(dst, w1h[:, w], zbh[:, n % 2], start=True, stop=False)
                mm(dst, w1l[:, w], zbh[:, n % 2], start=False, stop=False)
                mm(dst, w1h[:, w], zbl[:, n % 2], start=False, stop=True).then_inc(s_w1, 1)

            def hidden_back(k, n, f):
                pe.wait_ge(s_hid, k * FC + f + 1)
                return mm(psum[:, 7, :], w2c[:, f, :], hid[:, f, :], start=(f == 0), stop=(f == FC - 1))

            def slot(run):
                s0, s2_, s3, s4, s5 = (run(i) for i in (0, 2, 3, 4, 5))
                if s4:
                    k, n, lay = s4
                    pe.wait_ge(s_zl, k + 1)
                    if n == 0:
                        pe.wait_ge(s_w1s, lay + 1)
                    hidden(k, n, 0)
                    hidden(k, n, 1)
                if s3:
                    k, n, lay = s3
                    pe.wait_ge(s_xn2, k + 1)
                    pe.wait_ge(s_s, min(k + 3, NL * NCH) if isinstance(k, int) else k + 3)
                    transposes(0, xn2[:, n % 2]).then_inc(s_tc, 1)
                if s5:
                    k, n, lay = s5
                    pe.wait_ge(s_y, k + 1)
                    wait(pe, s_h2, k)
                    transposes(2, yb[:]).then_inc(s_td, 1)
                if s2_:
                    k, n, lay = s2_
                    pe.wait_ge(s_m, k + 1)
                    wait(pe, s_h1, k)
                    transposes(1, scan_c[:, n % 2]).then_inc(s_tb, 1)
                if s4:
                    k, n, lay = s4
                    hidden(k, n, 2)
                    hidden(k, n, 3)
                    wait(pe, s_y, k)
                    if n == 0:
                        pe.wait_ge(s_wl2, (lay + 1) * 16)
                    for f in range(FC - 1):
                        hidden_back(k, n, f)
                if s0:
                    k, n, lay = s0
                    pe.wait_ge(s_xn1, k + 1)
                    wait(pe, s_s, k)
                    wait(pe, s_z, k - 2)
                    transposes(0, xn1).then_inc(s_ta, 1)
                if s4:
                    k, n, lay = s4
                    hidden_back(k, n, FC - 1).then_inc(s_w2, 1)
            def front_transpose(c, bank=7):
                pe.wait_ge(f_xn, c + 2)
                wait(pe, o_gl, c - 3)
                for b in range(2):
                    ins = nc.tensor.transpose(psum[:, bank, b * H:(b + 1) * H], xz[:, b], ident[:])
                ins.then_inc(f_tp, 2)

            def front_wout(s, half):
                pe.wait_ge(f_zl, s - half + 2)
                wait(pe, f_x, s)
                for k in range(AH):
                    w = slice((half * AH + k) * P, (half * AH + k + 1) * P)
                    o = psum[:, k // 2, (k % 2) * 2 * H:(k % 2 + 1) * 2 * H]
                    mm(o, woh[:, w], zh[:], start=True, stop=False)
                    mm(o, wol[:, w], zh[:], start=False, stop=False)
                    ins = mm(o, woh[:, w], zl[:], start=False, stop=True)
                ins.then_inc(f_wo, 1)

            def ahead():
                pe.wait_ge(s_h1, NL * NCH)
                front_transpose(0, 1)

            def ahead_wout():
                pe.wait_ge(s_z, NL * NCH)
                pe.wait_ge(p_lo, A + 1)
                front_wout(0, 0)
            tower_slots(pe, slot, {NCH + 3: ahead, NCH + 4: ahead_wout})


            front_wout(1, 1)
            pe.wait_ge(s_y, NL * NCH)
            front_transpose(2)
            pe.wait_ge(p_arclo, 1)
            pe.wait_ge(p_lo, A + 2)

            def product(u, k, bank, at, o, n):
                dst = psum[:, bank, at:at + n]
                mm(dst, xh[:, u, k, :], wbh[:, k, o:o + n], start=(k == 0), stop=False)
                mm(dst, xh[:, u, k, :], wbl[:, k, o:o + n], start=False, stop=False)
                return mm(dst, xl[:, u, k, :], wbh[:, k, o:o + n], start=False, stop=(bank == 4 and k == A - 1))

            def lora(u, dst, o, n, start):
                mm(dst, gh[:, u], lbh[:, o:o + n], start=start, stop=False)
                mm(dst, gh[:, u], lbl[:, o:o + n], start=False, stop=False)
                return mm(dst, gl[:, u], lbh[:, o:o + n], start=False, stop=True)

            def base(u, chunks):
                for k in chunks:
                    for bank, at, o, n in BANKS[1:]:
                        product(u, k, bank, at, AR + o, n)

            def last(c, v):
                u = v % 2
                step_ahead = not (isinstance(c, int) and c >= C - 2)
                pair_ahead = not (isinstance(c, int) and c >= C - 4)
                pe.wait_ge(f_x, c - u + 2)
                wait(pe, o_h1, c)
                for k in range(A):
                    ins = nc.tensor.transpose(psum[:, 2 + k // 4, (k % 4) * P:(k % 4 + 1) * P], xf[:, v, k, :],
                                              ident[:])
                ins.then_inc(o_px, 1)
                wait(pe, o_first, c)
                if step_ahead:
                    front_wout(c + 2, u)
                wait(pe, o_out, c)
                pe.wait_ge(f_xl, c + 1)
                for k in range(A):
                    ins = product(u, k, 4, 0, 0, 512)
                ins.then_inc(o_pa, 1)
                if u == 1 and pair_ahead:
                    front_transpose(c + 3)
                base(u, range(0, GT))
                pe.wait_ge(o_g, c + 1)
                if u == 1 and pair_ahead:
                    pe.wait_ge(f_z, c + 5)
                nc.tensor.transpose(psum[:, 7, 0:ER], gated[:, u], ident[:]).then_inc(o_gt, 1)
                base(u, range(GT, A - 1))
                pe.wait_ge(o_gl, c + 1)
                if step_ahead:
                    pe.wait_ge(f_x, c + 3)
                lora(u, psum[:, 1, 0:N1], 0, N1, True).then_inc(o_l1, 1)
                base(u, range(A - 1, A))
                for bank, at, o, n in BANKS[1:]:
                    ins = lora(u, psum[:, bank, at:at + n], o, n, False)
                ins.then_inc(o_fin, 1)
            steps(pe, last, C, unroll=4, tail=4)


def kernel(x, L0_tok_log_dt, L0_tok_B, L0_tok_inv_A_real, L0_tok_A_imag, L0_attn_Win, L0_attn_bin, L0_attn_ln1_w,
           L0_attn_ln1_b, L0_attn_phz_re, L0_attn_phz_im, L0_attn_lc_re, L0_attn_lc_im, L0_attn_sc_lin,
           L0_attn_ln2_w, L0_attn_ln2_b, L0_attn_W1, L0_attn_b1, L0_attn_W2, L0_attn_b2, L0_attn_lnl_w,
           L0_attn_lnl_b, L0_attn_Wout, L0_attn_bout, L0_ffn_W_base, L0_ffn_b_base, L0_ffn_W_router, L0_ffn_A,
           L0_ffn_B):
    import numpy as np
    import concourse.bacc as bacc
    from concourse.bass_utils import run_bass_kernel_spmd

    def whole(a):
        return np.ascontiguousarray(a)

    x = np.asarray(x)
    x_re, x_im = (x[..., i].transpose(2, 1, 0) for i in range(2))

    def twice(a):
        return np.concatenate([np.asarray(a).T] * 2, axis=0)

    B = np.asarray(L0_tok_B)
    params = np.stack([twice(L0_tok_A_imag), twice(B[..., 0]), twice(B[..., 1]), twice(L0_tok_inv_A_real),
                       np.broadcast_to(np.asarray(L0_tok_log_dt)[None, :], (P, H))], axis=1)
    sign = np.repeat(np.array([1.0, -1.0], np.float32), P // 2)[:, None]
    quarter = np.repeat(np.array([0.25, 0.0], np.float32), P // 2)[:, None]
    vec_cols = [np.asarray(a).T for a in (L0_attn_ln1_w, L0_attn_ln1_b, L0_attn_ln2_w, L0_attn_ln2_b, L0_attn_b2)]
    vec_cols += [np.asarray(L0_attn_b1).reshape(NL * FC, P).T]
    vec_cols += [np.asarray(a).reshape(-1, P).T for a in (L0_attn_lnl_w, L0_attn_lnl_b, L0_attn_bout)]
    vec_cols += [np.asarray(a).T for a in (L0_attn_phz_re, L0_attn_phz_im, L0_attn_lc_re, L0_attn_lc_im,
                                           L0_attn_sc_lin)]
    router = np.asarray(L0_ffn_W_router)
    lora_a = np.asarray(L0_ffn_A).reshape(ER, L)

    def width_on_partitions(w):
        return np.asarray(w).T.reshape(A, P, -1).transpose(1, 0, 2)

    arrays = {
        "x1": np.concatenate([x_re, x_im], axis=0),
        "x2": np.concatenate([x_im, x_re], axis=0),
        "params": params,
        "vecs_in": np.concatenate(vec_cols + [sign, quarter], axis=1),
        "bin_in": np.broadcast_to(np.asarray(L0_attn_bin)[None, :], (P, D)),
        "win_t": width_on_partitions(L0_attn_Win),
        "w1_t": np.asarray(L0_attn_W1).transpose(0, 2, 1),
        "w2_t": np.asarray(L0_attn_W2).transpose(0, 2, 1).reshape(NL, FC, P, D).transpose(0, 2, 1, 3),
        "wout_t": np.asarray(L0_attn_Wout).T,
        "wbase_t": width_on_partitions(L0_ffn_W_base),
        "bbase_in": np.broadcast_to(np.asarray(L0_ffn_b_base)[None, :], (P, L)),
        "ar_t": width_on_partitions(np.concatenate([lora_a, router], axis=0)),
        "lora_b": np.asarray(L0_ffn_B).transpose(0, 2, 1).reshape(ER, L),
    }
    nc = bacc.Bacc("TRN2", target_bir_lowering=False, num_devices=1)
    args = {}
    for name, a in arrays.items():
        arrays[name] = a = whole(a)
        args[name] = nc.dram_tensor(name, a.shape, mybir.dt.from_np(a.dtype), kind="ExternalInput").ap()
    args["k_spill"] = nc.dram_tensor("k_spill", (C, P, A, H), F32, kind="Internal").ap()
    args["out"] = nc.dram_tensor("out", (C * H, L), F32, kind="ExternalOutput").ap()
    build_program(nc, **args)
    r = run_bass_kernel_spmd(nc, [arrays], core_ids=[0])
    return r.results[0]["out"].reshape(C, H, L)
```
